# Optimizing a Trainium2 kernel written in Bass

```python
import numpy as np
import jax
import jax.numpy as jnp

def _softmax(x, axis=-1):
    return jax.nn.softmax(x, axis=axis)

def _gelu(x):
    return jax.nn.gelu(x, approximate=True)

def _silu(x):
    return jax.nn.silu(x)

def _sigmoid(x):
    return jax.nn.sigmoid(x)

def _layernorm(x, axis=-1, eps=1e-05):
    m = jnp.mean(x, axis=axis, keepdims=True)
    v = jnp.var(x, axis=axis, keepdims=True)
    return (x - m) / jnp.sqrt(v + eps)

def _scatter_add(tgt, idx, src, axis=0):
    return tgt.at[idx].add(src)

def _segment_sum(src, seg, n):
    return jax.ops.segment_sum(src, seg, n)
kernel_name = 'mk_gps_d1_gnn_r8_444687'

def setup_inputs(seed: int=0):
    np.random.seed(seed)
    _w = jnp.asarray

    def _rec_inputs():
        import jax
        import jax.numpy as jnp
        _gk = jax.random.key(seed)
        x = -0.0003713 + 1 * jax.random.normal(jax.random.fold_in(_gk, 1), (6250, 256), jnp.float32)
        src = jax.random.randint(jax.random.fold_in(_gk, 2), (100000,), 0, 6250, jnp.int32)
        dst = jnp.minimum((6250 * jax.random.uniform(jax.random.fold_in(_gk, 3), (100000,)) ** 2.0).astype(jnp.int32), 49999)
        _o = jnp.argsort(dst, stable=True)
        src = src[_o]
        dst = dst[_o]
        return (x, src, dst)
    x, src, dst = _rec_inputs()

    def _L0_gnn_setup():
        import jax, jax.numpy as jnp
        import numpy as np
        N_NODES = 6250
        N_EDGES = 100000
        IN_FEATS = 256
        OUT_FEATS = 256
        NUM_HEADS = 8
        FEATS_PER_HEAD = OUT_FEATS // NUM_HEADS
        LN_EPS = 1e-05
        key = jax.random.key(seed)
        ks = jax.random.split(key, 8)
        glorot = lambda k, shp: jax.random.normal(k, shp, jnp.float32) * np.sqrt(2.0 / (shp[0] + shp[-1]))
        return {'feat': jax.random.normal(ks[0], (N_NODES, IN_FEATS), jnp.float32), 'Wsrc': glorot(ks[1], (OUT_FEATS, IN_FEATS)), 'bsrc': jnp.zeros((OUT_FEATS,), jnp.float32), 'Wdst': glorot(ks[2], (OUT_FEATS, IN_FEATS)), 'bdst': jnp.zeros((OUT_FEATS,), jnp.float32), 'Wval': glorot(ks[3], (OUT_FEATS, IN_FEATS)), 'bval': jnp.zeros((OUT_FEATS,), jnp.float32), 'attn': glorot(ks[4], (1, NUM_HEADS, FEATS_PER_HEAD)), 'src': jax.random.randint(ks[5], (N_EDGES,), 0, N_NODES, jnp.int32), 'dst': jax.random.randint(ks[6], (N_EDGES,), 0, N_NODES, jnp.int32)}
    _L0_gnn_all = _L0_gnn_setup()
    _L0_gnn_in = {k: v for k, v in _L0_gnn_all.items() if k in ('Wsrc', 'bsrc', 'Wdst', 'bdst', 'Wval', 'bval', 'attn')}
    del _L0_gnn_all

    def _L0_mix_setup():
        import jax, jax.numpy as jnp
        import numpy as np
        HEADS = 8
        EPS = 1e-05

        def _ln(t, w, b, headc):
            m = jnp.mean(t, axis=-1, keepdims=True)
            d = t - m
            std = jnp.sqrt(jnp.sum(d * d, axis=-1, keepdims=True) / (headc - 1))
            return w * (d / (std + EPS)) + b
        key = jax.random.key(seed)
        B, N, C = (32, 512, 256)
        headc = C // HEADS
        x = jax.random.normal(key, (B, N, C), dtype=jnp.float32)
        return {'x': x, 'kln_weight': jnp.ones((HEADS, 1, headc), dtype=jnp.float32), 'kln_bias': jnp.zeros((HEADS, 1, headc), dtype=jnp.float32), 'vln_weight': jnp.ones((HEADS, 1, headc), dtype=jnp.float32), 'vln_bias': jnp.zeros((HEADS, 1, headc), dtype=jnp.float32)}
    _L0_mix_all = _L0_mix_setup()
    _L0_mix_in = {k: v for k, v in _L0_mix_all.items() if k in ('kln_weight', 'kln_bias', 'vln_weight', 'vln_bias')}
    del _L0_mix_all

    def _L0_ffn_setup():
        import math
        import jax, jax.numpy as jnp
        import numpy as np
        CAPACITY_FACTOR = 1.25
        TOP_K = 2
        LN_EPS = 1e-05

        def _layer_norm(x, gamma, beta):
            mu = jnp.mean(x, axis=-1, keepdims=True)
            var = jnp.var(x, axis=-1, keepdims=True)
            return (x - mu) * jax.lax.rsqrt(var + LN_EPS) * gamma + beta
        key = jax.random.key(seed)
        ks = jax.random.split(key, 4)
        B, S, D, F, E = (8, 512, 256, 512, 8)
        x = jax.random.normal(ks[0], (B, S, D), dtype=jnp.float32)
        Wr = jax.random.normal(ks[1], (D, E), dtype=jnp.float32) / np.sqrt(D)
        br = jnp.zeros((E,), jnp.float32)
        W1 = jax.random.normal(ks[2], (E, D, F), dtype=jnp.float32) / np.sqrt(D)
        b1 = jnp.zeros((E, F), jnp.float32)
        W2 = jax.random.normal(ks[3], (E, F, D), dtype=jnp.float32) / np.sqrt(F)
        b2 = jnp.zeros((E, D), jnp.float32)
        gamma = jnp.ones((D,), jnp.float32)
        beta = jnp.zeros((D,), jnp.float32)
        return {'x': x, 'Wr': Wr, 'br': br, 'W1': W1, 'b1': b1, 'W2': W2, 'b2': b2, 'gamma': gamma, 'beta': beta}
    _L0_ffn_all = _L0_ffn_setup()
    _L0_ffn_in = {k: v for k, v in _L0_ffn_all.items() if k in ('Wr', 'br', 'W1', 'b1', 'W2', 'b2', 'gamma', 'beta')}
    del _L0_ffn_all
    return {'x': x, 'src': src, 'dst': dst, 'L0_gnn_Wsrc': _L0_gnn_in['Wsrc'], 'L0_gnn_bsrc': _L0_gnn_in['bsrc'], 'L0_gnn_Wdst': _L0_gnn_in['Wdst'], 'L0_gnn_bdst': _L0_gnn_in['bdst'], 'L0_gnn_Wval': _L0_gnn_in['Wval'], 'L0_gnn_bval': _L0_gnn_in['bval'], 'L0_gnn_attn': _L0_gnn_in['attn'], 'L0_mix_kln_weight': _L0_mix_in['kln_weight'], 'L0_mix_kln_bias': _L0_mix_in['kln_bias'], 'L0_mix_vln_weight': _L0_mix_in['vln_weight'], 'L0_mix_vln_bias': _L0_mix_in['vln_bias'], 'L0_ffn_Wr': _L0_ffn_in['Wr'], 'L0_ffn_br': _L0_ffn_in['br'], 'L0_ffn_W1': _L0_ffn_in['W1'], 'L0_ffn_b1': _L0_ffn_in['b1'], 'L0_ffn_W2': _L0_ffn_in['W2'], 'L0_ffn_b2': _L0_ffn_in['b2'], 'L0_ffn_gamma': _L0_ffn_in['gamma'], 'L0_ffn_beta': _L0_ffn_in['beta']}

def reference(x, src, dst, L0_gnn_Wsrc, L0_gnn_bsrc, L0_gnn_Wdst, L0_gnn_bdst, L0_gnn_Wval, L0_gnn_bval, L0_gnn_attn, L0_mix_kln_weight, L0_mix_kln_bias, L0_mix_vln_weight, L0_mix_vln_bias, L0_ffn_Wr, L0_ffn_br, L0_ffn_W1, L0_ffn_b1, L0_ffn_W2, L0_ffn_b2, L0_ffn_gamma, L0_ffn_beta):
    import jax
    import jax.numpy as jnp

    def _L0_gnn_ref(feat, Wsrc, bsrc, Wdst, bdst, Wval, bval, attn, src, dst):
        import jax, jax.numpy as jnp
        import numpy as np
        N_NODES = 6250
        N_EDGES = 100000
        IN_FEATS = 256
        OUT_FEATS = 256
        NUM_HEADS = 8
        FEATS_PER_HEAD = OUT_FEATS // NUM_HEADS
        LN_EPS = 1e-05
        N = feat.shape[0]
        mu = jnp.mean(feat, axis=-1, keepdims=True)
        var = jnp.var(feat, axis=-1, keepdims=True)
        h = (feat - mu) / jnp.sqrt(var + LN_EPS)
        feat_src = (h @ Wsrc.T + bsrc).reshape(N, NUM_HEADS, FEATS_PER_HEAD)
        feat_dst = (h @ Wdst.T + bdst).reshape(N, NUM_HEADS, FEATS_PER_HEAD)
        feat_val = (h @ Wval.T + bval).reshape(N, NUM_HEADS, FEATS_PER_HEAD)
        e = jax.nn.silu(feat_src[src] + feat_dst[dst])
        score = jnp.einsum('ehf,xhf->eh', e, attn)
        smax = jax.ops.segment_max(score, dst, num_segments=N)
        a = jnp.exp(score - smax[dst])
        denom = jax.ops.segment_sum(a, dst, num_segments=N)
        a = a / denom[dst]
        msg = feat_val[src] * a[:, :, None]
        h_upd = jax.ops.segment_sum(msg, dst, num_segments=N)
        h_upd = h_upd.reshape(N, OUT_FEATS)
        h_upd = h_upd + h
        return jax.nn.silu(h_upd)

    def _L0_mix_ref(x, kln_weight, kln_bias, vln_weight, vln_bias):
        import jax, jax.numpy as jnp
        import numpy as np
        HEADS = 8
        EPS = 1e-05

        def _ln(t, w, b, headc):
            m = jnp.mean(t, axis=-1, keepdims=True)
            d = t - m
            std = jnp.sqrt(jnp.sum(d * d, axis=-1, keepdims=True) / (headc - 1))
            return w * (d / (std + EPS)) + b
        B, N, C = x.shape
        headc = C // HEADS
        qkv = x.reshape(B, N, HEADS, headc).transpose(0, 2, 1, 3)
        k = _ln(qkv, kln_weight, kln_bias, headc)
        v = _ln(qkv, vln_weight, vln_bias, headc)
        kv = jnp.einsum('bhnd,bhne->bhde', k, v) / N
        out = jnp.einsum('bhnd,bhde->bhne', qkv, kv)
        out = out.transpose(0, 2, 1, 3).reshape(B, N, C)
        return out + x

    def _L0_ffn_ref(x, Wr, br, W1, b1, W2, b2, gamma, beta):
        import math
        import jax, jax.numpy as jnp
        import numpy as np
        CAPACITY_FACTOR = 1.25
        TOP_K = 2
        LN_EPS = 1e-05

        def _layer_norm(x, gamma, beta):
            mu = jnp.mean(x, axis=-1, keepdims=True)
            var = jnp.var(x, axis=-1, keepdims=True)
            return (x - mu) * jax.lax.rsqrt(var + LN_EPS) * gamma + beta
        B, S, D = x.shape
        E = Wr.shape[1]
        N = B * S
        K = TOP_K
        logits = jnp.mean(x, axis=1) @ Wr + br
        routing_weights = jax.nn.softmax(logits, axis=-1)
        capacity = float(math.ceil(N * CAPACITY_FACTOR / E))
        expected_loads = routing_weights.sum(axis=0) * (N / B)
        scale = jnp.where(expected_loads > capacity, capacity / expected_loads, 1.0)
        routing_weights = jax.nn.softmax(routing_weights * scale, axis=-1)
        rw_tok = jnp.broadcast_to(routing_weights[:, None, :], (B, S, E)).reshape(N, E)
        top_w, top_i = jax.lax.top_k(rw_tok, K)
        top_w = jax.nn.softmax(top_w, axis=-1)
        xf = x.reshape(N, D)
        h = jax.nn.gelu(jnp.einsum('nd,edf->enf', xf, W1) + b1[:, None, :], approximate=False)
        y = jnp.einsum('enf,efd->end', h, W2) + b2[:, None, :]
        w_dense = jnp.zeros((N, E), x.dtype).at[jnp.arange(N)[:, None], top_i].add(top_w)
        out = jnp.einsum('ne,end->nd', w_dense, y).reshape(B, S, D)
        out = _layer_norm(out + x, gamma, beta)
        return out
    xn = _layernorm(x, axis=-1)
    x = x + _L0_gnn_ref(xn, L0_gnn_Wsrc, L0_gnn_bsrc, L0_gnn_Wdst, L0_gnn_bdst, L0_gnn_Wval, L0_gnn_bval, L0_gnn_attn, src, dst) + _L0_mix_ref(xn[None], L0_mix_kln_weight, L0_mix_kln_bias, L0_mix_vln_weight, L0_mix_vln_bias)[0]
    x = x + _L0_ffn_ref(_layernorm(x, axis=-1)[None], L0_ffn_Wr, L0_ffn_br, L0_ffn_W1, L0_ffn_b1, L0_ffn_W2, L0_ffn_b2, L0_ffn_gamma, L0_ffn_beta)[0]
    return x

_drawn_inputs = setup_inputs


def setup_inputs(seed=0):
    import zlib

    import numpy as np

    out = dict(_drawn_inputs(seed))
    spreads = {'L0_gnn_bsrc': (0.0, 2.0),
     'L0_gnn_bdst': (0.0, 2.0),
     'L0_gnn_bval': (0.0, 0.457),
     'L0_mix_kln_weight': (1.0, 0.2),
     'L0_mix_kln_bias': (0.0, 0.561),
     'L0_mix_vln_weight': (1.0, 0.2),
     'L0_mix_vln_bias': (0.0, 0.56),
     'L0_ffn_br': (0.0, 0.1),
     'L0_ffn_b1': (0.0, 0.8),
     'L0_ffn_b2': (0.0, 0.566),
     'L0_ffn_gamma': (1.0, 0.2),
     'L0_ffn_beta': (0.0, 0.36)}
    factors = {'L0_ffn_Wr': 8.0, 'L0_gnn_Wdst': 3.005}
    for name, (base, spread) in spreads.items():
        noise = np.random.default_rng([zlib.crc32(name.encode()), seed]).standard_normal(out[name].shape)
        drawn = base * np.exp(spread * noise) if base else spread * noise
        out[name] = jnp.asarray(drawn.astype(out[name].dtype))
    for name, factor in factors.items():
        out[name] = (out[name] * factor).astype(out[name].dtype)
    return out
```

```python
import concourse.bass as bass
from concourse import mybir
from concourse.alu_op_type import AluOpType as ALU
from contextlib import ExitStack

FP32 = mybir.dt.float32
I32 = mybir.dt.int32
U32 = mybir.dt.uint32
I16 = mybir.dt.int16
ACT = mybir.ActivationFunctionType
AX = mybir.AxisListType

N_NODES, N_EDGES, D, HEADS, EXPERTS, FF = 6250, 100000, 256, 8, 8, 512
P = 128
HC = D // HEADS
NT = -(-N_NODES // P)
NP = NT * P
G = 7
NG = NT // G
CHUNKS = P // HEADS
BLOCKS = -(-N_EDGES // (CHUNKS * P))
ET = CHUNKS * BLOCKS
EP = ET * P
CE = BLOCKS * P
U = 8
H = U // 2
ROUNDS = ET // U
MSG = D + HEADS
PAD_NODE = NP - 1
FAR = 1e37
LN_EPS, MIX_EPS = 1e-5, 1e-5
CAPACITY = float(-(-int(N_NODES * 1.25) // EXPERTS)) if (N_NODES * 1.25) % 1 == 0 else float(
    -(-int(N_NODES * 1.25 + 1) // EXPERTS))
assert NT == G * NG and ET == U * ROUNDS

C_IDENT, C_BLOCK, C_IOTA = 0, P, 2 * P
C_BASE = 3 * P
C_NODE = C_BASE + NT
C_REAL = C_NODE + NT
C_END = C_REAL + 1


def reuse(u, ring, n=G):
    return u - ring + 1 if u >= ring else max(w for w in range(n) if w % ring == u) + 1 - n


class Steps:

    def __init__(self, eng, sem):
        self.eng, self.sem, self.base, self.k, self.i, self.n = eng, sem, 0, 0, None, 0

    def done(self, ins):
        ins.then_inc(self.sem, 1)
        self.k += 1

    def value(self):
        return self.base + self.k if self.i is None else self.i * self.n + (self.base + self.k)

    def link(self, ins):
        self.done(ins)
        self.eng.wait_ge(self.sem, self.value())

    def enter(self, i, n, first):
        self.base, self.k, self.i, self.n = self.base + self.k - first * n, 0, i, n

    def leave(self, last):
        assert self.k == self.n, (self.k, self.n)
        self.base, self.k, self.i = self.base + last * self.n, 0, None


def gps_layer(nc, a, out, dram):
    ctx = ExitStack()
    with ctx:
        def sb(stack, name, shape, dt=FP32):
            return stack.enter_context(nc.sbuf_tensor(name, shape, dt))

        def sem(name):
            return ctx.enter_context(nc.semaphore(name))

        r1 = sb(ctx, "r1", [P, NT * D + 2])
        r2 = sb(ctx, "r2", [P, NT * MSG])
        r3 = sb(ctx, "r3", [P, NT * D])
        const = sb(ctx, "const", [P, C_END])
        rows = sb(ctx, "rows", [P, 3 * D])
        bank = [ctx.enter_context(nc.psum_tensor(f"bank{i}", [P, 512], FP32)) for i in range(8)]
        ident = const[:, C_IDENT:C_IDENT + P]
        tiles = lambda r: r[:, 0:NT * D].rearrange("p (t d) -> p t d", d=D)
        X, XT_ALL, FDST = tiles(r1), tiles(r2), tiles(r3)

        node_phase(nc, ctx, sb, sem, a, dram, X, XT_ALL, FDST, const, rows, bank, ident)
        scores = r1[:, 0:ET * HEADS]
        weights = r1[:, ET * HEADS:2 * ET * HEADS]
        score_phase(nc, ctx, sb, sem, a, dram, FDST, scores, const, rows, bank, ident)
        softmax_phase(nc, ctx, sb, sem, a, r2, r3, scores, r1, bank, ident, weights)
        message_phase(nc, ctx, sb, sem, a, dram, weights, r2, const, bank)
        combine_phase(nc, ctx, sb, sem, dram, r2, tiles(r3))
        ffn_phase(nc, ctx, sb, sem, a, out, tiles(r3), r1, r2, const, bank, ident)


def node_phase(nc, ctx, sb, sem, a, dram, X, XT_ALL, FDST, const, rows, bank, ident):
    with ExitStack() as loc:
        wcat = sb(loc, "wcat", [P, 2, 3 * D])
        stats = sb(loc, "stats", [P, G, 6])
        aggr = sb(loc, "aggr", [P, G, 2])
        mv = sb(loc, "mv", [P, NT, 2])
        rs = sb(loc, "rs", [P, 4, NT])
        xn = sb(loc, "xn", [P, G, D])
        xt = sb(loc, "xt", [P, G, D])
        dz = sb(loc, "dz", [P, G, D])
        sq = sb(loc, "sq", [P, G, D])
        z = sb(loc, "z", [P, G, 2, P + 1])
        small = sb(loc, "small", [P, 4, G * HEADS])
        pj = sb(loc, "pj", [P, 2, 2 * D])
        hst = sb(loc, "hst", [P, G, D])
        kvw = sq[:, 0:4, :].rearrange("p a d -> p (a d)")
        kvc, cols = sq[:, 4, 0:4], sq[:, 4, 8:16]
        kv = dz[:, 0, :].rearrange("p (f q) -> p f q", f=2)
        tmp = dz[:, 1, :].rearrange("p (f q) -> p f q", f=2)
        x_loaded, stats_done = sem("x_loaded"), sem("stats_done")
        x_in, w_in, ones_set = sem("x_in"), sem("w_in"), sem("ones_set")
        dve_a, dve_b = sem("dve_a"), sem("dve_b")
        rstd_sq = sem("rstd_sq")
        var_ready = sem("var_ready")
        xn_ready, xt_in_psum, xt_ready, xt_kept = sem("xn_ready"), sem("xt_in_psum"), sem("xt_ready"), sem("xt_kept")
        dz_ready, sq_ready, ss_ready, sd_ready, z_ready = (
            sem("dz_ready"), sem("sq_ready"), sem("ss_ready"), sem("sd_ready"), sem("z_ready"))
        pj_in_psum, pj_ready, pj_stored = sem("pj_in_psum"), sem("pj_ready"), [sem("pj_stored0"), sem("pj_stored1")]
        pj_free = sem("pj_free")
        gram_done, proj_done, h_ready, h_stored = sem("gram_done"), sem("proj_done"), sem("h_ready"), sem("h_stored")
        x_rows = a["x"].rearrange("(t p) d -> p t d", p=P)
        tab_rows = dram["tab"].rearrange("(t p) d -> p t d", p=P)
        h_rows = dram["h"].rearrange("(t p) d -> p t d", p=P)
        base_rows = dram["base"].rearrange("(t p) d -> p t d", p=P)
        srow, scol = sem("srow"), sem("scol")
        mu = lambda t: mv[:, bass.ds(t, 1), 0:1].rearrange("p a b -> p (a b)")
        col = lambda k, t: rs[:, k, bass.ds(t, 1)]
        DVE_A0 = 2 * G + 1

        with nc.Block() as block:
            @block.sync
            def _(sp):
                sp.dma_start(wcat[:, :, :], a["wcat"]).then_inc(w_in, 16)
                sp.dma_start(const[:, :], a["const"]).then_inc(w_in, 16)
                sp.dma_start(rows[:, :], a["proj_bias"].partition_broadcast(P)).then_inc(w_in, 16)
                with sp.Fori(0, NG) as g:
                    sp.dma_start(X[:, bass.ds(g * G, G), :], x_rows[:, bass.ds(g * G, G), :]).then_inc(x_in, 16)
                    sp.wait_ge(x_in, g * 16 + 16)
                    sp.sem_inc(x_loaded, 1)

            @block.gpsimd
            def _(pool):
                pool.memset(z[:, :, :, P:P + 1], 1.0).then_inc(ones_set, 1)

            @block.vector
            def _(dve):
                st = Steps(dve, dve_a)
                with dve.Fori(0, NG) as g:
                    st.enter(g, DVE_A0, 0)
                    dve.wait_ge(x_in, g * 16 + 16)
                    for u in range(G - 1):
                        st.done(dve.bn_stats(stats[:, u, :], X[:, bass.ds(g * G + u, 1), :].rearrange("p a d -> p (a d)")))
                    st.link(dve.bn_stats(stats[:, G - 1, :], X[:, bass.ds(g * G + G - 1, 1), :].rearrange("p a d -> p (a d)")))
                    dve.sem_inc(stats_done, 1)
                    for u in range(G - 1):
                        st.done(dve.bn_aggr(aggr[:, u, :], stats[:, u, :]))
                    st.link(dve.bn_aggr(aggr[:, G - 1, :], stats[:, G - 1, :]))
                    st.link(dve.tensor_copy(mv[:, bass.ds(g * G, G), :], aggr[:, :, :]))
                    st.leave(NG)
                var = mv[:, :, 1:2].rearrange("p t o -> p (t o)")
                dve.tensor_scalar(rs[:, 0, :], var, LN_EPS, None, ALU.add).then_inc(var_ready, 1)
                dve.wait_ge(rstd_sq, 1)
                st.link(dve.reciprocal(rs[:, 0, :], rs[:, 2, :]))
                st.link(dve.tensor_tensor(rs[:, 3, :], var, rs[:, 0, :], ALU.mult))
                st.link(dve.tensor_tensor(rs[:, 3, :], rs[:, 3, :], rs[:, 0, :], ALU.mult))
                dve.tensor_scalar(rs[:, 3, :], rs[:, 3, :], LN_EPS, None, ALU.add).then_inc(var_ready, 1)
                dve.wait_ge(rstd_sq, 2)
                st.link(dve.reciprocal(rs[:, 1, :], rs[:, 2, :]))

            @block.scalar
            def _(act):
                act.wait_ge(var_ready, 1)
                act.activation(rs[:, 2, :], rs[:, 0, :], ACT.Sqrt).then_inc(rstd_sq, 1)
                act.wait_ge(var_ready, 2)
                act.activation(rs[:, 2, :], rs[:, 3, :], ACT.Sqrt).then_inc(rstd_sq, 1)

        heads = lambda r: r[:, :, :].rearrange("p t (h c) -> p (t h) c", c=HC)
        bc = lambda c: c.unsqueeze(2).to_broadcast([P, G * HEADS, HC])
        N_DVE_B = 6

        with nc.Block() as block:
            @block.vector
            def _(dve):
                st = Steps(dve, dve_b)

                def evac(g, us):
                    for u in us:
                        dve.wait_ge(pj_in_psum, g * G + (u + 1))
                        s = u % 2
                        if not (isinstance(g, int) and g == 0 and u < 2):
                            dve.wait_ge(pj_free, g * G + reuse(u, 2))
                        b = (bank[2], bank[3]) if s == 0 else (bank[4], bank[5])
                        dve.scalar_tensor_tensor(pj[:, s, :], b[0][:, :], col(1, g * G + u), rows[:, 0:2 * D],
                                                 ALU.mult, ALU.add).then_inc(pj_ready, 1)
                        dve.scalar_tensor_tensor(FDST[:, bass.ds(g * G + u, 1), :].rearrange("p a d -> p (a d)"),
                                                 b[1][:, 0:D], col(1, g * G + u), rows[:, 2 * D:3 * D],
                                                 ALU.mult, ALU.add).then_inc(proj_done, 1)

                def group(g, before):
                    first = isinstance(g, int) and g == 0
                    if not first:
                        dve.wait_ge(xt_in_psum, g * 4)
                        dve.wait_ge(h_ready, g * G)
                    for u in range(G):
                        t = g * G + u
                        dve.tensor_scalar(xn[:, u, :], X[:, bass.ds(t, 1), :].rearrange("p a d -> p (a d)"),
                                          mu(t), col(0, t), ALU.subtract, ALU.mult).then_inc(xn_ready, 1)
                    before(range(0, 3))
                    dve.wait_ge(xn_ready, g * G + G)
                    st.link(dve.tensor_reduce(small[:, 0, :], heads(xn), AX.X, ALU.add))
                    before(range(3, 4))
                    if not first:
                        dve.wait_ge(z_ready, g)
                    dve.scalar_tensor_tensor(heads(dz), bc(small[:, 0, :]), -1.0 / HC, heads(xn),
                                             ALU.mult, ALU.add).then_inc(dz_ready, 1)
                    before(range(4, 6))
                    dve.wait_ge(sq_ready, g + 1)
                    dve.tensor_reduce(small[:, 1, :], heads(sq), AX.X, ALU.add).then_inc(ss_ready, 1)
                    before(range(6, 7))
                    dve.wait_ge(sd_ready, g + 1)
                    st.link(dve.tensor_scalar(small[:, 2, :], small[:, 2, :], MIX_EPS, None, ALU.add))
                    st.link(dve.reciprocal(small[:, 3, :], small[:, 2, :]))
                    if not first:
                        dve.wait_ge(gram_done, g)
                    dve.wait_ge(dz_ready, g + 1)
                    zz = z[:, :, :, 0:P].rearrange("p t f (h c) -> p (t f) h c", c=HC)
                    zi = dz[:, :, :].rearrange("p t (f h c) -> p (t f) h c", f=2, c=HC)
                    zr = small[:, 3, :].rearrange("p (t h) -> p t h", h=4).unsqueeze(3).to_broadcast(
                        [P, 2 * G, 4, HC])
                    dve.tensor_tensor(zz, zi, zr, ALU.mult).then_inc(z_ready, 1)

                st.enter(None, 3, 0)
                group(0, lambda us: None)
                group(1, lambda us: evac(0, us))
                with dve.Fori(2, NG) as g:
                    st.enter(g, 3, 2)
                    group(g, lambda us: evac(g - 1, us))
                    st.leave(NG)
                for u in range(G):
                    evac(NG - 1, [u])

            @block.scalar
            def _(act):
                def group(g):
                    first = isinstance(g, int) and g == 0
                    if not first:
                        act.wait_ge(pj_in_psum, g * G)
                        act.wait_ge(xt_kept, g)
                    for k in range(4):
                        n = min(2, G - 2 * k)
                        act.wait_ge(xt_in_psum, g * 4 + (k + 1))
                        act.activation(xt[:, 2 * k:2 * k + n, :].rearrange("p t d -> p (t d)"),
                                       bank[k % 2][:, 0:n * D], ACT.Copy).then_inc(xt_ready, 1)
                    act.wait_ge(dz_ready, g + 1)
                    act.activation(sq[:, :, :], dz[:, :, :], ACT.Square).then_inc(sq_ready, 1)
                    act.wait_ge(ss_ready, g + 1)
                    act.activation(small[:, 2, :], small[:, 1, :], ACT.Sqrt, scale=1.0 / (HC - 1)).then_inc(sd_ready, 1)
                    if not first:
                        act.wait_ge(h_stored, g * 16)
                    for u in range(G):
                        act.activation(hst[:, u, :], xn[:, u, :], ACT.Copy, scale=col(1, g * G + u)).then_inc(h_ready, 1)

                group(0)
                with act.Fori(1, NG) as g:
                    group(g)

            @block.gpsimd
            def _(pool):
                with pool.Fori(0, NG) as g:
                    pool.wait_ge(xt_ready, g * 4 + 4)
                    pool.tensor_copy(XT_ALL[:, bass.ds(g * G, G), :], xt[:, :, :]).then_inc(xt_kept, 1)

            @block.tensor
            def _(pe):
                def gram(g, start=False, stop=False):
                    pe.wait_ge(z_ready, g + 1)
                    for u in range(G):
                        for f in range(2):
                            last = pe.matmul(bank[6 + f][:, 0:P + 1], z[:, u, f, 0:P], z[:, u, f, :],
                                             start=start and u == 0, stop=stop and u == G - 1)
                    last.then_inc(gram_done, 1)

                def group(g, before):
                    first = isinstance(g, int) and g == 0
                    for k in range(4):
                        n = min(2, G - 2 * k)
                        pe.wait_ge(xn_ready, g * G + (2 * k + n))
                        if not (first and k < 2):
                            pe.wait_ge(xt_ready, g * 4 + (k - 1))
                        for u in range(n):
                            for f in range(2):
                                last = pe.transpose(bank[k % 2][:, (2 * u + f) * P:(2 * u + f + 1) * P],
                                                    xn[:, 2 * k + u, f * P:(f + 1) * P], ident)
                        last.then_inc(xt_in_psum, 1)
                    before()
                    for u in range(G):
                        if u % 2 == 0:
                            pe.wait_ge(xt_ready, g * 4 + (u // 2 + 1))
                        if not (first and u < 2):
                            pe.wait_ge(proj_done, g * G + reuse(u, 2))
                        b = (bank[2], bank[3]) if u % 2 == 0 else (bank[4], bank[5])
                        for f in range(2):
                            w = xt[:, u, f * P:(f + 1) * P]
                            pe.matmul(b[0][:, :], w, wcat[:, f, 0:2 * D], start=f == 0, stop=f == 1)
                            last = pe.matmul(b[1][:, 0:D], w, wcat[:, f, 2 * D:3 * D], start=f == 0, stop=f == 1)
                        last.then_inc(pj_in_psum, 1)

                group(0, lambda: None)
                gram(0, start=True)
                with pe.Fori(1, NG - 1) as g:
                    group(g, lambda: None)
                    gram(g)
                group(NG - 1, lambda: None)
                gram(NG - 1, stop=True)

            @block.sync
            def _(sp):
                def store(g):
                    for u in range(G):
                        s = u % 2
                        sp.wait_ge(pj_ready, g * G + (u + 1))
                        sp.dma_start(tab_rows[:, bass.ds(g * G + u, 1), :].rearrange("p a d -> p (a d)"),
                                     pj[:, s, :]).then_inc(pj_stored[0], 16)
                        sp.wait_ge(pj_stored[0], (g * G + (u + 1)) * 16)
                        sp.sem_inc(pj_free, 1)
                        if u == G - 1:
                            sp.wait_ge(h_ready, g * G + G)
                            sp.dma_start(h_rows[:, bass.ds(g * G, G), :], hst[:, :, :]).then_inc(h_stored, 16)
                with sp.Fori(0, NG) as g:
                    store(g)
                sp.wait_ge(h_stored, NG * 16)

        dve_k, kv_ready, row_in_psum, kvin = sem("dve_k"), sem("kv_ready"), sem("row_in_psum"), sem("kvin")
        xt_again, mix_in_psum, base_ready, base_stored = (
            sem("xt_again"), sem("mix_in_psum"), sem("base_ready"), sem("base_stored"))
        WKB, BKB, WVB, BVB = 0, 1, 2, 3

        with nc.Block() as block:
            @block.sync
            def _(sp):
                sp.dma_start(kvw[:, :], a["mix_rows"].partition_broadcast(P)).then_inc(kvin, 16)
                sp.dma_start(kvc[:, :], a["mix_cols"]).then_inc(kvin, 16)
                with sp.Fori(0, NG) as g:
                    sp.wait_ge(base_ready, g * G + G)
                    sp.dma_start(base_rows[:, bass.ds(g * G, G), :], hst[:, :, :]).then_inc(base_stored, 16)
                sp.wait_ge(base_stored, NG * 16)

            @block.vector
            def _(dve):
                st = Steps(dve, dve_k)
                dve.wait_ge(kvin, 32)
                for f in range(2):
                    st.link(dve.tensor_copy(cols[:, f:f + 1], bank[6 + f][:, P:P + 1]))
                    dve.tensor_copy(tmp[:, f, :], cols[:, f:f + 1].to_broadcast([P, P])).then_inc(scol, 1)
                for f in range(2):
                    wk, bk = kvc[:, f:f + 1], kvc[:, 2 + f:3 + f]
                    wv = kvw[:, 2 * D + f * P:2 * D + (f + 1) * P]
                    bv = kvw[:, 3 * D + f * P:3 * D + (f + 1) * P]
                    o = kv[:, f, :]
                    dve.wait_ge(row_in_psum, f + 1)
                    st.link(dve.tensor_scalar(o, bank[6 + f][:, 0:P], wk, None, ALU.mult))
                    st.link(dve.scalar_tensor_tensor(o, bank[f][:, 0:P], bk, o, ALU.mult, ALU.add))
                    st.link(dve.tensor_tensor(o, o, wv, ALU.mult))
                    st.link(dve.tensor_tensor(cols[:, 2:3], cols[:, f:f + 1], wk, ALU.mult))
                    st.link(dve.scalar_tensor_tensor(cols[:, 3:4], bk, float(N_NODES), cols[:, 2:3], ALU.mult, ALU.add))
                    st.link(dve.scalar_tensor_tensor(o, bv, cols[:, 3:4], o, ALU.mult, ALU.add))
                    st.link(dve.scalar_tensor_tensor(o, o, 1.0 / N_NODES, const[:, C_BLOCK:C_BLOCK + P],
                                                     ALU.mult, ALU.mult))
                    dve.tensor_tensor(o, o, ident, ALU.add).then_inc(kv_ready, 1)

                def group(g):
                    if not isinstance(g, int):
                        dve.wait_ge(base_stored, g * 16)
                    for u in range(G):
                        dve.wait_ge(mix_in_psum, g * G + (u + 1))
                        dve.tensor_tensor(hst[:, u, :], bank[2 + u % 4][:, 0:D],
                                          X[:, bass.ds(g * G + u, 1), :].rearrange("p a d -> p (a d)"),
                                          ALU.add).then_inc(base_ready, 1)
                group(0)
                with dve.Fori(1, NG) as g:
                    group(g)

            @block.scalar
            def _(act):
                act.activation(xt[:, :, :], XT_ALL[:, 0:G, :], ACT.Copy).then_inc(xt_again, 1)
                with act.Fori(1, NG) as g:
                    act.wait_ge(mix_in_psum, g * G)
                    act.activation(xt[:, :, :], XT_ALL[:, bass.ds(g * G, G), :], ACT.Copy).then_inc(xt_again, 1)

            @block.tensor
            def _(pe):
                for f in range(2):
                    pe.wait_ge(scol, f + 1)
                    pe.matmul(bank[f][:, 0:P], tmp[:, f, :], ident, start=True, stop=True).then_inc(row_in_psum, 1)
                pe.wait_ge(kv_ready, 2)

                def group(g):
                    pe.wait_ge(xt_again, g + 1)
                    for u in range(G):
                        if not (isinstance(g, int) and u < 4):
                            pe.wait_ge(base_ready, g * G + reuse(u, 4))
                        for f in range(2):
                            last = pe.matmul(bank[2 + u % 4][:, f * P:(f + 1) * P], xt[:, u, f * P:(f + 1) * P],
                                             kv[:, f, :], start=True, stop=True)
                        last.then_inc(mix_in_psum, 1)
                group(0)
                with pe.Fori(1, NG) as g:
                    group(g)


def pair_loop(eng, cur, prev, last, first_pair, extra_pair):
    d0 = eng.snap(cur, min_val=0, max_val=NT - 1)
    first_pair(d0)
    with eng.If(last > d0):
        with eng.Fori(d0 + 1, last + 1) as d:
            extra_pair(d)
        eng.nop()
    eng.nop()
    eng.reg_mov(prev, cur)
    eng.reg_mov(cur, last)


def score_phase(nc, ctx, sb, sem, a, dram, FDST, scores, const, rows, bank, ident):
    with ExitStack() as loc:
        src = sb(loc, "src", [P, ET], I32)
        dlast = sb(loc, "dlast", [1, ET // H], I32)
        dline = sb(loc, "dline", [112, EP // 112], I32)
        dline16 = sb(loc, "dline16", [112, EP // 112], I16)
        idx = sb(loc, "idx", [P, U], I32)
        gath = sb(loc, "gath", [P, U, 2 * D])
        dstb = sb(loc, "dstb", [P, 2, 4 * P], I16)
        oht = sb(loc, "oht", [P, 2, H * P])
        sil = sb(loc, "sil", [P, 4, 2 * D])
        attn = sb(loc, "attn", [P, 2 * D])
        mark = sb(loc, "mark", [P, 1])
        mul_done = sem("mul_done")
        slot_free = sem("slot_free")
        in_s, d16, d16_out, dl = sem("in_s"), sem("d16"), sem("d16_out"), sem("dl")
        idx_set = sem("idx_set")
        g_in = [sem(f"g_in{u}") for u in range(U)]
        fv_out = [sem(f"fv_out{k}") for k in range(U // 2)]
        dstb_in = [sem("dstb_in0"), sem("dstb_in1")]
        oht_ready, oht_used, z_done, sil_done, score_done, prod_done = (
            sem("oht_ready"), sem("oht_used"), sem("z_done"), sem("sil_done"), sem("score_done"), sem("prod_done"))
        fv_rows = dram["fv"].rearrange("(t p) d -> p t d", p=P)
        W112 = EP // 112
        d16_line = dram["d16"].rearrange("(q w) -> q w", w=W112)

        with nc.Block() as block:
            @block.sync
            def _(sp):
                sp.dma_start(src[:, :], a["src_t"]).then_inc(in_s, 16)
                sp.dma_start(dline[:, :], a["dst_line"].rearrange("(q w) -> q w", w=W112)).then_inc(in_s, 16)
                sp.dma_start(dlast[0:1, :], a["dst_last"]).then_inc(in_s, 16)
                sp.dma_start(attn[:, 0:D], a["attn"].partition_broadcast(P)).then_inc(in_s, 16)
                sp.dma_start(attn[:, D:2 * D], a["attn"].partition_broadcast(P)).then_inc(in_s, 16)
                sp.wait_ge(d16, 1)
                sp.dma_start(d16_line, dline16[:, :]).then_inc(d16_out, 16)
                sp.wait_ge(d16_out, 16)

            @block.vector
            def _(dve):
                dve.wait_ge(in_s, 80)
                dve.tensor_copy(dline16[:, :], dline[:, :]).then_inc(d16, 1)
                dve.tensor_scalar(dlast[0:1, :], dlast[0:1, :], 7, None, ALU.arith_shift_right).then_inc(dl, 1)

        def dtile(eng, s):
            return eng.value_load(dlast[0:1, bass.ds(s, 1)], min_val=0, max_val=NT - 1)

        with nc.Block() as block:
            @block.gpsimd
            def _(pool):
                def rnd(i):
                    first = isinstance(i, int)
                    for u in range(U):
                        if u % 4 == 0:
                            if not first:
                                for v in range(u, u + 4):
                                    pool.wait_ge(g_in[v], i * 16)
                            pool.tensor_copy(idx[:, u:u + 4], src[:, bass.ds(i * U + u, 4)]).then_inc(idx_set, 1)
                            pool.wait_ge(idx_set, i * 2 + (u // 4 + 1))
                            pool.sem_inc(slot_free, 1)
                        if not first:
                            pool.wait_ge(z_done, i * U + (u - U + 1))
                            pool.wait_ge(fv_out[u // 2], i * 16)
                            pool.sem_inc(slot_free, 1)
                        pool.indirect_dma_start(gath[:, u, :], None, dram["tab"],
                                                bass.IndirectOffsetOnAxis(ap=idx[:, u:u + 1].bitcast(U32), axis=0)
                                                ).then_inc(g_in[u], 16)
                rnd(0)
                with pool.Fori(1, ROUNDS) as i:
                    rnd(i)

            @block.sync
            def _(sp):
                def rnd(i):
                    first = isinstance(i, int)
                    for hf in range(2):
                        if not first:
                            sp.wait_ge(prod_done, (i - 1) * 2 + (hf + 1))
                        sp.dma_start(dstb[:, hf, :],
                                     dram["d16"][bass.ds((i * 2 + hf) * 4 * P, 4 * P)].partition_broadcast(P)
                                     ).then_inc(dstb_in[hf], 16)
                    for k in range(U // 2):
                        for u in (2 * k, 2 * k + 1):
                            sp.wait_ge(g_in[u], i * 16 + 16)
                        sp.dma_start(fv_rows[:, bass.ds(i * U + 2 * k, 2), :],
                                     gath[:, 2 * k:2 * k + 2, D:2 * D]).then_inc(fv_out[k], 16)
                rnd(0)
                with sp.Fori(1, ROUNDS) as i:
                    rnd(i)
                for k in range(U // 2):
                    sp.wait_ge(fv_out[k], ROUNDS * 16)

            @block.vector
            def _(dve):
                cur, prev = dve.alloc_register("cur_s1v"), dve.alloc_register("prev_s1v")
                dve.reg_mov(cur, 0)
                dve.reg_mov(prev, 0)

                def one_hot(hf, d):
                    return dve.tensor_scalar(oht[:, hf, :], dstb[:, hf, :],
                                             const[:, bass.ds(d + C_NODE, 1)], None, ALU.is_equal)

                def onehots(i, hf, first):
                    s = i * 2 + hf
                    last = dtile(dve, s)
                    dve.wait_ge(dstb_in[hf], i * 16 + 16)

                    def first_pair(d):
                        if not first:
                            dve.wait_ge(oht_used, dve.snap(prev, min_val=0, max_val=NT - 1) + (s - 1))
                        one_hot(hf, d).then_inc(oht_ready, 1)

                    def extra_pair(d):
                        dve.wait_ge(oht_used, d + s)
                        one_hot(hf, d).then_inc(oht_ready, 1)
                    pair_loop(dve, cur, prev, last, first_pair, extra_pair)

                def score(i, k):
                    dve.wait_ge(sil_done, i * 4 + (k + 1))
                    dve.tensor_tensor(sil[:, k, :], sil[:, k, :], attn[:, :], ALU.mult).then_inc(mul_done, 1)
                    dve.wait_ge(mul_done, i * 4 + (k + 1))
                    dve.tensor_reduce(scores[:, bass.ds((i * U + 2 * k) * HEADS, 2 * HEADS)],
                                      sil[:, k, :].rearrange("p (q c) -> p q c", c=HC), AX.X, ALU.add
                                      ).then_inc(score_done, 1)

                def rnd(i):
                    first = isinstance(i, int)
                    for hf in range(2):
                        onehots(i, hf, first)
                        if not first:
                            score(i - 1, 2 * hf)
                        if hf or not first:
                            dve.wait_ge(prod_done, i * 2 + hf)
                        dve.tensor_copy(mark[:, :], ident[:, 0:1]).then_inc(prod_done, 1)
                        if not first:
                            score(i - 1, 2 * hf + 1)
                rnd(0)
                with dve.Fori(1, ROUNDS) as i:
                    rnd(i)
                for k in range(4):
                    score(ROUNDS - 1, k)

            @block.tensor
            def _(pe):
                cur, prev = pe.alloc_register("cur_s1p"), pe.alloc_register("prev_s1p")
                pe.reg_mov(cur, 0)
                dest = lambda u: bank[u // 2][:, (u % 2) * D:(u % 2 + 1) * D]

                def rnd(i):
                    first = isinstance(i, int)
                    for hf in range(2):
                        s = i * 2 + hf
                        last = dtile(pe, s)
                        us = range(hf * H, hf * H + H)
                        if not first:
                            pe.wait_ge(sil_done, i * 4 + (2 * hf - 2))

                        def pair(d, start):
                            pe.wait_ge(oht_ready, d + (s + 1))
                            for u in us:
                                ins = pe.matmul(dest(u), oht[:, hf, (u % H) * P:(u % H + 1) * P],
                                                FDST[:, bass.ds(d, 1), :].rearrange("p a d -> p (a d)"),
                                                start=start and u % 2 == 0, stop=False, skip_group_check=True)
                            ins.then_inc(oht_used, 1)
                        pair_loop(pe, cur, prev, last, lambda d: pair(d, True), lambda d: pair(d, False))
                        for u in us:
                            pe.wait_ge(g_in[u], i * 16 + 16)
                            pe.matmul(dest(u), ident, gath[:, u, 0:D], start=False, stop=True,
                                      skip_group_check=True).then_inc(z_done, 1)
                rnd(0)
                with pe.Fori(1, ROUNDS) as i:
                    rnd(i)

            @block.scalar
            def _(act):
                def rnd(i):
                    for k in range(4):
                        act.wait_ge(z_done, i * U + (2 * k + 2))
                        if not isinstance(i, int):
                            act.wait_ge(score_done, i * 4 + (k - 3))
                        act.activation(sil[:, k, :], bank[k][:, :], ACT.Silu).then_inc(sil_done, 1)
                rnd(0)
                with act.Fori(1, ROUNDS) as i:
                    rnd(i)


def softmax_phase(nc, ctx, sb, sem, a, r2, r3, scores, r1, bank, ident, weights):
    with ExitStack() as loc:
        stage = sb(loc, "stage", [P, G, P])
        stage2 = sb(loc, "stage2", [P, G, P])
        line = sb(loc, "line", [1, 4 * P])
        colv = sb(loc, "colv", [P, 8])
        dst_c = r1[:, ET * HEADS:ET * HEADS + CE + 2].bitcast(I32)
        brk = r2[:, 0:CE + 1]
        sc = r3[:, 0:CE]
        run = r2[:, CE + 1:2 * CE + 1]
        top = r3[:, CE:2 * CE]
        brow = sb(loc, "brow", [1, P])
        in_c, dvs, staged, tin, tout = sem("in_c"), sem("dvs"), sem("staged"), sem("tin"), sem("tout")
        lt, lf = sem("lt"), sem("lf")
        sc4 = scores.rearrange("p (j b h) -> p b h j", b=BLOCKS, h=HEADS)
        w4 = weights.rearrange("p (j b h) -> p b h j", b=BLOCKS, h=HEADS)

        with nc.Block() as block:
            @block.sync
            def _(sp):
                for h in range(HEADS):
                    sp.dma_start(dst_c[h * CHUNKS:(h + 1) * CHUNKS, :], a["dst_chunks"]).then_inc(in_c, 16)

            @block.scalar
            def _(act):
                def group(g):
                    if not isinstance(g, int):
                        act.wait_ge(tin, g * 2)
                    for u in range(G):
                        act.activation(stage[:, u, :].rearrange("p (h j) -> p h j", h=HEADS),
                                       sc4[:, bass.ds(g * G + u, 1), :, :].rearrange("p a h j -> p (a h) j"),
                                       ACT.Copy).then_inc(staged, 1)
                group(0)
                with act.Fori(1, NG) as g:
                    group(g)

            @block.tensor
            def _(pe):
                def group(g):
                    for k in range(2):
                        if not isinstance(g, int):
                            pe.wait_ge(tout, g * 2 + (k - 1))
                        n = 4 - k
                        pe.wait_ge(staged, g * G + (4 * k + n))
                        for u in range(n):
                            last = pe.transpose(bank[k][:, u * P:(u + 1) * P], stage[:, 4 * k + u, :], ident)
                        last.then_inc(tin, 1)
                group(0)
                with pe.Fori(1, NG) as g:
                    group(g)
                for r in range(2):
                    pe.wait_ge(lt, 2 * r + 1)
                    for k in range(2):
                        last = pe.transpose(bank[2][0:1, k * P:(k + 1) * P], colv[:, k:k + 1], ident)
                    last.then_inc(lf, 1)
                    pe.wait_ge(lt, 2 * r + 2)
                    pe.matmul(bank[3][:, 0:1], brow[0:1, :], ident[0:1, 0:1], start=True, stop=True).then_inc(lf, 1)

            @block.vector
            def _(dve):
                st = Steps(dve, dvs)
                with dve.Fori(0, NG) as g:
                    for k in range(2):
                        n = 4 - k
                        dve.wait_ge(tin, g * 2 + (k + 1))
                        dve.tensor_copy(sc[:, bass.ds((g * G + 4 * k) * P, n * P)], bank[k][:, 0:n * P]).then_inc(tout, 1)
                dve.wait_ge(in_c, HEADS * 16)
                st.link(dve.tensor_tensor(brk, dst_c[:, 0:CE + 1], dst_c[:, 1:CE + 2], ALU.not_equal))
                st.link(dve.tensor_scalar(brk, brk, -FAR, None, ALU.mult))
                st.link(dve.tensor_reduce(colv[:, 2:3], brk[:, 1:CE], AX.X, ALU.min))
                dve.wait_ge(tout, NG * 2)

                def scan(dst, rev, init):
                    if rev:
                        return dve.tensor_tensor_scan(dst[:, ::-1], brk[:, CE:0:-1], run[:, ::-1], init, ALU.add, ALU.max)
                    return dve.tensor_tensor_scan(dst, brk[:, 0:CE], sc, init, ALU.add, ALU.max)

                for r in range(2):
                    dst = top if r else run
                    st.link(scan(dst, r, -FAR))
                    st.link(dve.tensor_copy(colv[:, 0:1], dst[:, 0:1] if r else dst[:, CE - 1:CE]))
                    edge = brk[:, CE:CE + 1] if r else brk[:, 0:1]
                    dve.tensor_tensor(colv[:, 1:2], edge, colv[:, 2:3], ALU.add).then_inc(lt, 1)
                    dve.wait_ge(lf, 2 * r + 1)
                    st.link(dve.tensor_copy(line[:, 0:2 * P], bank[2][0:1, 0:2 * P]))
                    if r:
                        st.link(dve.tensor_tensor_scan(line[:, 3 * P - 1:2 * P - 1:-1], line[:, 2 * P - 1:P - 1:-1],
                                                       line[:, P - 1::-1], -FAR, ALU.add, ALU.max))
                    else:
                        st.link(dve.tensor_tensor_scan(line[:, 2 * P:3 * P], line[:, P:2 * P], line[:, 0:P],
                                                       -FAR, ALU.add, ALU.max))
                    st.link(dve.memset(brow[:, :], -FAR))
                    hj = lambda v: v.rearrange("p (h j) -> p h j", j=CHUNKS)
                    to, of = (slice(0, CHUNKS - 1), slice(1, CHUNKS)) if r else (slice(1, CHUNKS), slice(0, CHUNKS - 1))
                    dve.tensor_copy(hj(brow[:, :])[:, :, to], hj(line[:, 2 * P:3 * P])[:, :, of]).then_inc(lt, 1)
                    dve.wait_ge(lf, 2 * r + 2)
                    st.link(dve.tensor_copy(colv[:, 3 + r:4 + r], bank[3][:, 0:1]))
                    st.link(scan(dst, r, colv[:, 3 + r:4 + r]))

        sub, ex, wps, wev = sem("sub"), sem("ex"), sem("wps"), sem("wev")
        with nc.Block() as block:
            @block.vector
            def _(dve):
                def group(g):
                    if not isinstance(g, int):
                        dve.wait_ge(wps, g * 2)
                    sl = bass.ds(g * G * P, G * P)
                    dve.tensor_tensor(stage[:, :, :].rearrange("p u q -> p (u q)"), sc[:, sl], top[:, sl],
                                      ALU.subtract).then_inc(sub, 1)
                    for k in range(2):
                        n = 4 - k
                        dve.wait_ge(wps, g * 2 + (k + 1))
                        for u in range(n):
                            ins = dve.tensor_copy(
                                w4[:, bass.ds(g * G + 4 * k + u, 1), :, :].rearrange("p a h j -> p (a h) j"),
                                bank[k][:, u * P:(u + 1) * P].rearrange("p (h j) -> p h j", h=HEADS))
                        ins.then_inc(wev, 1)
                group(0)
                with dve.Fori(1, NG) as g:
                    group(g)

            @block.scalar
            def _(act):
                def group(g):
                    act.wait_ge(sub, g + 1)
                    if not isinstance(g, int):
                        act.wait_ge(wps, g * 2)
                    act.activation(stage2[:, :, :], stage[:, :, :], ACT.Exp).then_inc(ex, 1)
                group(0)
                with act.Fori(1, NG) as g:
                    group(g)

            @block.tensor
            def _(pe):
                def group(g):
                    pe.wait_ge(ex, g + 1)
                    for k in range(2):
                        if not isinstance(g, int):
                            pe.wait_ge(wev, g * 2 + (k - 1))
                        for u in range(4 - k):
                            last = pe.transpose(bank[k][:, u * P:(u + 1) * P], stage2[:, 4 * k + u, :], ident)
                        last.then_inc(wps, 1)
                group(0)
                with pe.Fori(1, NG) as g:
                    group(g)


def message_phase(nc, ctx, sb, sem, a, dram, weights, r2, const, bank):
    with ExitStack() as loc:
        dlast = sb(loc, "dlast2", [1, ET // H], I32)
        dst = sb(loc, "dst2", [P, ET], I32)
        dstf = sb(loc, "dstf", [P, ET])
        fv = sb(loc, "fv", [P, U, D])
        msg = sb(loc, "msg", [P, U, MSG])
        oh = sb(loc, "oh", [P, 2, H, P])
        zero = sb(loc, "zero", [P, MSG])
        acc = r2[:, :].rearrange("p (t m) -> p t m", m=MSG)
        in_m, dl2, dl3 = sem("in_m"), sem("dl2"), sem("dl3")
        fv_in = [sem("fv_in0"), sem("fv_in1")]
        msg_ready, oh_ready, oh_used, flushed, wcol = (
            sem("msg_ready"), sem("oh_ready"), sem("oh_used"), sem("flushed"), sem("wcol"))
        fv_rows = dram["fv"].rearrange("(t p) d -> p t d", p=P)
        iota = const[:, C_IOTA:C_IOTA + P]
        sums = bank[0][:, 0:MSG]

        with nc.Block() as block:
            @block.sync
            def _(sp):
                sp.dma_start(dst[:, :], a["dst_t"]).then_inc(in_m, 16)
                sp.dma_start(dlast[0:1, :], a["dst_last"]).then_inc(in_m, 16)

            @block.vector
            def _(dve):
                dve.wait_ge(in_m, 32)
                dve.tensor_copy(dstf[:, :], dst[:, :])
                dve.memset(zero[:, :], 0.0)
                dve.memset(msg[:, :, :], 0.0)
                dve.tensor_scalar(dlast[0:1, :], dlast[0:1, :], 7, None, ALU.arith_shift_right).then_inc(dl2, 1)

        def dtile(eng, s):
            return eng.value_load(dlast[0:1, bass.ds(s, 1)], min_val=0, max_val=NT - 1)

        with nc.Block() as block:
            @block.sync
            def _(sp):
                def rnd(i):
                    for hf in range(2):
                        if not isinstance(i, int):
                            sp.wait_ge(msg_ready, i * 2 + (hf - 1))
                        sp.dma_start(fv[:, hf * H:hf * H + H, :],
                                     fv_rows[:, bass.ds(i * U + hf * H, H), :]).then_inc(fv_in[hf], 16)
                rnd(0)
                with sp.Fori(1, ROUNDS) as i:
                    rnd(i)

            @block.scalar
            def _(act):
                with act.Fori(0, ROUNDS) as i:
                    for hf in range(2):
                        act.wait_ge(msg_ready, i * 2 + (hf + 1))
                        act.activation(msg[:, hf * H:hf * H + H, D:MSG],
                                       weights[:, bass.ds((i * U + hf * H) * HEADS, H * HEADS)].rearrange(
                                           "p (u h) -> p u h", h=HEADS), ACT.Copy).then_inc(wcol, 1)

            @block.vector
            def _(dve):
                cur, prev = dve.alloc_register("cur_s2v"), dve.alloc_register("prev_s2v")
                dve.reg_mov(cur, 0)
                dve.reg_mov(prev, 0)

                def rnd(i):
                    first = isinstance(i, int)
                    for hf in range(2):
                        s = i * 2 + hf
                        us = slice(hf * H, hf * H + H)
                        last = dtile(dve, s)
                        dve.wait_ge(fv_in[hf], i * 16 + 16)
                        if not first:
                            dve.wait_ge(oh_used, dve.snap(prev, min_val=0, max_val=NT - 1) + (s - 1))
                        wt = weights[:, bass.ds(s * H * HEADS, H * HEADS)].rearrange(
                            "p (u h) -> p u h", h=HEADS).unsqueeze(3).to_broadcast([P, H, HEADS, HC])
                        dve.tensor_tensor(msg[:, us, 0:D].rearrange("p u (h c) -> p u h c", c=HC),
                                          fv[:, us, :].rearrange("p u (h c) -> p u h c", c=HC), wt,
                                          ALU.mult).then_inc(msg_ready, 1)

                        def one_hot(d):
                            return dve.scalar_tensor_tensor(
                                oh[:, hf, :, :], iota.unsqueeze(1).to_broadcast([P, H, P]),
                                const[:, bass.ds(d + C_BASE, 1)],
                                dstf[:, bass.ds(s * H, H)].unsqueeze(2).to_broadcast([P, H, P]),
                                ALU.add, ALU.is_equal)

                        def first_pair(d):
                            one_hot(d).then_inc(oh_ready, 1)

                        def extra_pair(d):
                            dve.wait_ge(oh_used, d + s)
                            dve.tensor_copy(acc[:, bass.ds(d - 1, 1), :].rearrange("p a m -> p (a m)"),
                                            sums).then_inc(flushed, 1)
                            one_hot(d).then_inc(oh_ready, 1)
                        pair_loop(dve, cur, prev, last, first_pair, extra_pair)
                rnd(0)
                with dve.Fori(1, ROUNDS) as i:
                    rnd(i)
                dve.wait_ge(oh_used, ET // H + NT - 1)
                dve.tensor_copy(acc[:, NT - 1, :], sums).then_inc(flushed, 1)

            @block.tensor
            def _(pe):
                cur, prev = pe.alloc_register("cur_s2p"), pe.alloc_register("prev_s2p")
                pe.reg_mov(cur, 0)
                pe.matmul(sums, zero[:, 0:P], zero[:, :], start=True, stop=True)

                with pe.Fori(0, ROUNDS) as i:
                    for hf in range(2):
                        s = i * 2 + hf
                        last = dtile(pe, s)
                        pe.wait_ge(wcol, s + 1)

                        def pair(d, start):
                            pe.wait_ge(oh_ready, d + (s + 1))
                            for u in range(H):
                                ins = pe.matmul(sums, oh[:, hf, u, :], msg[:, hf * H + u, :],
                                                start=start and u == 0, stop=True, skip_group_check=True)
                            ins.then_inc(oh_used, 1)

                        def extra_pair(d):
                            pe.wait_ge(flushed, d)
                            pair(d, True)
                        pair_loop(pe, cur, prev, last, lambda d: pair(d, False), extra_pair)


def combine_phase(nc, ctx, sb, sem, dram, r2, x1):
    with ExitStack() as loc:
        acc = r2[:, :].rearrange("p (t m) -> p t m", m=MSG)
        base = sb(loc, "base_g", [P, G, D])
        hh = sb(loc, "hh", [P, G, D])
        den = sb(loc, "den", [P, G, HEADS])
        rec = sb(loc, "rec", [P, G, HEADS])
        pre = sb(loc, "pre", [P, G, D])
        sl = sb(loc, "sl", [P, G, D])
        in_b, in_h, dvc, pre_ready, sl_ready, x1_ready = (
            sem("in_b"), sem("in_h"), sem("dvc"), sem("pre_ready"), sem("sl_ready"), sem("x1_ready"))
        h_rows = dram["h"].rearrange("(t p) d -> p t d", p=P)
        base_rows = dram["base"].rearrange("(t p) d -> p t d", p=P)
        with nc.Block() as block:
            @block.sync
            def _(sp):
                def group(g):
                    if not isinstance(g, int):
                        sp.wait_ge(x1_ready, g)
                    sp.dma_start(base[:, :, :], base_rows[:, bass.ds(g * G, G), :]).then_inc(in_b, 16)
                    sp.dma_start(hh[:, :, :], h_rows[:, bass.ds(g * G, G), :]).then_inc(in_h, 16)
                group(0)
                with sp.Fori(1, NG) as g:
                    group(g)

            @block.vector
            def _(dve):
                st = Steps(dve, dvc)
                with dve.Fori(0, NG) as g:
                    st.enter(g, 2 + G, 0)
                    st.link(dve.tensor_scalar(den[:, :, :], acc[:, bass.ds(g * G, G), D:MSG], 1e-30, None, ALU.max))
                    st.link(dve.reciprocal(rec[:, :, :], den[:, :, :]))
                    for u in range(G):
                        ins = dve.tensor_tensor(
                            pre[:, u, :].rearrange("p (h c) -> p h c", c=HC),
                            acc[:, bass.ds(g * G + u, 1), 0:D].rearrange("p a (h c) -> p (a h) c", c=HC),
                            rec[:, u, :].unsqueeze(2).to_broadcast([P, HEADS, HC]), ALU.mult)
                        st.done(ins) if u < G - 1 else st.link(ins)
                    dve.wait_ge(in_h, g * 16 + 16)
                    dve.tensor_tensor(pre[:, :, :], pre[:, :, :], hh[:, :, :], ALU.add).then_inc(pre_ready, 1)
                    dve.wait_ge(sl_ready, g + 1)
                    dve.wait_ge(in_b, g * 16 + 16)
                    dve.tensor_tensor(x1[:, bass.ds(g * G, G), :], base[:, :, :], sl[:, :, :], ALU.add
                                      ).then_inc(x1_ready, 1)
                    st.leave(NG)

            @block.scalar
            def _(act):
                with act.Fori(0, NG) as g:
                    act.wait_ge(pre_ready, g + 1)
                    act.activation(sl[:, :, :], pre[:, :, :], ACT.Silu).then_inc(sl_ready, 1)


def ffn_phase(nc, ctx, sb, sem, a, out, x1, r1, r2, const, bank, ident):
    xf = r1[:, 0:NT * D].rearrange("p (t d) -> p t d", d=D)
    xft = r2[:, 0:NT * D].rearrange("p (t f q) -> p f t q", f=2, q=P)
    FC = FF // P
    with ExitStack() as loc:
        stats = sb(loc, "stats_f", [P, G, 6])
        aggr = sb(loc, "aggr_f", [P, G, 2])
        mv = sb(loc, "mv_f", [P, NT, 2])
        rs = sb(loc, "rs_f", [P, 2, NT])
        wr = sb(loc, "wr", [P, 2, EXPERTS])
        ones = sb(loc, "ones", [P, P])
        br = sb(loc, "br", [1, EXPERTS])
        w1 = sb(loc, "w1", [P, 2, 2, FF])
        w2 = sb(loc, "w2", [P, 2, FC, D])
        b1 = sb(loc, "b1", [P, 2, FC])
        b2 = sb(loc, "b2", [P, 2, D])
        b2c = sb(loc, "b2c", [P, D])
        gb = sb(loc, "gb", [P, 2, D])
        rt = sb(loc, "rt", [1, 12, 8])
        rti = sb(loc, "rti", [1, 8], U32)
        mrow = sb(loc, "mrow", [1, D])
        mcol = sb(loc, "mcol", [P, 2])
        wb = sb(loc, "wb", [P, 2])
        gt = sb(loc, "gt", [P, 2 * FC, G * P])
        xs = gt[:, 0:2, :].rearrange("p a b -> p (a b)").rearrange("p (u d) -> p u d", d=D)
        stats_done = sem("stats_done_f")
        w_in, dva, dvb, var_ready, sd = sem("w_in_f"), sem("dva"), sem("dvb"), sem("var_f"), sem("sd_f")

        def stats_pass(dve, st, src, wait):
            with dve.Fori(0, NG) as g:
                st.enter(g, 2 * G + 1, 0)
                wait(g)
                for u in range(G):
                    ins = dve.bn_stats(stats[:, u, :], src[:, bass.ds(g * G + u, 1), :].rearrange("p a d -> p (a d)"))
                    st.done(ins) if u < G - 1 else st.link(ins)
                dve.sem_inc(stats_done, 1)
                for u in range(G):
                    ins = dve.bn_aggr(aggr[:, u, :], stats[:, u, :])
                    st.done(ins) if u < G - 1 else st.link(ins)
                st.link(dve.tensor_copy(mv[:, bass.ds(g * G, G), :], aggr[:, :, :]))
                st.leave(NG)

        with nc.Block() as block:
            @block.sync
            def _(sp):
                sp.dma_start(wr[:, :, :], a["wr"]).then_inc(w_in, 16)
                sp.dma_start(br[:, :], a["br"]).then_inc(w_in, 16)
                sp.dma_start(gb[:, 0, :], a["gamma"].partition_broadcast(P)).then_inc(w_in, 16)
                sp.dma_start(gb[:, 1, :], a["beta"].partition_broadcast(P)).then_inc(w_in, 16)
                sp.wait_ge(w_in, 64)

            @block.vector
            def _(dve):
                st = Steps(dve, dva)
                dve.memset(ones[:, :], 1.0)
                stats_pass(dve, st, x1, lambda g: None)
                dve.tensor_scalar(rs[:, 0, :], mv[:, :, 1:2].rearrange("p t o -> p (t o)"), LN_EPS, None,
                                  ALU.add).then_inc(var_ready, 1)
                dve.wait_ge(sd, 1)
                st.link(dve.reciprocal(rs[:, 0, :], rs[:, 1, :]))

            @block.scalar
            def _(act):
                act.wait_ge(var_ready, 1)
                act.activation(rs[:, 1, :], rs[:, 0, :], ACT.Sqrt).then_inc(sd, 1)

        xs_ready, t_ps, t_ev, kept, sum_done = sem("xs_ready"), sem("t_ps"), sem("t_ev"), sem("kept"), sem("sum_done")
        mr, mc, lg, exs, exd, wbd, wbp = sem("mr"), sem("mc"), sem("lg"), sem("exs"), sem("exd"), sem("wbd"), sem("wbp")
        idx_ready, ex_in, w2_ready = sem("idx_ready"), sem("ex_in"), sem("w2_ready")
        col = lambda k, t: rs[:, k, bass.ds(t, 1)]
        mu = lambda t: mv[:, bass.ds(t, 1), 0:1].rearrange("p a b -> p (a b)")

        with nc.Block() as block:
            @block.vector
            def _(dve):
                def group(g):
                    if not isinstance(g, int):
                        dve.wait_ge(t_ps, g * 4)
                        dve.wait_ge(kept, g)
                        dve.wait_ge(sum_done, g)
                    for u in range(G):
                        t = g * G + u
                        dve.tensor_scalar(xs[:, u, :], x1[:, bass.ds(t, 1), :].rearrange("p a d -> p (a d)"),
                                          mu(t), col(0, t), ALU.subtract, ALU.mult).then_inc(xs_ready, 1)
                group(0)
                with dve.Fori(1, NG) as g:
                    group(g)
                st = Steps(dve, dvb)
                dve.wait_ge(sum_done, NG)
                dve.tensor_scalar(mrow[:, :], bank[6][0:1, 0:D], 1.0 / N_NODES, None, ALU.mult).then_inc(mr, 1)
                dve.wait_ge(mc, 1)
                st.link(dve.tensor_copy(mcol[:, :], bank[7][:, 0:2]))
                dve.tensor_copy(mcol[:, :], mcol[:, :]).then_inc(mr, 1)
                dve.wait_ge(mc, 2)
                r = lambda k: rt[:, k, :]
                r1c = lambda k, c: rt[:, k, c:c + 1]
                st.link(dve.tensor_tensor(r(0), bank[5][0:1, 0:EXPERTS], br[:, :], ALU.add))

                def softmax(src, n, dst, k):
                    st.link(dve.tensor_reduce(r1c(k, 0), rt[:, src, 0:n], AX.X, ALU.max))
                    dve.tensor_scalar(rt[:, dst, 0:n], rt[:, src, 0:n], r1c(k, 0), None, ALU.subtract).then_inc(exs, 1)
                    count[0] += 1
                    dve.wait_ge(exd, count[0])
                    st.link(dve.tensor_reduce(r1c(k, 1), rt[:, dst, 0:n], AX.X, ALU.add))
                    st.link(dve.reciprocal(r1c(k, 2), r1c(k, 1)))
                    st.link(dve.tensor_scalar(rt[:, dst, 0:n], rt[:, dst, 0:n], r1c(k, 2), None, ALU.mult))
                count = [0]
                softmax(0, EXPERTS, 1, 2)
                st.link(dve.tensor_scalar(r(3), r(1), float(N_NODES), 1e-30, ALU.mult, ALU.max))
                st.link(dve.reciprocal(r(3), r(3)))
                st.link(dve.tensor_scalar(r(3), r(3), CAPACITY, 1.0, ALU.mult, ALU.min))
                st.link(dve.tensor_tensor(r(4), r(3), r(1), ALU.mult))
                softmax(4, EXPERTS, 5, 6)
                st.link(dve.max(r(7), r(5)))
                dve.max_index(rti[:, :], r(7), r(5)).then_inc(idx_ready, 1)
                softmax(7, 2, 8, 9)
                dve.tensor_copy(rt[:, 10, 0:2], rt[:, 8, 0:2]).then_inc(wbp, 1)
                dve.wait_ge(wbd, 1)
                st.link(dve.tensor_copy(wb[:, :], bank[4][:, 0:2]))
                dve.wait_ge(ex_in, 8 * 16)
                for e in range(2):
                    st.link(dve.tensor_scalar(w2[:, e, :, :], w2[:, e, :, :], wb[:, e:e + 1], None, ALU.mult))
                st.link(dve.tensor_scalar(b2c[:, :], b2[:, 0, :], wb[:, 0:1], None, ALU.mult))
                st.link(dve.scalar_tensor_tensor(b2c[:, :], b2[:, 1, :], wb[:, 1:2], b2c[:, :], ALU.mult, ALU.add))

            @block.gpsimd
            def _(pool):
                with pool.Fori(0, NG) as g:
                    pool.wait_ge(xs_ready, g * G + G)
                    pool.tensor_copy(xf[:, bass.ds(g * G, G), :], xs[:, :, :]).then_inc(kept, 1)

            @block.tensor
            def _(pe):
                def group(g, start, stop):
                    first = isinstance(g, int) and start
                    for k in range(4):
                        n = min(2, G - 2 * k)
                        pe.wait_ge(xs_ready, g * G + (2 * k + n))
                        if not (first and k < 2):
                            pe.wait_ge(t_ev, g * 4 + (k - 1))
                        for u in range(n):
                            for f in range(2):
                                last = pe.transpose(bank[k % 2][:, (2 * u + f) * P:(2 * u + f + 1) * P],
                                                    xs[:, 2 * k + u, f * P:(f + 1) * P], ident)
                        last.then_inc(t_ps, 1)
                    for u in range(G):
                        one = const[:, C_REAL:C_REAL + 1] if stop and u == G - 1 else ones[:, 0:1]
                        last = pe.matmul(bank[6][0:1, 0:D], one, xs[:, u, :],
                                         start=start and u == 0, stop=stop and u == G - 1)
                    last.then_inc(sum_done, 1)
                group(0, True, False)
                with pe.Fori(1, NG - 1) as g:
                    group(g, False, False)
                group(NG - 1, False, True)
                pe.wait_ge(mr, 1)
                for f in range(2):
                    last = pe.matmul(bank[7][:, f:f + 1], mrow[0:1, f * P:(f + 1) * P], ones[0:1, 0:1],
                                     start=True, stop=True)
                last.then_inc(mc, 1)
                pe.wait_ge(mr, 2)
                for f in range(2):
                    last = pe.matmul(bank[5][0:1, 0:EXPERTS], mcol[:, f:f + 1], wr[:, f, :], start=f == 0, stop=f == 1)
                last.then_inc(mc, 1)
                pe.wait_ge(wbp, 1)
                pe.matmul(bank[4][:, 0:2], ones[0:1, :], rt[:, 10, 0:2], start=True, stop=True).then_inc(wbd, 1)

            @block.scalar
            def _(act):
                with act.Fori(0, NG) as g:
                    for k in range(4):
                        n = min(2, G - 2 * k)
                        act.wait_ge(t_ps, g * 4 + (k + 1))
                        act.activation(r2[:, bass.ds((g * G + 2 * k) * D, n * D)], bank[k % 2][:, 0:n * D],
                                       ACT.Copy).then_inc(t_ev, 1)
                for c, (dst, n) in enumerate(((1, EXPERTS), (5, EXPERTS), (8, 2))):
                    act.wait_ge(exs, c + 1)
                    act.activation(rt[:, dst, 0:n], rt[:, dst, 0:n], ACT.Exp).then_inc(exd, 1)

            @block.sync
            def _(sp):
                sp.wait_ge(idx_ready, 1)
                for e in range(2):
                    x = sp.value_load(rti[0:1, e:e + 1], min_val=0, max_val=EXPERTS - 1)
                    one = lambda v: v[bass.ds(x, 1)]
                    sp.dma_start(w1[:, e, :, :], one(a["w1"]).rearrange("a p k f -> p (a k) f")).then_inc(ex_in, 16)
                    sp.dma_start(w2[:, e, :, :], one(a["w2"]).rearrange("a p k f -> p (a k) f")).then_inc(ex_in, 16)
                    sp.dma_start(b1[:, e, :], one(a["b1"]).rearrange("a p k -> p (a k)")).then_inc(ex_in, 16)
                    sp.dma_start(b2[:, e, :], one(a["b2"]).rearrange("a d -> (a d)").partition_broadcast(P)
                                 ).then_inc(ex_in, 16)
                sp.wait_ge(ex_in, 8 * 16)

        up, act_done, y_ps, o_ready, x1b, dvf = sem("up"), sem("act_done"), sem("y_ps"), sem("o_ready"), sem("x1b"), sem("dvf")
        add_b = sem("add_b")
        Q = G * P // 2
        xft3 = r2[:, 0:NT * D].rearrange("p (t f q) -> p f t q", f=2, q=P)
        HT = 2 * FC * 4

        with nc.Block() as block:
            @block.tensor
            def _(pe):
                def group(g):
                    first = isinstance(g, int) and g == 0
                    n = 0
                    for e in range(2):
                        for c in range(FC):
                            for q in range(2):
                                t0, nt = (0, 4) if q == 0 else (4, 3)
                                if not (first and n < 4):
                                    pe.wait_ge(act_done, g * (4 * FC) + (n - 3))
                                for f in range(2):
                                    last = pe.matmul(bank[n % 4][:, 0:nt * P].rearrange("p (t q) -> p t q", q=P),
                                                     w1[:, e, f, c * P:(c + 1) * P],
                                                     xft3[:, f, bass.ds(g * G + t0, nt), :],
                                                     start=f == 0, stop=f == 1)
                                last.then_inc(up, 1)
                                n += 1
                    pe.wait_ge(act_done, g * (4 * FC) + 4 * FC)
                    for u in range(G):
                        if not (first and u < 4):
                            pe.wait_ge(o_ready, g * G + reuse(u, 4))
                        for m in range(2 * FC):
                            last = pe.matmul(bank[4 + u % 4][:, 0:D], gt[:, m, u * P:(u + 1) * P],
                                             w2[:, m // FC, m % FC, :], start=m == 0, stop=m == 2 * FC - 1)
                        last.then_inc(y_ps, 1)
                group(0)
                with pe.Fori(1, NG) as g:
                    group(g)

            @block.scalar
            def _(act):
                def group(g):
                    if not isinstance(g, int):
                        act.wait_ge(y_ps, g * G)
                    n = 0
                    for e in range(2):
                        for c in range(FC):
                            for q in range(2):
                                t0, nt = (0, 4) if q == 0 else (4, 3)
                                act.wait_ge(up, g * (4 * FC) + (n + 1))
                                act.activation(gt[:, e * FC + c, t0 * P:(t0 + nt) * P], bank[n % 4][:, 0:nt * P],
                                               ACT.Gelu, bias=b1[:, e, c:c + 1]).then_inc(act_done, 1)
                                n += 1
                group(0)
                with act.Fori(1, NG) as g:
                    group(g)

            @block.gpsimd
            def _(pool):
                with pool.Fori(0, NT) as t:
                    v = x1[:, bass.ds(t, 1), :].rearrange("p a d -> p (a d)")
                    pool.tensor_tensor(v, v, gb[:, 1, :], ALU.add).then_inc(x1b, 1)

            @block.vector
            def _(dve):
                with dve.Fori(0, NG) as g:
                    for u in range(G):
                        v = xf[:, bass.ds(g * G + u, 1), :].rearrange("p a d -> p (a d)")
                        dve.tensor_tensor(v, v, b2c[:, :], ALU.add).then_inc(add_b, 1)
                    for u in range(G):
                        v = xf[:, bass.ds(g * G + u, 1), :].rearrange("p a d -> p (a d)")
                        dve.wait_ge(add_b, g * G + (u + 1))
                        dve.wait_ge(y_ps, g * G + (u + 1))
                        dve.tensor_tensor(v, bank[4 + u % 4][:, 0:D], v, ALU.add).then_inc(o_ready, 1)
                st = Steps(dve, dvf)
                stats_pass(dve, st, xf, lambda g: dve.wait_ge(o_ready, NT))
                dve.tensor_scalar(rs[:, 0, :], mv[:, :, 1:2].rearrange("p t o -> p (t o)"), LN_EPS, None,
                                  ALU.add).then_inc(var_ready, 1)

        o1, out_ready, stored = sem("o1"), sem("out_ready"), sem("stored")
        o_rows = out.rearrange("(t p) d -> p t d", p=P)
        with nc.Block() as block:
            @block.scalar
            def _(act):
                act.activation(rs[:, 1, :], rs[:, 0, :], ACT.Sqrt).then_inc(sd, 1)

            @block.vector
            def _(dve):
                dve.wait_ge(sd, 2)
                dve.reciprocal(rs[:, 0, :], rs[:, 1, :]).then_inc(o1, 1)
                dve.wait_ge(o1, 1)

                def group(g):
                    if not isinstance(g, int):
                        dve.wait_ge(stored, g * 16)
                    for u in range(G):
                        t = g * G + u
                        dve.scalar_tensor_tensor(xs[:, u, :], xf[:, bass.ds(t, 1), :].rearrange("p a d -> p (a d)"),
                                                 mu(t), gb[:, 0, :], ALU.subtract, ALU.mult).then_inc(o1, 1)
                    for u in range(G):
                        t = g * G + u
                        dve.wait_ge(o1, g * G + (u + 2))
                        dve.scalar_tensor_tensor(xs[:, u, :], xs[:, u, :], col(0, t),
                                                 x1[:, bass.ds(t, 1), :].rearrange("p a d -> p (a d)"),
                                                 ALU.mult, ALU.add).then_inc(out_ready, 1)
                group(0)
                with dve.Fori(1, NG) as g:
                    group(g)

            @block.sync
            def _(sp):
                with sp.Fori(0, NG) as g:
                    sp.wait_ge(out_ready, g * G + G)
                    sp.dma_start(o_rows[:, bass.ds(g * G, G), :], xs[:, :, :]).then_inc(stored, 16)
                sp.wait_ge(stored, NG * 16)


DEBUG = False


def kernel(x, src, dst, L0_gnn_Wsrc, L0_gnn_bsrc, L0_gnn_Wdst, L0_gnn_bdst, L0_gnn_Wval, L0_gnn_bval, L0_gnn_attn,
           L0_mix_kln_weight, L0_mix_kln_bias, L0_mix_vln_weight, L0_mix_vln_bias, L0_ffn_Wr, L0_ffn_br, L0_ffn_W1,
           L0_ffn_b1, L0_ffn_W2, L0_ffn_b2, L0_ffn_gamma, L0_ffn_beta):
    import numpy as np
    import concourse.bacc as bacc
    from concourse.bass_utils import run_bass_kernel_spmd as run

    A = lambda v: np.ascontiguousarray(np.asarray(v))
    halves = lambda m: m.reshape(2, P, -1).transpose(1, 0, 2)
    pad_edges = np.full(EP - N_EDGES, PAD_NODE, np.int32)
    dst_p = np.concatenate([A(dst), pad_edges])
    src_p = np.concatenate([A(src), np.zeros(EP - N_EDGES, np.int32)])
    around = np.concatenate([np.int32([-1]), dst_p, np.int32([NP])])
    iota = np.arange(P, dtype=np.float32)
    const = np.zeros((P, C_END), np.float32)
    const[:, C_IDENT:C_IDENT + P] = np.eye(P)
    const[:, C_BLOCK:C_BLOCK + P] = np.kron(np.eye(P // HC), np.ones((HC, HC)))
    const[:, C_IOTA:C_IOTA + P] = iota
    const[:, C_BASE:C_BASE + NT] = P * np.arange(NT)
    const[:, C_NODE:C_NODE + NT] = P * np.arange(NT) + iota[:, None]
    const[:, C_REAL] = P * (NT - 1) + iota < N_NODES
    flat = lambda v: A(v).reshape(-1)
    cols = lambda v: flat(v).reshape(2, P).T
    arrays = {
        "x": np.concatenate([A(x), np.zeros((NP - N_NODES, D), np.float32)]),
        "src_t": src_p.reshape(ET, P).T,
        "dst_t": dst_p.reshape(ET, P).T,
        "dst_last": dst_p.reshape(ET // H, H * P)[:, -1][None, :],
        "dst_line": dst_p,
        "dst_chunks": np.stack([around[j * CE:(j + 1) * CE + 2] for j in range(CHUNKS)]),
        "wcat": halves(np.concatenate([A(L0_gnn_Wsrc).T, A(L0_gnn_Wval).T, A(L0_gnn_Wdst).T], axis=1)),
        "proj_bias": np.concatenate([A(L0_gnn_bsrc), A(L0_gnn_bval), A(L0_gnn_bdst)]),
        "attn": flat(L0_gnn_attn),
        "mix_rows": np.concatenate([flat(L0_mix_kln_weight), flat(L0_mix_kln_bias),
                                    flat(L0_mix_vln_weight), flat(L0_mix_vln_bias)]),
        "mix_cols": np.concatenate([cols(L0_mix_kln_weight), cols(L0_mix_kln_bias)], axis=1),
        "const": const,
        "wr": halves(A(L0_ffn_Wr)),
        "br": A(L0_ffn_br)[None, :],
        "w1": A(L0_ffn_W1).reshape(EXPERTS, 2, P, FF).transpose(0, 2, 1, 3),
        "w2": A(L0_ffn_W2).reshape(EXPERTS, FF // P, P, D).transpose(0, 2, 1, 3),
        "b1": A(L0_ffn_b1).reshape(EXPERTS, FF // P, P).transpose(0, 2, 1),
        "b2": A(L0_ffn_b2),
        "gamma": A(L0_ffn_gamma),
        "beta": A(L0_ffn_beta),
    }
    nc = bacc.Bacc("TRN2", target_bir_lowering=False, num_devices=1)
    args = {}
    for name, v in arrays.items():
        arrays[name] = np.ascontiguousarray(v)
        args[name] = nc.dram_tensor(f"in_{name}", v.shape, mybir.dt.from_np(v.dtype), kind="ExternalInput").ap()
    out = nc.dram_tensor("out", (NP, D), FP32, kind="ExternalOutput").ap()
    kind = "ExternalOutput" if DEBUG else "Internal"
    dram = {name: nc.dram_tensor(f"s_{name}", shape, dt, kind=kind).ap() for name, shape, dt in (
        ("tab", (NP, 2 * D), FP32), ("h", (NP, D), FP32), ("base", (NP, D), FP32), ("fv", (EP, D), FP32),
        ("d16", (EP,), I16))}
    gps_layer(nc, args, out, dram)
    r = run(nc, [{f"in_{name}": v for name, v in arrays.items()}], core_ids=[0])
    if DEBUG:
        return tuple(r.results[0][f"s_{n}"][:N_NODES] for n in ("tab", "h", "base")) + (r.results[0]["out"][:N_NODES],)
    return r.results[0]["out"][:N_NODES]
```

```python
import concourse.bass as bass
from concourse import mybir
from concourse.alu_op_type import AluOpType as ALU
from contextlib import ExitStack

FP32 = mybir.dt.float32
I32 = mybir.dt.int32
U32 = mybir.dt.uint32
I16 = mybir.dt.int16
ACT = mybir.ActivationFunctionType
AX = mybir.AxisListType

N_NODES, N_EDGES, D, HEADS, EXPERTS, FF = 6250, 100000, 256, 8, 8, 512
P = 128
HC = D // HEADS
NT = -(-N_NODES // P)
NP = NT * P
G = 7
NG = NT // G
CHUNKS = P // HEADS
BLOCKS = -(-N_EDGES // (CHUNKS * P))
ET = CHUNKS * BLOCKS
EP = ET * P
CE = BLOCKS * P
U = 16
H = 4
Q = U // H
K = U // 2
ROUNDS = ET // U
MSG = D + HEADS
PAD_NODE = NP - 1
FAR = 1e37
LN_EPS, MIX_EPS = 1e-5, 1e-5
TABLES = ("src_t", "dst_t", "dst_last", "dst_line", "dst_chunks")
CAPACITY = float(-(-int(N_NODES * 1.25) // EXPERTS)) if (N_NODES * 1.25) % 1 == 0 else float(
    -(-int(N_NODES * 1.25 + 1) // EXPERTS))
assert NT == G * NG and ET == U * ROUNDS

C_IDENT, C_BLOCK, C_IOTA = 0, P, 2 * P
C_BASE = 3 * P
C_NODE = C_BASE + NT
C_REAL = C_NODE + NT
C_ONE = C_REAL + 1
C_END = C_ONE + 1
LINES = 112
LW = EP // LINES


def reuse(u, ring, n=G):
    return u - ring + 1 if u >= ring else max(w for w in range(n) if w % ring == u) + 1 - n


class Steps:

    def __init__(self, eng, sem):
        self.eng, self.sem, self.base, self.k, self.i, self.n = eng, sem, 0, 0, None, 0

    def done(self, ins):
        ins.then_inc(self.sem, 1)
        self.k += 1

    def value(self):
        return self.base + self.k if self.i is None else self.i * self.n + (self.base + self.k)

    def link(self, ins):
        self.done(ins)
        self.eng.wait_ge(self.sem, self.value())

    def enter(self, i, n, first):
        self.base, self.k, self.i, self.n = self.base + self.k - first * n, 0, i, n

    def leave(self, last):
        assert self.k == self.n, (self.k, self.n)
        self.base, self.k, self.i = self.base + last * self.n, 0, None


def gps_layer(nc, a, out, dram):
    ctx = ExitStack()
    with ctx:
        def sb(stack, name, shape, dt=FP32):
            return stack.enter_context(nc.sbuf_tensor(name, shape, dt))

        def sem(name):
            return ctx.enter_context(nc.semaphore(name))

        r1 = sb(ctx, "r1", [P, NT * D + 2])
        r2 = sb(ctx, "r2", [P, NT * MSG])
        r3 = sb(ctx, "r3", [P, NT * D])
        const = sb(ctx, "const", [P, C_END])
        rows = sb(ctx, "rows", [P, 3 * D])
        bank01 = ctx.enter_context(nc.psum_tensor("bank01", [P, 2, 512], FP32))
        bank = [bank01[:, 0, :], bank01[:, 1, :]] + [
            ctx.enter_context(nc.psum_tensor(f"bank{i}", [P, 512], FP32)) for i in range(2, 8)]
        ident = const[:, C_IDENT:C_IDENT + P]
        tiles = lambda r: r[:, 0:NT * D].rearrange("p (t d) -> p t d", d=D)
        X, XT_ALL, FDST = tiles(r1), tiles(r2), tiles(r3)

        unsorted = sb(ctx, "unsorted", [1, 1], I32)
        node_phase(nc, ctx, sb, sem, a, dram, X, XT_ALL, FDST, r2, unsorted, const, rows, bank, ident)
        sort_phase(nc, ctx, sb, sem, a, dram, r1, r2, unsorted, const)
        scores = r1[:, 0:ET * HEADS]
        weights = r1[:, ET * HEADS:2 * ET * HEADS]
        score_phase(nc, ctx, sb, sem, a, dram, FDST, scores, r2, const, rows, bank, ident)
        softmax_phase(nc, ctx, sb, sem, dram, r2, r3, scores, r1, bank, ident, weights)
        message_phase(nc, ctx, sb, sem, a, dram, weights, r2, r3, const, bank01)
        ffn_phase(nc, ctx, sb, sem, a, dram, out, tiles(r3), r1, r2, const, bank, ident)


def node_phase(nc, ctx, sb, sem, a, dram, X, XT_ALL, FDST, r2, unsorted, const, rows, bank, ident):
    with ExitStack() as loc:
        PJ = 4
        uses = lambda s: len(range(s, G, PJ))
        wcat = sb(loc, "wcat", [P, 2, 3 * D])
        stats = sb(loc, "stats", [P, G, 6])
        aggr = sb(loc, "aggr", [P, G, 2])
        mv = sb(loc, "mv", [P, NT, 2])
        rs = sb(loc, "rs", [P, 4, NT])
        xn = sb(loc, "xn", [P, G, D])
        xt = sb(loc, "xt", [P, G, D])
        dz = sb(loc, "dz", [P, G, D])
        z = sb(loc, "z", [P, G, 2, P + 1])
        small = sb(loc, "small", [P, 3, G * HEADS])
        pj = sb(loc, "pj", [P, PJ, 2 * D])
        hst = sb(loc, "hst", [P, G, D])
        sq = lambda g: FDST[:, bass.ds(g * G, G), :]
        kvw = hst[:, 0:4, :].rearrange("p a d -> p (a d)")
        kvc, cols = hst[:, 4, 0:4], hst[:, 4, 8:16]
        kv = dz[:, 0, :].rearrange("p (f q) -> p f q", f=2)
        tmp = dz[:, 1, :].rearrange("p (f q) -> p f q", f=2)
        x_loaded, stats_done = sem("x_loaded"), sem("stats_done")
        x_in, w_in, ones_set = [sem("x_in0"), sem("x_in1")], sem("w_in"), sem("ones_set")
        dve_a, dve_b = sem("dve_a"), sem("dve_b")
        rstd_sq = sem("rstd_sq")
        var_ready = sem("var_ready")
        xn_ready, xt_in_psum, xt_ready, xt_kept = sem("xn_ready"), sem("xt_in_psum"), sem("xt_ready"), sem("xt_kept")
        dz_ready, sq_ready, ss_ready, sd_ready, z_ready = (
            sem("dz_ready"), sem("sq_ready"), sem("ss_ready"), sem("sd_ready"), sem("z_ready"))
        pj_in_psum, pj_ready, pj_stored = sem("pj_in_psum"), sem("pj_ready"), [sem(f"pj_stored{s}") for s in range(PJ)]
        gram_done, proj_done, h_ready, h_stored = sem("gram_done"), sem("proj_done"), sem("h_ready"), sem("h_stored")
        x_rows = a["x"].rearrange("(t p) d -> p t d", p=P)
        tab_rows = dram["tab"].rearrange("(t p) d -> p t d", p=P)
        h_rows = dram["h"].rearrange("(t p) d -> p t d", p=P)
        base_rows = dram["base"].rearrange("(t p) d -> p t d", p=P)
        scol = sem("scol")
        mu = lambda t: mv[:, bass.ds(t, 1), 0:1].rearrange("p a b -> p (a b)")
        col = lambda k, t: rs[:, k, bass.ds(t, 1)]
        DVE_A0 = 2 * G + 1

        line = r2[0:LINES, 0:LW + 2].bitcast(I32)
        falls, most = r2[0:LINES, LW + 2:2 * LW + 3], r2[0:LINES, 2 * LW + 3:2 * LW + 4]
        line_in, fall, fall_sum, tables_out = sem("line_in"), sem("fall"), sem("fall_sum"), sem("tables_out")

        with nc.Block() as block:
            @block.sync
            def _(sp):
                sp.dma_start(line[:, :], a["dst_line"]).then_inc(line_in, 16)
                sp.dma_start(wcat[:, :, :], a["wcat"]).then_inc(w_in, 16)
                sp.dma_start(const[:, :], a["const"]).then_inc(w_in, 16)
                sp.dma_start(rows[:, :], a["proj_bias"].partition_broadcast(P)).then_inc(w_in, 16)

                def load(g, k):
                    sp.dma_start(X[:, bass.ds(g * G, G), :], x_rows[:, bass.ds(g * G, G), :]).then_inc(x_in[k], 16)
                load(0, 0)
                load(1, 1)
                with sp.Fori(1, NG // 2) as j:
                    for k in range(2):
                        sp.wait_ge(x_in[k], j * 16)
                        sp.sem_inc(x_loaded, 1)
                        load(j * 2 + k, k)
                sp.wait_ge(x_in[0], NG // 2 * 16)
                load(NG - 1, 0)
                for name in TABLES:
                    sp.dma_start(dram["t_" + name], a[name]).then_inc(tables_out, 16)
                sp.wait_ge(tables_out, 16 * len(TABLES))

            @block.gpsimd
            def _(pool):
                pool.memset(z[:, :, :, P:P + 1], 1.0).then_inc(ones_set, 1)

            @block.vector
            def _(dve):
                dve.wait_ge(line_in, 16)
                dve.tensor_tensor(falls, line[:, 0:LW + 1], line[:, 1:LW + 2], ALU.is_gt).then_inc(fall, 1)
                dve.wait_ge(fall, 1)
                dve.tensor_reduce(most, falls, AX.X, ALU.max).then_inc(fall, 1)
                st = Steps(dve, dve_a)

                def stats_of(g, j, k):
                    st.enter(g, DVE_A0, 0)
                    dve.wait_ge(x_in[k], j * 16 + 16)
                    dve.sem_inc(stats_done, 1)
                    for u in range(G - 1):
                        st.done(dve.bn_stats(stats[:, u, :], X[:, bass.ds(g * G + u, 1), :].rearrange("p a d -> p (a d)")))
                    st.link(dve.bn_stats(stats[:, G - 1, :], X[:, bass.ds(g * G + G - 1, 1), :].rearrange("p a d -> p (a d)")))
                    dve.sem_inc(stats_done, 1)
                    for u in range(G - 1):
                        st.done(dve.bn_aggr(aggr[:, u, :], stats[:, u, :]))
                    st.link(dve.bn_aggr(aggr[:, G - 1, :], stats[:, G - 1, :]))
                    st.link(dve.tensor_copy(mv[:, bass.ds(g * G, G), :], aggr[:, :, :]))
                    st.leave(0)
                    st.base = 0
                with dve.Fori(0, NG // 2) as j:
                    for k in range(2):
                        stats_of(j * 2 + k, j, k)
                stats_of(NG - 1, NG // 2, 0)
                st.base = NG * DVE_A0
                var = mv[:, :, 1:2].rearrange("p t o -> p (t o)")
                dve.tensor_scalar(rs[:, 0, :], var, LN_EPS, None, ALU.add).then_inc(var_ready, 1)
                dve.wait_ge(rstd_sq, 1)
                st.link(dve.reciprocal(rs[:, 0, :], rs[:, 2, :]))
                st.link(dve.tensor_tensor(rs[:, 3, :], var, rs[:, 0, :], ALU.mult))
                st.link(dve.tensor_tensor(rs[:, 3, :], rs[:, 3, :], rs[:, 0, :], ALU.mult))
                dve.tensor_scalar(rs[:, 3, :], rs[:, 3, :], LN_EPS, None, ALU.add).then_inc(var_ready, 1)
                dve.wait_ge(rstd_sq, 2)
                st.link(dve.reciprocal(rs[:, 1, :], rs[:, 2, :]))
                dve.wait_ge(fall_sum, 1)
                dve.tensor_copy(unsorted[:, :], bank[0][0:1, 0:1]).then_inc(fall, 1)

            @block.tensor
            def _(pe):
                pe.wait_ge(fall, 2)
                pe.wait_ge(w_in, 48)
                pe.matmul(bank[0][0:1, 0:1], most, const[0:LINES, C_ONE:C_ONE + 1], start=True, stop=True
                          ).then_inc(fall_sum, 1)

            @block.scalar
            def _(act):
                act.wait_ge(var_ready, 1)
                act.activation(rs[:, 2, :], rs[:, 0, :], ACT.Sqrt).then_inc(rstd_sq, 1)
                act.wait_ge(var_ready, 2)
                act.activation(rs[:, 2, :], rs[:, 3, :], ACT.Sqrt).then_inc(rstd_sq, 1)

        heads = lambda r: r[:, :, :].rearrange("p t (h c) -> p (t h) c", c=HC)
        bc = lambda c: c.unsqueeze(2).to_broadcast([P, G * HEADS, HC])
        N_DVE_B = 6

        with nc.Block() as block:
            @block.vector
            def _(dve):
                st = Steps(dve, dve_b)

                def evac(g, us):
                    for u in us:
                        dve.wait_ge(pj_in_psum, g * G + (u + 1))
                        s = u % PJ
                        if not (isinstance(g, int) and g == 0 and u < PJ):
                            dve.wait_ge(pj_stored[s], g * (16 * uses(s)) + 16 * (u // PJ))
                        b = (bank[2], bank[3]) if u % 2 == 0 else (bank[4], bank[5])
                        dve.scalar_tensor_tensor(pj[:, s, :], b[0][:, :], col(1, g * G + u), rows[:, 0:2 * D],
                                                 ALU.mult, ALU.add).then_inc(pj_ready, 1)
                        dve.scalar_tensor_tensor(FDST[:, bass.ds(g * G + u, 1), :].rearrange("p a d -> p (a d)"),
                                                 b[1][:, 0:D], col(1, g * G + u), rows[:, 2 * D:3 * D],
                                                 ALU.mult, ALU.add).then_inc(proj_done, 1)

                def group(g, before):
                    first = isinstance(g, int) and g == 0
                    if not first:
                        dve.wait_ge(xt_in_psum, g * 4)
                        dve.wait_ge(h_ready, g)
                    for u in range(G):
                        t = g * G + u
                        dve.tensor_scalar(xn[:, u, :], X[:, bass.ds(t, 1), :].rearrange("p a d -> p (a d)"),
                                          mu(t), col(0, t), ALU.subtract, ALU.mult).then_inc(xn_ready, 1)
                    before(range(0, 3))
                    dve.wait_ge(xn_ready, g * G + G)
                    st.link(dve.tensor_reduce(small[:, 0, :], heads(xn), AX.X, ALU.add))
                    before(range(3, 4))
                    if not first:
                        dve.wait_ge(z_ready, g)
                    dve.scalar_tensor_tensor(heads(dz), bc(small[:, 0, :]), -1.0 / HC, heads(xn),
                                             ALU.mult, ALU.add).then_inc(dz_ready, 1)
                    before(range(4, 6))
                    dve.wait_ge(sq_ready, g + 1)
                    dve.tensor_reduce(small[:, 1, :], sq(g).rearrange("p t (h c) -> p (t h) c", c=HC), AX.X, ALU.add
                                      ).then_inc(ss_ready, 1)
                    before(range(6, 7))
                    dve.wait_ge(sd_ready, g + 1)
                    st.link(dve.tensor_scalar(small[:, 2, :], small[:, 2, :], MIX_EPS, None, ALU.add))
                    st.link(dve.reciprocal(small[:, 1, :], small[:, 2, :]))
                    if not first:
                        dve.wait_ge(gram_done, g)
                    dve.wait_ge(dz_ready, g + 1)
                    zz = z[:, :, :, 0:P].rearrange("p t f (h c) -> p (t f) h c", c=HC)
                    zi = dz[:, :, :].rearrange("p t (f h c) -> p (t f) h c", f=2, c=HC)
                    zr = small[:, 1, :].rearrange("p (t h) -> p t h", h=4).unsqueeze(3).to_broadcast(
                        [P, 2 * G, 4, HC])
                    dve.tensor_tensor(zz, zi, zr, ALU.mult).then_inc(z_ready, 1)

                st.enter(None, 3, 0)
                group(0, lambda us: None)
                group(1, lambda us: evac(0, us))
                with dve.Fori(2, NG) as g:
                    st.enter(g, 3, 2)
                    group(g, lambda us: evac(g - 1, us))
                    st.leave(NG)
                for u in range(G):
                    evac(NG - 1, [u])

            @block.scalar
            def _(act):
                def group(g):
                    first = isinstance(g, int) and g == 0
                    def evac():
                        for k in range(4):
                            n = min(2, G - 2 * k)
                            act.wait_ge(xt_in_psum, g * 4 + (k + 1))
                            act.activation(xt[:, 2 * k:2 * k + n, :].rearrange("p t d -> p (t d)"),
                                           bank[k % 2][:, 0:n * D], ACT.Copy).then_inc(xt_ready, 1)
                    if first:
                        evac()
                    act.wait_ge(dz_ready, g + 1)
                    act.activation(sq(g), dz[:, :, :], ACT.Square).then_inc(sq_ready, 1)
                    act.wait_ge(ss_ready, g + 1)
                    act.activation(small[:, 2, :], small[:, 1, :], ACT.Sqrt, scale=1.0 / (HC - 1)).then_inc(sd_ready, 1)
                    if not first:
                        act.wait_ge(pj_in_psum, g * G)
                        act.wait_ge(xt_kept, g)
                        evac()
                group(0)
                with act.Fori(1, NG) as g:
                    group(g)

            @block.gpsimd
            def _(pool):
                def group(g):
                    pool.wait_ge(xn_ready, g * G + G)
                    if not isinstance(g, int):
                        pool.wait_ge(h_stored, g * 16)
                    pool.tensor_tensor(hst[:, :, :], xn[:, :, :],
                                       rs[:, 1, bass.ds(g * G, G)].unsqueeze(2).to_broadcast([P, G, D]), ALU.mult
                                       ).then_inc(h_ready, 1)
                    pool.wait_ge(xt_ready, g * 4 + 4)
                    pool.tensor_copy(XT_ALL[:, bass.ds(g * G, G), :], xt[:, :, :]).then_inc(xt_kept, 1)
                group(0)
                with pool.Fori(1, NG) as g:
                    group(g)

            @block.tensor
            def _(pe):
                def gram(g, start=False, stop=False):
                    pe.wait_ge(z_ready, g + 1)
                    for u in range(G):
                        for f in range(2):
                            last = pe.matmul(bank[6 + f][:, 0:P + 1], z[:, u, f, 0:P], z[:, u, f, :],
                                             start=start and u == 0, stop=stop and u == G - 1)
                    last.then_inc(gram_done, 1)

                def group(g, before):
                    first = isinstance(g, int) and g == 0
                    for k in range(4):
                        n = min(2, G - 2 * k)
                        pe.wait_ge(xn_ready, g * G + (2 * k + n))
                        if not (first and k < 2):
                            pe.wait_ge(xt_ready, g * 4 + (k - 1))
                        for u in range(n):
                            for f in range(2):
                                last = pe.transpose(bank[k % 2][:, (2 * u + f) * P:(2 * u + f + 1) * P],
                                                    xn[:, 2 * k + u, f * P:(f + 1) * P], ident)
                        last.then_inc(xt_in_psum, 1)
                    before()
                    for u in range(G):
                        if u % 2 == 0:
                            pe.wait_ge(xt_ready, g * 4 + (u // 2 + 1))
                        if not (first and u < 2):
                            pe.wait_ge(proj_done, g * G + reuse(u, 2))
                        b = (bank[2], bank[3]) if u % 2 == 0 else (bank[4], bank[5])
                        for f in range(2):
                            w = xt[:, u, f * P:(f + 1) * P]
                            pe.matmul(b[0][:, :], w, wcat[:, f, 0:2 * D], start=f == 0, stop=f == 1)
                            last = pe.matmul(b[1][:, 0:D], w, wcat[:, f, 2 * D:3 * D], start=f == 0, stop=f == 1)
                        last.then_inc(pj_in_psum, 1)

                group(0, lambda: None)
                gram(0, start=True)
                with pe.Fori(1, NG - 1) as g:
                    group(g, lambda: None)
                    gram(g)
                group(NG - 1, lambda: None)
                gram(NG - 1, stop=True)

            @block.sync
            def _(sp):
                def store(g):
                    sp.wait_ge(h_ready, g + 1)
                    sp.dma_start(h_rows[:, bass.ds(g * G, G), :], hst[:, :, :]).then_inc(h_stored, 16)
                    for u in range(G):
                        s = u % PJ
                        sp.wait_ge(pj_ready, g * G + (u + 1))
                        sp.dma_start(tab_rows[:, bass.ds(g * G + u, 1), :].rearrange("p a d -> p (a d)"),
                                     pj[:, s, :]).then_inc(pj_stored[s], 16)
                with sp.Fori(0, NG) as g:
                    store(g)
                sp.wait_ge(h_stored, NG * 16)
                for s in range(PJ):
                    sp.wait_ge(pj_stored[s], NG * 16 * uses(s))

        dve_k, kv_ready, row_in_psum, kvin = sem("dve_k"), sem("kv_ready"), sem("row_in_psum"), sem("kvin")
        xt_again, mix_in_psum, base_ready, base_stored = (
            sem("xt_again"), sem("mix_in_psum"), sem("base_ready"), sem("base_stored"))
        xts = (xt[:, :, :], z[:, :, :, :].rearrange("p t f q -> p (t f q)")[:, 0:G * D].rearrange("p (t d) -> p t d", d=D))
        assert NG % 2 == 1

        with nc.Block() as block:
            @block.sync
            def _(sp):
                sp.dma_start(kvw[:, :], a["mix_rows"].partition_broadcast(P)).then_inc(kvin, 16)
                sp.dma_start(kvc[:, :], a["mix_cols"]).then_inc(kvin, 16)
                with sp.Fori(0, NG) as g:
                    sp.wait_ge(base_ready, g * G + G)
                    sp.dma_start(base_rows[:, bass.ds(g * G, G), :], X[:, bass.ds(g * G, G), :]
                                 ).then_inc(base_stored, 16)
                sp.wait_ge(base_stored, NG * 16)

            @block.vector
            def _(dve):
                st = Steps(dve, dve_k)
                dve.wait_ge(kvin, 32)
                for f in range(2):
                    st.link(dve.tensor_copy(cols[:, f:f + 1], bank[6 + f][:, P:P + 1]))
                    dve.tensor_copy(tmp[:, f, :], cols[:, f:f + 1].to_broadcast([P, P])).then_inc(scol, 1)
                for f in range(2):
                    wk, bk = kvc[:, f:f + 1], kvc[:, 2 + f:3 + f]
                    wv = kvw[:, 2 * D + f * P:2 * D + (f + 1) * P]
                    bv = kvw[:, 3 * D + f * P:3 * D + (f + 1) * P]
                    o = kv[:, f, :]
                    dve.wait_ge(row_in_psum, f + 1)
                    st.link(dve.tensor_scalar(o, bank[6 + f][:, 0:P], wk, None, ALU.mult))
                    st.link(dve.scalar_tensor_tensor(o, bank[f][:, 0:P], bk, o, ALU.mult, ALU.add))
                    st.link(dve.tensor_tensor(o, o, wv, ALU.mult))
                    st.link(dve.tensor_tensor(cols[:, 2:3], cols[:, f:f + 1], wk, ALU.mult))
                    st.link(dve.scalar_tensor_tensor(cols[:, 3:4], bk, float(N_NODES), cols[:, 2:3], ALU.mult, ALU.add))
                    st.link(dve.scalar_tensor_tensor(o, bv, cols[:, 3:4], o, ALU.mult, ALU.add))
                    st.link(dve.scalar_tensor_tensor(o, o, 1.0 / N_NODES, const[:, C_BLOCK:C_BLOCK + P],
                                                     ALU.mult, ALU.mult))
                    dve.tensor_tensor(o, o, ident, ALU.add).then_inc(kv_ready, 1)

                with dve.Fori(0, NG) as g:
                    for u in range(G):
                        dve.wait_ge(mix_in_psum, g * G + (u + 1))
                        x = X[:, bass.ds(g * G + u, 1), :].rearrange("p a d -> p (a d)")
                        dve.tensor_tensor(x, bank[2 + u % 4][:, 0:D], x, ALU.add).then_inc(base_ready, 1)

            @block.scalar
            def _(act):
                def put(g, k):
                    act.activation(xts[k], XT_ALL[:, bass.ds(g * G, G), :], ACT.Copy).then_inc(xt_again, 1)
                put(0, 0)
                put(1, 1)
                with act.Fori(1, NG // 2) as j:
                    act.wait_ge(mix_in_psum, j * (2 * G) - G)
                    put(j * 2, 0)
                    act.wait_ge(mix_in_psum, j * (2 * G))
                    put(j * 2 + 1, 1)
                act.wait_ge(mix_in_psum, (NG - 2) * G)
                put(NG - 1, 0)

            @block.tensor
            def _(pe):
                for f in range(2):
                    pe.wait_ge(scol, f + 1)
                    pe.matmul(bank[f][:, 0:P], tmp[:, f, :], ident, start=True, stop=True).then_inc(row_in_psum, 1)
                pe.wait_ge(kv_ready, 2)

                def group(g, k, first=False):
                    pe.wait_ge(xt_again, g + 1)
                    for u in range(G):
                        if not (first and u < 4):
                            pe.wait_ge(base_ready, g * G + reuse(u, 4))
                        for f in range(2):
                            last = pe.matmul(bank[2 + u % 4][:, f * P:(f + 1) * P], xts[k][:, u, f * P:(f + 1) * P],
                                             kv[:, f, :], start=True, stop=True)
                        last.then_inc(mix_in_psum, 1)
                group(0, 0, True)
                with pe.Fori(0, NG // 2) as j:
                    group(j * 2 + 1, 1)
                    group(j * 2 + 2, 0)


def pair_loop(eng, cur, prev, last, first_pair, extra_pair, second_pair=None):
    d0 = eng.snap(cur, min_val=0, max_val=NT - 1)
    first_pair(d0)
    with eng.If(last > d0):
        if second_pair:
            second_pair(d0 + 1)
            with eng.If(last > d0 + 1):
                with eng.Fori(d0 + 2, last + 1) as d:
                    extra_pair(d)
                eng.nop()
        else:
            with eng.Fori(d0 + 1, last + 1) as d:
                extra_pair(d)
        eng.nop()
    eng.nop()
    if prev is not None:
        eng.reg_mov(prev, cur)
    eng.reg_mov(cur, last)


def sort_phase(nc, ctx, sb, sem, a, dram, r1, r2, unsorted, const):
    with ExitStack() as loc:
        dst = sb(loc, "so_dst", [P, ET], I32)
        src = sb(loc, "so_src", [P, ET], I32)
        dstf = sb(loc, "so_dstf", [P, ET])
        own = sb(loc, "so_own", [P, ET])
        part = sb(loc, "so_part", [P, ET])
        rank = sb(loc, "so_rank", [P, ET])
        edge = sb(loc, "so_edge", [P, 2], I32)
        place = sb(loc, "so_place", [P, 1], I32)
        chunk, key = r2[:, 0:CE].bitcast(I32), r2[:, CE:2 * CE]
        work, number = r1[:, 0:CE], r1[:, CE:2 * CE]
        cols_in, chunk_in, key_set, prepared = sem("so_in"), sem("so_chunk"), sem("so_key"), sem("so_prepared")
        s1, s2, s3, s4 = sem("so_s1"), sem("so_s2"), sem("so_s3"), sem("so_s4")
        own_set, rank_set, carry = sem("so_own_set"), sem("so_rank_set"), sem("so_carry")
        assert BLOCKS <= NT

        with nc.Block() as block:
            @block.sync
            def _(sp):
                with sp.If(sp.value_load(unsorted[0:1, 0:1], min_val=0, max_val=LINES) > 0):
                    sp.dma_start(dst[:, :], a["dst_t"]).then_inc(cols_in, 16)
                    sp.dma_start(src[:, :], a["src_t"]).then_inc(cols_in, 16)
                    sp.dma_start(number, a["count_row"].partition_broadcast(P)).then_inc(cols_in, 16)

                    def load(c):
                        sp.dma_start(chunk, a["dst_chunks"][bass.ds(c, 1), 1:1 + CE].rearrange("a e -> (a e)"
                                     ).partition_broadcast(P)).then_inc(chunk_in, 16)
                    load(0)
                    with sp.Fori(1, CHUNKS) as c:
                        sp.wait_ge(key_set, c)
                        sp.sem_inc(carry, 1)
                        load(c)

            @block.vector
            def _(dve):
                with dve.If(dve.value_load(unsorted[0:1, 0:1], min_val=0, max_val=LINES) > 0):
                    dve.wait_ge(cols_in, 48)
                    for c in range(CHUNKS):
                        dve.tensor_scalar(own[:, c * BLOCKS:(c + 1) * BLOCKS], const[:, C_NODE:C_NODE + BLOCKS],
                                          float(c * CE), None, ALU.add)
                    dve.tensor_copy(dstf[:, :], dst[:, :])
                    dve.memset(rank[:, :], 0.0).then_inc(prepared, 1)
                    dve.wait_ge(prepared, 1)
                    with dve.Fori(0, CHUNKS) as c:
                        dve.wait_ge(chunk_in, c * 16 + 16)
                        dve.tensor_copy(key, chunk).then_inc(key_set, 1)
                        dve.wait_ge(key_set, c + 1)
                        dve.sem_inc(carry, 1)
                        with dve.Fori(0, ET) as t:
                            n = c * ET + t
                            dve.tensor_scalar(work, key, dstf[:, bass.ds(t, 1)], float(EP), ALU.subtract, ALU.mult
                                              ).then_inc(s1, 1)
                            dve.wait_ge(s1, n + 1)
                            dve.scalar_tensor_tensor(work, work, own[:, bass.ds(t, 1)], number, ALU.subtract, ALU.add
                                                     ).then_inc(s2, 1)
                            dve.wait_ge(s2, n + 1)
                            dve.tensor_scalar(work, work, 0.0, None, ALU.is_lt).then_inc(s3, 1)
                            dve.wait_ge(s3, n + 1)
                            dve.tensor_reduce(part[:, bass.ds(t, 1)], work, AX.X, ALU.add).then_inc(s4, 1)
                            dve.wait_ge(s4, n + 1)
                        dve.tensor_scalar(own[:, :], own[:, :], -float(CE), None, ALU.add).then_inc(own_set, 1)
                        dve.tensor_tensor(rank[:, :], rank[:, :], part[:, :], ALU.add).then_inc(rank_set, 1)
                        dve.wait_ge(own_set, c + 1)
                        dve.wait_ge(rank_set, c + 1)

        place_set, moved = sem("so_place_set"), sem("so_moved")
        with nc.Block() as block:
            @block.gpsimd
            def _(pool):
                with pool.If(pool.value_load(unsorted[0:1, 0:1], min_val=0, max_val=LINES) > 0):
                    def move(t):
                        if not isinstance(t, int):
                            pool.wait_ge(moved, t * 16)
                        pool.tensor_copy(place[:, :], rank[:, bass.ds(t, 1)]).then_inc(place_set, 1)
                        pool.tensor_copy(edge[:, 0:1], src[:, bass.ds(t, 1)]).then_inc(place_set, 1)
                        pool.tensor_copy(edge[:, 1:2], dst[:, bass.ds(t, 1)]).then_inc(place_set, 1)
                        pool.wait_ge(place_set, t * 3 + 3)
                        pool.sem_inc(carry, 1)
                        pool.indirect_dma_start(dram["edges"],
                                                bass.IndirectOffsetOnAxis(ap=place[:, :].bitcast(U32), axis=0),
                                                edge[:, :], None).then_inc(moved, 16)
                    move(0)
                    with pool.Fori(1, ET) as t:
                        move(t)
                    pool.wait_ge(moved, ET * 16)

        made = sem("so_made")
        with nc.Block() as block:
            @block.sync
            def _(sp):
                with sp.If(sp.value_load(unsorted[0:1, 0:1], min_val=0, max_val=LINES) > 0):
                    srcs, dsts = dram["edges"][:, 0:1], dram["edges"][:, 1:2]
                    with sp.Fori(0, ET) as t:
                        sp.dma_start(dram["t_src_t"][:, bass.ds(t, 1)], srcs[bass.ds(t * P, P), :],
                                     allow_slow_non_contiguous=True).then_inc(made, 16)
                        sp.dma_start(dram["t_dst_t"][:, bass.ds(t, 1)], dsts[bass.ds(t * P, P), :],
                                     allow_slow_non_contiguous=True).then_inc(made, 16)
                        sp.wait_ge(made, t * 32 + 32)
                        sp.sem_inc(carry, 1)
                    for name, n, w in (("t_dst_line", LINES, LW), ("t_dst_chunks", CHUNKS, CE)):
                        for q in range(n):
                            lo, hi = max(q * w - 1, 0), min((q + 1) * w + 1, EP)
                            at = lo - (q * w - 1)
                            sp.dma_start(dram[name][q:q + 1, at:at + hi - lo].rearrange("a e -> e a"),
                                         dsts[lo:hi, :],
                                     allow_slow_non_contiguous=True).then_inc(made, 16)
                    sp.dma_start(dram["t_dst_last"].rearrange("a s -> s a"),
                                 dram["edges"].rearrange("(s w) c -> s (w c)", w=H * P)[:, 2 * H * P - 1:2 * H * P],
                                     allow_slow_non_contiguous=True).then_inc(made, 16)
                    sp.wait_ge(made, ET * 32 + (LINES + CHUNKS + 1) * 16)


def score_phase(nc, ctx, sb, sem, a, dram, FDST, scores, r2, const, rows, bank, ident):
    with ExitStack() as loc:
        src = sb(loc, "src", [P, ET], I32)
        dlast = sb(loc, "dlast", [1, ET // H], I32)
        dline = sb(loc, "dline", [LINES, LW], I32)
        dline16 = sb(loc, "dline16", [LINES, LW], I16)
        idx = sb(loc, "idx", [P, U], I32)
        gath = r2[:, 0:U * 2 * D].rearrange("p (u d) -> p u d", d=2 * D)
        dstb = sb(loc, "dstb", [P, Q, H * P], I16)
        oht = sb(loc, "oht", [P, 2, 2, H * P])
        sil = sb(loc, "sil", [P, 4, 2 * D])
        attn = sb(loc, "attn", [P, 2 * D])
        mark = sb(loc, "mark", [P, 1])
        mul_done = sem("mul_done")
        slot_free = sem("slot_free")
        in_s, d16, d16_out, dl = sem("in_s"), sem("d16"), sem("d16_out"), sem("dl")
        idx_set = sem("idx_set")
        g_in = [sem(f"g_in{q}") for q in range(Q)]
        fv_out = [sem(f"fv_out{q}") for q in range(Q)]
        dstb_in = [sem(f"dstb_in{q}") for q in range(Q)]
        oht_ready, oht_used, z_done, sil_done, score_done, prod_done = (
            sem("oht_ready"), sem("oht_used"), sem("z_done"), sem("sil_done"), sem("score_done"), sem("prod_done"))
        fv_rows = dram["fv"].rearrange("(t p) d -> p t d", p=P)
        halves = dram["tab"].rearrange("n (o d) -> (n o) d", o=2)
        AHEAD = 3
        d16_line = dram["d16"].rearrange("(q w) -> q w", w=LW)

        with nc.Block() as block:
            @block.sync
            def _(sp):
                sp.dma_start(src[:, :], dram["t_src_t"]).then_inc(in_s, 16)
                sp.dma_start(dline[:, :], dram["t_dst_line"][:, 1:1 + LW]).then_inc(in_s, 16)
                sp.dma_start(dlast[0:1, :], dram["t_dst_last"]).then_inc(in_s, 16)
                sp.dma_start(attn[:, 0:D], a["attn"].partition_broadcast(P)).then_inc(in_s, 16)
                sp.dma_start(attn[:, D:2 * D], a["attn"].partition_broadcast(P)).then_inc(in_s, 16)
                sp.wait_ge(d16, 1)
                sp.dma_start(d16_line, dline16[:, :]).then_inc(d16_out, 16)
                sp.wait_ge(d16_out, 16)

            @block.vector
            def _(dve):
                dve.wait_ge(in_s, 80)
                dve.tensor_copy(dline16[:, :], dline[:, :]).then_inc(d16, 1)
                odd = src[:, :].rearrange("p (t o) -> p t o", o=2)[:, :, 1:2]
                dve.tensor_scalar(odd, odd, 2, None, ALU.mult)
                dve.tensor_scalar(dlast[0:1, :], dlast[0:1, :], 7, None, ALU.arith_shift_right).then_inc(dl, 1)

        def dtile(eng, s):
            return eng.value_load(dlast[0:1, bass.ds(s, 1)], min_val=0, max_val=NT - 1)

        with nc.Block() as block:
            @block.gpsimd
            def _(pool):
                def rnd(i):
                    first = isinstance(i, int)
                    for u in range(U):
                        if u % H == 0:
                            pool.wait_ge(idx_set, i * Q + (u // H + 1))
                            pool.sem_inc(slot_free, 1)
                        if not first:
                            pool.wait_ge(z_done, i * U + (u - U + 1))
                            if u % 2 == 0:
                                pool.wait_ge(fv_out[u // H], i * 16)
                            pool.sem_inc(slot_free, 1)
                        table, width = (halves, D) if u % 2 else (dram["tab"], 2 * D)
                        pool.indirect_dma_start(gath[:, u, 0:width], None, table,
                                                bass.IndirectOffsetOnAxis(ap=idx[:, u:u + 1].bitcast(U32), axis=0)
                                                ).then_inc(g_in[u // H], 16)
                rnd(0)
                with pool.Fori(1, ROUNDS) as i:
                    rnd(i)

            @block.sync
            def _(sp):
                def destinations(s, slot, first):
                    if not first:
                        sp.wait_ge(prod_done, s + (1 - Q))
                    sp.dma_start(dstb[:, slot, :], dram["d16"][bass.ds(s * (H * P), H * P)].partition_broadcast(P)
                                 ).then_inc(dstb_in[slot], 16)
                for s in range(AHEAD):
                    destinations(s, s, True)

                def rnd(i, more=True):
                    for q in range(Q):
                        if more or q + AHEAD < Q:
                            destinations(i * Q + (q + AHEAD), (q + AHEAD) % Q,
                                         isinstance(i, int) and i == 0 and q + AHEAD < Q)
                        sp.wait_ge(g_in[q], i * (16 * H) + 16 * H)
                        sp.dma_start(fv_rows[:, bass.ds((i * Q + q) * (H // 2), H // 2), :],
                                     gath[:, q * H:(q + 1) * H:2, D:2 * D]).then_inc(fv_out[q], 16)
                rnd(0)
                with sp.Fori(1, ROUNDS - 1) as i:
                    rnd(i)
                rnd(ROUNDS - 1, False)
                for q in range(Q):
                    sp.wait_ge(fv_out[q], ROUNDS * 16)

            @block.vector
            def _(dve):
                cur, prev = dve.alloc_register("cur_s1v"), dve.alloc_register("prev_s1v")
                dve.reg_mov(cur, 0)
                dve.reg_mov(prev, 0)

                def one_hot(q, k, d):
                    return dve.tensor_scalar(oht[:, q % 2, k, :], dstb[:, q, :],
                                             const[:, bass.ds(d + C_NODE, 1)], None, ALU.is_equal)

                def onehots(i, q, first):
                    s, hf = i * Q + q, q % 2
                    last = dtile(dve, s)
                    dve.wait_ge(dstb_in[q], i * 16 + 16)

                    def first_pair(d):
                        if not first:
                            dve.wait_ge(oht_used, dve.snap(prev, min_val=0, max_val=NT - 1) + (s - 1))
                        one_hot(q, 0, d).then_inc(oht_ready, 1)

                    def extra_pair(d):
                        dve.wait_ge(oht_used, d + s)
                        one_hot(q, 1, d).then_inc(oht_ready, 1)
                    pair_loop(dve, cur, prev, last, first_pair, extra_pair,
                              lambda d: one_hot(q, 1, d).then_inc(oht_ready, 1))

                def times_attn(s, hf):
                    dve.wait_ge(sil_done, s * 2 + 2)
                    v = sil[:, 2 * hf:2 * hf + 2, :]
                    dve.tensor_tensor(v, v, attn[:, :].unsqueeze(1).to_broadcast([P, 2, 2 * D]), ALU.mult
                                      ).then_inc(mul_done, 1)

                def head_sums(s, hf):
                    dve.wait_ge(mul_done, s + 1)
                    dve.tensor_reduce(scores[:, bass.ds(s * (H * HEADS), H * HEADS)],
                                      sil[:, 2 * hf:2 * hf + 2, :].rearrange("p k (q c) -> p (k q) c", c=HC),
                                      AX.X, ALU.add).then_inc(score_done, 1)

                def rnd(i):
                    for q in range(Q):
                        late = not isinstance(i, int) or q >= 2
                        if late:
                            times_attn(i * Q + (q - 2), q % 2)
                        onehots(i, q, not late)
                        if q or not isinstance(i, int):
                            dve.wait_ge(prod_done, i * Q + q)
                        dve.tensor_copy(mark[:, :], ident[:, 0:1]).then_inc(prod_done, 1)
                        if late:
                            head_sums(i * Q + (q - 2), q % 2)
                rnd(0)
                with dve.Fori(1, ROUNDS) as i:
                    rnd(i)
                for s in (ROUNDS * Q - 2, ROUNDS * Q - 1):
                    times_attn(s, s % 2)
                    head_sums(s, s % 2)

            @block.tensor
            def _(pe):
                cur = pe.alloc_register("cur_s1p")
                pe.reg_mov(cur, 0)
                dest = lambda u: bank[u // 2 % 4][:, (u % 2) * D:(u % 2 + 1) * D]

                def rnd(i):
                    first = isinstance(i, int)
                    for q in range(Q):
                        s, hf = i * Q + q, q % 2
                        last = dtile(pe, s)
                        us = range(q * H, q * H + H)
                        if q >= 2 or not first:
                            pe.wait_ge(sil_done, i * K + (2 * q - 2))

                        def pair(d, start, k):
                            pe.wait_ge(oht_ready, d + (s + 1))
                            for u in us:
                                ins = pe.matmul(dest(u), oht[:, hf, k, (u % H) * P:(u % H + 1) * P],
                                                FDST[:, bass.ds(d, 1), :].rearrange("p a d -> p (a d)"),
                                                start=start and u % 2 == 0, stop=False, skip_group_check=True)
                            ins.then_inc(oht_used, 1)
                        pair_loop(pe, cur, None, last, lambda d: pair(d, True, 0), lambda d: pair(d, False, 1))
                        pe.wait_ge(g_in[q], i * (16 * H) + 16 * H)
                        for u in us:
                            pe.matmul(dest(u), ident, gath[:, u, 0:D], start=False, stop=True,
                                      skip_group_check=True).then_inc(z_done, 1)
                rnd(0)
                with pe.Fori(1, ROUNDS) as i:
                    rnd(i)

            @block.scalar
            def _(act):
                def indices(i, q):
                    act.activation(idx[:, q * H:(q + 1) * H], src[:, bass.ds(i * U + q * H, H)], ACT.Copy
                                   ).then_inc(idx_set, 1)
                for q in range(Q):
                    indices(0, q)

                def rnd(i, more=True):
                    for k in range(K):
                        act.wait_ge(z_done, i * U + (2 * k + 2))
                        if k >= 4 or not (isinstance(i, int) and i == 0):
                            act.wait_ge(score_done, i * Q + (k // 2 - 1))
                        act.activation(sil[:, k % 4, :], bank[k % 4][:, :], ACT.Silu).then_inc(sil_done, 1)
                        if more and k % (H // 2) == H // 2 - 1:
                            indices(i + 1, k // (H // 2))
                rnd(0)
                with act.Fori(1, ROUNDS - 1) as i:
                    rnd(i)
                rnd(ROUNDS - 1, False)


def softmax_phase(nc, ctx, sb, sem, dram, r2, r3, scores, r1, bank, ident, weights):
    with ExitStack() as loc:
        stage = sb(loc, "stage", [P, G, P])
        stage2 = sb(loc, "stage2", [P, G, P])
        line = sb(loc, "line", [1, 4 * P])
        colv = sb(loc, "colv", [P, 8])
        dst_c = r1[:, ET * HEADS:ET * HEADS + CE + 2].bitcast(I32)
        brk = r2[:, 0:CE + 1]
        sc = r3[:, 0:CE]
        run = r2[:, CE + 1:2 * CE + 1]
        top = r3[:, CE:2 * CE]
        brow = sb(loc, "brow", [1, P])
        in_c, dvs, staged, tin, tout = sem("in_c"), sem("dvs"), sem("staged"), sem("tin"), sem("tout")
        lt, lf = sem("lt"), sem("lf")
        sc4 = scores.rearrange("p (j b h) -> p b h j", b=BLOCKS, h=HEADS)
        w4 = weights.rearrange("p (j b h) -> p b h j", b=BLOCKS, h=HEADS)

        with nc.Block() as block:
            @block.sync
            def _(sp):
                for h in range(HEADS):
                    sp.dma_start(dst_c[h * CHUNKS:(h + 1) * CHUNKS, :], dram["t_dst_chunks"]).then_inc(in_c, 16)

            @block.scalar
            def _(act):
                def group(g):
                    for u in range(G):
                        if not isinstance(g, int) and u % 4 == 0:
                            act.wait_ge(tin, g * 2 + (u // 4 - 1))
                        act.activation(stage[:, u, :].rearrange("p (h j) -> p h j", h=HEADS),
                                       sc4[:, bass.ds(g * G + u, 1), :, :].rearrange("p a h j -> p (a h) j"),
                                       ACT.Copy).then_inc(staged, 1)
                group(0)
                with act.Fori(1, NG) as g:
                    group(g)

            @block.tensor
            def _(pe):
                def group(g):
                    for k in range(2):
                        if not isinstance(g, int):
                            pe.wait_ge(tout, g * 2 + (k - 1))
                        n = 4 - k
                        pe.wait_ge(staged, g * G + (4 * k + n))
                        for u in range(n):
                            last = pe.transpose(bank[k][:, u * P:(u + 1) * P], stage[:, 4 * k + u, :], ident)
                        last.then_inc(tin, 1)
                group(0)
                with pe.Fori(1, NG) as g:
                    group(g)
                for r in range(2):
                    pe.wait_ge(lt, 2 * r + 1)
                    for k in range(2):
                        last = pe.transpose(bank[2][0:1, k * P:(k + 1) * P], colv[:, k:k + 1], ident)
                    last.then_inc(lf, 1)
                    pe.wait_ge(lt, 2 * r + 2)
                    pe.matmul(bank[3][:, 0:1], brow[0:1, :], ident[0:1, 0:1], start=True, stop=True).then_inc(lf, 1)

            @block.vector
            def _(dve):
                st = Steps(dve, dvs)
                with dve.Fori(0, NG) as g:
                    for k in range(2):
                        n = 4 - k
                        dve.wait_ge(tin, g * 2 + (k + 1))
                        dve.tensor_copy(sc[:, bass.ds((g * G + 4 * k) * P, n * P)], bank[k][:, 0:n * P]).then_inc(tout, 1)
                dve.wait_ge(in_c, HEADS * 16)
                st.link(dve.tensor_tensor(brk, dst_c[:, 0:CE + 1], dst_c[:, 1:CE + 2], ALU.not_equal))
                st.link(dve.tensor_scalar(brk, brk, -FAR, None, ALU.mult))
                st.link(dve.tensor_tensor(colv[:, 2:3], dst_c[:, 1:2], dst_c[:, CE:CE + 1], ALU.not_equal))
                st.link(dve.tensor_scalar(colv[:, 2:3], colv[:, 2:3], -FAR, None, ALU.mult))
                dve.wait_ge(tout, NG * 2)

                def scan(dst, rev, init):
                    if rev:
                        return dve.tensor_tensor_scan(dst[:, ::-1], brk[:, CE:0:-1], run[:, ::-1], init, ALU.add, ALU.max)
                    return dve.tensor_tensor_scan(dst, brk[:, 0:CE], sc, init, ALU.add, ALU.max)

                for r in range(2):
                    dst = top if r else run
                    st.link(scan(dst, r, -FAR))
                    st.link(dve.tensor_copy(colv[:, 0:1], dst[:, 0:1] if r else dst[:, CE - 1:CE]))
                    edge = brk[:, CE:CE + 1] if r else brk[:, 0:1]
                    dve.tensor_tensor(colv[:, 1:2], edge, colv[:, 2:3], ALU.add).then_inc(lt, 1)
                    dve.wait_ge(lf, 2 * r + 1)
                    st.link(dve.tensor_copy(line[:, 0:2 * P], bank[2][0:1, 0:2 * P]))
                    if r:
                        st.link(dve.tensor_tensor_scan(line[:, 3 * P - 1:2 * P - 1:-1], line[:, 2 * P - 1:P - 1:-1],
                                                       line[:, P - 1::-1], -FAR, ALU.add, ALU.max))
                    else:
                        st.link(dve.tensor_tensor_scan(line[:, 2 * P:3 * P], line[:, P:2 * P], line[:, 0:P],
                                                       -FAR, ALU.add, ALU.max))
                    st.link(dve.memset(brow[:, :], -FAR))
                    hj = lambda v: v.rearrange("p (h j) -> p h j", j=CHUNKS)
                    to, of = (slice(0, CHUNKS - 1), slice(1, CHUNKS)) if r else (slice(1, CHUNKS), slice(0, CHUNKS - 1))
                    dve.tensor_copy(hj(brow[:, :])[:, :, to], hj(line[:, 2 * P:3 * P])[:, :, of]).then_inc(lt, 1)
                    dve.wait_ge(lf, 2 * r + 2)
                    st.link(dve.tensor_copy(colv[:, 3 + r:4 + r], bank[3][:, 0:1]))
                    st.link(scan(dst, r, colv[:, 3 + r:4 + r]))

        sub, ex, wps, wev = sem("sub"), sem("ex"), sem("wps"), sem("wev")
        with nc.Block() as block:
            @block.vector
            def _(dve):
                def differences(g, first=False):
                    if not first:
                        dve.wait_ge(ex, g)
                    sl = bass.ds(g * G * P, G * P)
                    dve.tensor_tensor(stage[:, :, :].rearrange("p u q -> p (u q)"), sc[:, sl], top[:, sl],
                                      ALU.subtract).then_inc(sub, 1)

                def back(g):
                    for k in range(2):
                        n = 4 - k
                        dve.wait_ge(wps, g * 2 + (k + 1))
                        for u in range(n):
                            ins = dve.tensor_copy(
                                w4[:, bass.ds(g * G + 4 * k + u, 1), :, :].rearrange("p a h j -> p (a h) j"),
                                bank[k][:, u * P:(u + 1) * P].rearrange("p (h j) -> p h j", h=HEADS))
                        ins.then_inc(wev, 1)
                differences(0, True)
                with dve.Fori(0, NG - 1) as g:
                    differences(g + 1)
                    back(g)
                back(NG - 1)

            @block.scalar
            def _(act):
                def group(g):
                    act.wait_ge(sub, g + 1)
                    if not isinstance(g, int):
                        act.wait_ge(wps, g * 2)
                    act.activation(stage2[:, :, :], stage[:, :, :], ACT.Exp).then_inc(ex, 1)
                group(0)
                with act.Fori(1, NG) as g:
                    group(g)

            @block.tensor
            def _(pe):
                def group(g):
                    pe.wait_ge(ex, g + 1)
                    for k in range(2):
                        if not isinstance(g, int):
                            pe.wait_ge(wev, g * 2 + (k - 1))
                        for u in range(4 - k):
                            last = pe.transpose(bank[k][:, u * P:(u + 1) * P], stage2[:, 4 * k + u, :], ident)
                        last.then_inc(wps, 1)
                group(0)
                with pe.Fori(1, NG) as g:
                    group(g)


def message_phase(nc, ctx, sb, sem, a, dram, weights, r2, r3, const, bank01):
    with ExitStack() as loc:
        dlast = sb(loc, "dlast2", [1, ET // H], I32)
        dst = sb(loc, "dst2", [P, ET], I32)
        src = sb(loc, "src2", [P, ET // 2, 2], I32)
        idx = sb(loc, "idx2", [P, Q, H // 2, 1], I32)
        dstf = sb(loc, "dstf", [P, ET])
        fv = r3[:, 0:U * D].rearrange("p (u d) -> p u d", d=D)
        msg = sb(loc, "msg", [P, 2 * H, MSG])
        oh = sb(loc, "oh", [P, 2, 2, H, P])
        zero = sb(loc, "zero", [P, MSG])
        acc = r2[:, :].rearrange("p (t m) -> p t m", m=MSG)
        in_m, dl2 = sem("in_m"), sem("dl2")
        fv_in = [sem(f"fv_in{q}") for q in range(Q)]
        halves = dram["tab"].rearrange("n (o d) -> (n o) d", o=2)
        idx_set, slot_free = sem("idx_set2"), sem("slot_free2")
        fv_gathered = [sem(f"fv_gathered{q}") for q in range(Q)]
        msg_ready, oh_ready, oh_used, flushed, wcol = (
            sem("msg_ready"), sem("oh_ready"), sem("oh_used"), sem("flushed"), sem("wcol"))
        fv_rows = dram["fv"].rearrange("(t p) d -> p t d", p=P)
        iota = const[:, C_IOTA:C_IOTA + P]
        sums = lambda d: bank01[:, bass.ds(d % 2, 1), 0:MSG].rearrange("p a m -> p (a m)")

        with nc.Block() as block:
            @block.sync
            def _(sp):
                sp.dma_start(dst[:, :], dram["t_dst_t"]).then_inc(in_m, 16)
                sp.dma_start(src[:, :, :], dram["t_src_t"].rearrange("p (t o) -> p t o", o=2)).then_inc(in_m, 16)
                sp.dma_start(dlast[0:1, :], dram["t_dst_last"]).then_inc(in_m, 16)

            @block.vector
            def _(dve):
                dve.wait_ge(in_m, 48)
                dve.tensor_copy(dstf[:, :], dst[:, :])
                dve.tensor_scalar(src[:, :, :], src[:, :, :], 2, 1, ALU.mult, ALU.add)
                dve.memset(zero[:, :], 0.0)
                dve.memset(msg[:, :, :], 0.0)
                dve.tensor_scalar(dlast[0:1, :], dlast[0:1, :], 7, None, ALU.arith_shift_right).then_inc(dl2, 1)

        def dtile(eng, s):
            return eng.value_load(dlast[0:1, bass.ds(s, 1)], min_val=0, max_val=NT - 1)

        with nc.Block() as block:
            @block.sync
            def _(sp):
                def rnd(i):
                    for q in range(Q):
                        if not isinstance(i, int):
                            sp.wait_ge(msg_ready, i * Q + (q + 1 - Q))
                        sp.dma_start(fv[:, q * H:q * H + H:2, :],
                                     fv_rows[:, bass.ds((i * Q + q) * (H // 2), H // 2), :]).then_inc(fv_in[q], 16)
                rnd(0)
                with sp.Fori(1, ROUNDS) as i:
                    rnd(i)

            @block.gpsimd
            def _(pool):
                with pool.Fori(0, ROUNDS) as i:
                    for q in range(Q):
                        pool.wait_ge(idx_set, i * Q + (q + 1))
                        pool.sem_inc(slot_free, 1)
                        for k in range(H // 2):
                            pool.indirect_dma_start(
                                fv[:, q * H + 2 * k + 1, :], None, halves,
                                bass.IndirectOffsetOnAxis(ap=idx[:, q, k, :].bitcast(U32), axis=0)
                                ).then_inc(fv_gathered[q], 16)

            @block.scalar
            def _(act):
                cur = act.alloc_register("cur_s2a")
                act.reg_mov(cur, 0)

                def indices(s, q):
                    act.activation(idx[:, q, :, :], src[:, bass.ds(s * (H // 2), H // 2), 1:2], ACT.Copy
                                   ).then_inc(idx_set, 1)
                for q in range(Q):
                    indices(q, q)

                def rnd(i, more=True):
                    for q in range(Q):
                        s = i * Q + q
                        last = dtile(act, s)
                        act.wait_ge(msg_ready, s + 1)
                        act.activation(msg[:, q % 2 * H:q % 2 * H + H, D:MSG],
                                       weights[:, bass.ds(s * H * HEADS, H * HEADS)].rearrange(
                                           "p (u h) -> p u h", h=HEADS), ACT.Copy).then_inc(wcol, 1)

                        def extra_pair(d):
                            act.wait_ge(oh_used, d + s)
                            act.activation(acc[:, bass.ds(d - 1, 1), :].rearrange("p a m -> p (a m)"),
                                           sums(d - 1), ACT.Copy).then_inc(flushed, 1)
                        pair_loop(act, cur, None, last, lambda d: None, extra_pair)
                        if more:
                            indices(s + Q, q)
                with act.Fori(0, ROUNDS - 1) as i:
                    rnd(i)
                rnd(ROUNDS - 1, False)
                act.wait_ge(oh_used, ET // H + NT - 1)
                act.activation(acc[:, NT - 1, :], sums(NT - 1), ACT.Copy).then_inc(flushed, 1)

            @block.vector
            def _(dve):
                cur, prev = dve.alloc_register("cur_s2v"), dve.alloc_register("prev_s2v")
                dve.reg_mov(cur, 0)
                dve.reg_mov(prev, 0)

                def rnd(i):
                    first = isinstance(i, int)
                    for q in range(Q):
                        s, hf = i * Q + q, q % 2
                        us = slice(hf * H, hf * H + H)
                        last = dtile(dve, s)
                        dve.wait_ge(fv_in[q], i * 16 + 16)
                        dve.wait_ge(fv_gathered[q], i * (8 * H) + 8 * H)
                        if q >= 2 or not first:
                            dve.wait_ge(oh_used, dve.snap(prev, min_val=0, max_val=NT - 1) + (s - 1))
                        wt = weights[:, bass.ds(s * H * HEADS, H * HEADS)].rearrange(
                            "p (u h) -> p u h", h=HEADS).unsqueeze(3).to_broadcast([P, H, HEADS, HC])
                        dve.tensor_tensor(msg[:, us, 0:D].rearrange("p u (h c) -> p u h c", c=HC),
                                          fv[:, q * H:q * H + H, :].rearrange("p u (h c) -> p u h c", c=HC), wt,
                                          ALU.mult).then_inc(msg_ready, 1)

                        def one_hot(d, k):
                            return dve.scalar_tensor_tensor(
                                oh[:, hf, k, :, :], iota.unsqueeze(1).to_broadcast([P, H, P]),
                                const[:, bass.ds(d + C_BASE, 1)],
                                dstf[:, bass.ds(s * H, H)].unsqueeze(2).to_broadcast([P, H, P]),
                                ALU.add, ALU.is_equal)

                        def extra_pair(d):
                            dve.wait_ge(oh_used, d + s)
                            one_hot(d, 1).then_inc(oh_ready, 1)
                        pair_loop(dve, cur, prev, last, lambda d: one_hot(d, 0).then_inc(oh_ready, 1), extra_pair,
                                  lambda d: one_hot(d, 1).then_inc(oh_ready, 1))
                rnd(0)
                with dve.Fori(1, ROUNDS) as i:
                    rnd(i)

            @block.tensor
            def _(pe):
                cur = pe.alloc_register("cur_s2p")
                pe.reg_mov(cur, 0)
                pe.matmul(sums(0), zero[:, 0:P], zero[:, :], start=True, stop=True).then_inc(flushed, 1)

                with pe.Fori(0, ROUNDS) as i:
                    for q in range(Q):
                        s, hf = i * Q + q, q % 2
                        last = dtile(pe, s)
                        pe.wait_ge(wcol, s + 1)

                        def pair(d, start, k):
                            pe.wait_ge(oh_ready, d + (s + 1))
                            for u in range(H):
                                ins = pe.matmul(sums(d), oh[:, hf, k, u, :], msg[:, hf * H + u, :],
                                                start=start and u == 0, stop=True, skip_group_check=True)
                            ins.then_inc(oh_used, 1)

                        def extra_pair(d):
                            pe.wait_ge(flushed, d)
                            pair(d, True, 1)
                        pair_loop(pe, cur, None, last, lambda d: pair(d, False, 0), extra_pair)


def ffn_phase(nc, ctx, sb, sem, a, dram, out, x1, r1, r2, const, bank, ident):
    xf = r1[:, 0:NT * D].rearrange("p (t d) -> p t d", d=D)
    xft = r2[:, 0:NT * D].rearrange("p (t f q) -> p f t q", f=2, q=P)
    FC = FF // P
    with ExitStack() as loc:
        stats = sb(loc, "stats_f", [P, G, 6])
        aggr = sb(loc, "aggr_f", [P, G, 2])
        mv = sb(loc, "mv_f", [P, NT, 2])
        rs = sb(loc, "rs_f", [P, 2, NT])
        wr = sb(loc, "wr", [P, 2, EXPERTS])
        ones = sb(loc, "ones", [P, P])
        br = sb(loc, "br", [1, EXPERTS])
        w1 = sb(loc, "w1", [P, 2, 2, FF])
        w2 = sb(loc, "w2", [P, 2, FC, D])
        b1 = sb(loc, "b1", [P, 2, FC])
        b2 = sb(loc, "b2", [P, 2, D])
        b2c = sb(loc, "b2c", [P, D])
        gb = sb(loc, "gb", [P, 2, D])
        rt = sb(loc, "rt", [1, 12, 8])
        rti = sb(loc, "rti", [1, 8], U32)
        mrow = sb(loc, "mrow", [1, D])
        mcol = sb(loc, "mcol", [P, 2])
        wb = sb(loc, "wb", [P, 2])
        gt = sb(loc, "gt", [P, 2 * FC, G * P])
        slot = lambda k: gt[:, 2 * k:2 * k + 2, :].rearrange("p a b -> p (a b)").rearrange("p (u d) -> p u d", d=D)
        xs, base, hh, pre = slot(0), slot(1), slot(2), slot(3)
        sl = w1[:, :, :, :].rearrange("p e k f -> p (e k f)")[:, 0:G * D].rearrange("p (u d) -> p u d", d=D)
        den = sb(loc, "den", [P, G, HEADS])
        rec = sb(loc, "rec", [P, G, HEADS])
        acc = r2[:, :].rearrange("p (t m) -> p t m", m=MSG)
        h_rows = dram["h"].rearrange("(t p) d -> p t d", p=P)
        base_rows = dram["base"].rearrange("(t p) d -> p t d", p=P)
        stats_done = sem("stats_done_f")
        w_in, dva, dvb, var_ready, sd = sem("w_in_f"), sem("dva"), sem("dvb"), sem("var_f"), sem("sd_f")

        def row_stats(dve, st, src, g):
            dve.sem_inc(stats_done, 1)
            for u in range(G):
                ins = dve.bn_stats(stats[:, u, :], src[:, bass.ds(g * G + u, 1), :].rearrange("p a d -> p (a d)"))
                st.done(ins) if u < G - 1 else st.link(ins)
            dve.sem_inc(stats_done, 1)
            for u in range(G):
                ins = dve.bn_aggr(aggr[:, u, :], stats[:, u, :])
                st.done(ins) if u < G - 1 else st.link(ins)
            st.link(dve.tensor_copy(mv[:, bass.ds(g * G, G), :], aggr[:, :, :]))

        in_b, in_h, dvc, pre_ready, sl_ready, x1_ready, ones_set = (
            sem("in_b"), sem("in_h"), sem("dvc"), sem("pre_ready"), sem("sl_ready"), sem("x1_ready"), sem("ones_set_f"))
        xs_ready, t_ps, t_ev, kept, sum_done = sem("xs_ready"), sem("t_ps"), sem("t_ev"), sem("kept"), sem("sum_done")
        mr, mc, exs, exd, wbd, wbp = sem("mr"), sem("mc"), sem("exs"), sem("exd"), sem("wbd"), sem("wbp")
        idx_ready, ex_in, w1_in = sem("idx_ready"), sem("ex_in"), [sem("w1_in0"), sem("w1_in1")]
        col = lambda k, t: rs[:, k, bass.ds(t, 1)]
        mu = lambda t: mv[:, bass.ds(t, 1), 0:1].rearrange("p a b -> p (a b)")

        with nc.Block() as block:
            @block.vector
            def _(dve):
                dve.memset(ones[:, :], 1.0).then_inc(ones_set, 1)
                sa, sc = Steps(dve, dvc), Steps(dve, dva)

                def combine(g):
                    first = isinstance(g, int) and g == 0
                    sa.enter(g, 3, 0)
                    sa.link(dve.tensor_scalar(den[:, :, :], acc[:, bass.ds(g * G, G), D:MSG], 1e-30, None, ALU.max))
                    sa.link(dve.reciprocal(rec[:, :, :], den[:, :, :]))
                    if not first:
                        dve.wait_ge(sl_ready, g)
                    sa.link(dve.tensor_tensor(
                        pre[:, :, :].rearrange("p t (h c) -> p t h c", c=HC),
                        acc[:, bass.ds(g * G, G), 0:D].rearrange("p t (h c) -> p t h c", c=HC),
                        rec[:, :, :].unsqueeze(3).to_broadcast([P, G, HEADS, HC]), ALU.mult))
                    dve.wait_ge(in_h, g * 16 + 16)
                    dve.tensor_tensor(pre[:, :, :], pre[:, :, :], hh[:, :, :], ALU.add).then_inc(pre_ready, 1)
                    sa.leave(0)
                    sa.base = 0

                def norm(g):
                    first = isinstance(g, int) and g == 0
                    sc.enter(g, 2 * G + 2, 0)
                    dve.wait_ge(x1_ready, g + 1)
                    row_stats(dve, sc, x1, g)
                    dve.tensor_scalar(rs[:, 0, bass.ds(g * G, G)], aggr[:, :, 1:2].rearrange("p t o -> p (t o)"),
                                      LN_EPS, None, ALU.add).then_inc(var_ready, 1)
                    dve.wait_ge(sd, g + 1)
                    sc.link(dve.reciprocal(rs[:, 0, bass.ds(g * G, G)], rs[:, 1, bass.ds(g * G, G)]))
                    if not first:
                        dve.wait_ge(t_ps, g * 4)
                        dve.wait_ge(kept, g)
                        dve.wait_ge(sum_done, g)
                    for u in range(G):
                        t = g * G + u
                        dve.tensor_scalar(xs[:, u, :], x1[:, bass.ds(t, 1), :].rearrange("p a d -> p (a d)"),
                                          mu(t), col(0, t), ALU.subtract, ALU.mult).then_inc(xs_ready, 1)
                    sc.leave(0)
                    sc.base = 0
                combine(0)
                combine(1)
                norm(0)
                with dve.Fori(2, NG) as g:
                    combine(g)
                    norm(g - 1)
                norm(NG - 1)
                st = Steps(dve, dvb)
                dve.wait_ge(sum_done, NG)
                dve.tensor_scalar(mrow[:, :], bank[6][0:1, 0:D], 1.0 / N_NODES, None, ALU.mult).then_inc(mr, 1)
                dve.wait_ge(mc, 1)
                st.link(dve.tensor_copy(mcol[:, :], bank[7][:, 0:2]))
                dve.tensor_copy(mcol[:, :], mcol[:, :]).then_inc(mr, 1)
                dve.wait_ge(mc, 2)
                r = lambda k: rt[:, k, :]
                r1c = lambda k, c: rt[:, k, c:c + 1]
                st.link(dve.tensor_tensor(r(0), bank[5][0:1, 0:EXPERTS], br[:, :], ALU.add))

                def softmax(src, n, dst, k):
                    st.link(dve.tensor_reduce(r1c(k, 0), rt[:, src, 0:n], AX.X, ALU.max))
                    dve.tensor_scalar(rt[:, dst, 0:n], rt[:, src, 0:n], r1c(k, 0), None, ALU.subtract).then_inc(exs, 1)
                    count[0] += 1
                    dve.wait_ge(exd, count[0])
                    st.link(dve.tensor_reduce(r1c(k, 1), rt[:, dst, 0:n], AX.X, ALU.add))
                    st.link(dve.reciprocal(r1c(k, 2), r1c(k, 1)))
                    st.link(dve.tensor_scalar(rt[:, dst, 0:n], rt[:, dst, 0:n], r1c(k, 2), None, ALU.mult))
                count = [0]
                softmax(0, EXPERTS, 1, 2)
                st.link(dve.tensor_scalar(r(3), r(1), float(N_NODES), 1e-30, ALU.mult, ALU.max))
                st.link(dve.reciprocal(r(3), r(3)))
                st.link(dve.tensor_scalar(r(3), r(3), CAPACITY, 1.0, ALU.mult, ALU.min))
                st.link(dve.tensor_tensor(r(4), r(3), r(1), ALU.mult))
                softmax(4, EXPERTS, 5, 6)
                st.link(dve.max(r(7), r(5)))
                dve.max_index(rti[:, :], r(7), r(5)).then_inc(idx_ready, 1)
                softmax(7, 2, 8, 9)
                dve.tensor_copy(rt[:, 10, 0:2], rt[:, 8, 0:2]).then_inc(wbp, 1)
                dve.wait_ge(wbd, 1)
                st.link(dve.tensor_copy(wb[:, :], bank[4][:, 0:2]))

            @block.gpsimd
            def _(pool):
                with pool.Fori(0, NG) as g:
                    pool.wait_ge(sl_ready, g + 1)
                    pool.wait_ge(in_b, g * 16 + 16)
                    pool.tensor_tensor(x1[:, bass.ds(g * G, G), :], base[:, :, :], sl[:, :, :], ALU.add
                                       ).then_inc(x1_ready, 1)

            @block.tensor
            def _(pe):
                pe.wait_ge(ones_set, 1)
                pe.wait_ge(w_in, 64)

                def group(g, start, stop):
                    first = isinstance(g, int) and start
                    for k in range(4):
                        n = min(2, G - 2 * k)
                        pe.wait_ge(xs_ready, g * G + (2 * k + n))
                        if not (first and k < 2):
                            pe.wait_ge(t_ev, g * 4 + (k - 1))
                        for u in range(n):
                            for f in range(2):
                                last = pe.transpose(bank[k % 2][:, (2 * u + f) * P:(2 * u + f + 1) * P],
                                                    xs[:, 2 * k + u, f * P:(f + 1) * P], ident)
                        last.then_inc(t_ps, 1)
                    for u in range(G):
                        one = const[:, C_REAL:C_REAL + 1] if stop and u == G - 1 else ones[:, 0:1]
                        last = pe.matmul(bank[6][0:1, 0:D], one, xs[:, u, :],
                                         start=start and u == 0, stop=stop and u == G - 1)
                    last.then_inc(sum_done, 1)
                group(0, True, False)
                with pe.Fori(1, NG - 1) as g:
                    group(g, False, False)
                group(NG - 1, False, True)
                pe.wait_ge(mr, 1)
                for f in range(2):
                    last = pe.matmul(bank[7][:, f:f + 1], mrow[0:1, f * P:(f + 1) * P], ones[0:1, 0:1],
                                     start=True, stop=True)
                last.then_inc(mc, 1)
                pe.wait_ge(mr, 2)
                for f in range(2):
                    last = pe.matmul(bank[5][0:1, 0:EXPERTS], mcol[:, f:f + 1], wr[:, f, :], start=f == 0, stop=f == 1)
                last.then_inc(mc, 1)
                pe.wait_ge(wbp, 1)
                pe.matmul(bank[4][:, 0:2], ones[0:1, :], rt[:, 10, 0:2], start=True, stop=True).then_inc(wbd, 1)

            @block.scalar
            def _(act):
                def silu(g):
                    if not isinstance(g, int):
                        act.wait_ge(x1_ready, g)
                    act.wait_ge(pre_ready, g + 1)
                    act.activation(sl[:, :, :], pre[:, :, :], ACT.Silu).then_inc(sl_ready, 1)

                def norm(g):
                    act.wait_ge(var_ready, g + 1)
                    act.activation(rs[:, 1, bass.ds(g * G, G)], rs[:, 0, bass.ds(g * G, G)], ACT.Sqrt).then_inc(sd, 1)
                    for k in range(4):
                        n = min(2, G - 2 * k)
                        act.wait_ge(t_ps, g * 4 + (k + 1))
                        act.activation(r2[:, bass.ds((g * G + 2 * k) * D, n * D)], bank[k % 2][:, 0:n * D],
                                       ACT.Copy).then_inc(t_ev, 1)
                    act.activation(xf[:, bass.ds(g * G, G), :], xs[:, :, :], ACT.Copy).then_inc(kept, 1)
                silu(0)
                with act.Fori(1, NG) as g:
                    silu(g)
                    norm(g - 1)
                norm(NG - 1)
                for c, (dst, n) in enumerate(((1, EXPERTS), (5, EXPERTS), (8, 2))):
                    act.wait_ge(exs, c + 1)
                    act.activation(rt[:, dst, 0:n], rt[:, dst, 0:n], ACT.Exp).then_inc(exd, 1)

            @block.sync
            def _(sp):
                def rows_in(g):
                    if not isinstance(g, int):
                        sp.wait_ge(pre_ready, g)
                    sp.dma_start(hh[:, :, :], h_rows[:, bass.ds(g * G, G), :]).then_inc(in_h, 16)
                    if not isinstance(g, int):
                        sp.wait_ge(x1_ready, g)
                    sp.dma_start(base[:, :, :], base_rows[:, bass.ds(g * G, G), :]).then_inc(in_b, 16)
                rows_in(0)
                sp.dma_start(wr[:, :, :], a["wr"]).then_inc(w_in, 16)
                sp.dma_start(br[:, :], a["br"]).then_inc(w_in, 16)
                sp.dma_start(gb[:, 0, :], a["gamma"].partition_broadcast(P)).then_inc(w_in, 16)
                sp.dma_start(gb[:, 1, :], a["beta"].partition_broadcast(P)).then_inc(w_in, 16)
                with sp.Fori(1, NG) as g:
                    rows_in(g)
                sp.wait_ge(idx_ready, 1)
                xs_ = []
                for e in range(2):
                    xs_.append(sp.value_load(rti[0:1, e:e + 1], min_val=0, max_val=EXPERTS - 1))
                    one = lambda v: v[bass.ds(xs_[e], 1)]
                    sp.dma_start(w1[:, e, :, :], one(a["w1"]).rearrange("a p k f -> p (a k) f")).then_inc(w1_in[e], 16)
                    sp.dma_start(b1[:, e, :], one(a["b1"]).rearrange("a p k -> p (a k)")).then_inc(w1_in[e], 16)
                for e in range(2):
                    one = lambda v: v[bass.ds(xs_[e], 1)]
                    sp.dma_start(w2[:, e, :, :], one(a["w2"]).rearrange("a p k f -> p (a k) f")).then_inc(ex_in, 16)
                    sp.dma_start(b2[:, e, :], one(a["b2"]).rearrange("a d -> (a d)").partition_broadcast(P)
                                 ).then_inc(ex_in, 16)

        up, act_done, y_ps, o_ready, x1b, dvf = sem("up"), sem("act_done"), sem("y_ps"), sem("o_ready"), sem("x1b"), sem("dvf")
        w2_scaled = sem("w2_scaled")
        add_b, o1, out_ready, stored = sem("add_b"), sem("o1"), sem("out_ready"), sem("stored")
        o_rows = out.rearrange("(t p) d -> p t d", p=P)
        Q = G * P // 2
        xft3 = r2[:, 0:NT * D].rearrange("p (t f q) -> p f t q", f=2, q=P)
        HT = 2 * FC * 4

        with nc.Block() as block:
            @block.tensor
            def _(pe):
                def group(g):
                    first = isinstance(g, int) and g == 0
                    n = 0
                    for e in range(2):
                        if first:
                            pe.wait_ge(w1_in[e], 32)
                        for c in range(FC):
                            for q in range(2):
                                t0, nt = (0, 4) if q == 0 else (4, 3)
                                if not (first and n < 4):
                                    pe.wait_ge(act_done, g * (4 * FC) + (n - 3))
                                for f in range(2):
                                    last = pe.matmul(bank[n % 4][:, 0:nt * P].rearrange("p (t q) -> p t q", q=P),
                                                     w1[:, e, f, c * P:(c + 1) * P],
                                                     xft3[:, f, bass.ds(g * G + t0, nt), :],
                                                     start=f == 0, stop=f == 1)
                                last.then_inc(up, 1)
                                n += 1
                    pe.wait_ge(act_done, g * (4 * FC) + 4 * FC)
                    if first:
                        pe.wait_ge(w2_scaled, 1)
                    for u in range(G):
                        if not (first and u < 4):
                            pe.wait_ge(o_ready, g * G + reuse(u, 4))
                        for m in range(2 * FC):
                            last = pe.matmul(bank[4 + u % 4][:, 0:D], gt[:, m, u * P:(u + 1) * P],
                                             w2[:, m // FC, m % FC, :], start=m == 0, stop=m == 2 * FC - 1)
                        last.then_inc(y_ps, 1)
                group(0)
                with pe.Fori(1, NG) as g:
                    group(g)

            @block.scalar
            def _(act):
                def root(g):
                    act.wait_ge(var_ready, g + (NG + 1))
                    act.activation(rs[:, 1, bass.ds(g * G, G)], rs[:, 0, bass.ds(g * G, G)], ACT.Sqrt).then_inc(sd, 1)

                def group(g):
                    if not isinstance(g, int):
                        act.wait_ge(y_ps, g * G)
                    n = 0
                    for e in range(2):
                        for c in range(FC):
                            for q in range(2):
                                if n == 2 * FC and not isinstance(g, int):
                                    root(g - 1)
                                t0, nt = (0, 4) if q == 0 else (4, 3)
                                act.wait_ge(up, g * (4 * FC) + (n + 1))
                                act.activation(gt[:, e * FC + c, t0 * P:(t0 + nt) * P], bank[n % 4][:, 0:nt * P],
                                               ACT.Gelu, bias=b1[:, e, c:c + 1]).then_inc(act_done, 1)
                                n += 1
                group(0)
                with act.Fori(1, NG) as g:
                    group(g)
                root(NG - 1)

            @block.gpsimd
            def _(pool):
                with pool.Fori(0, NT) as t:
                    v = x1[:, bass.ds(t, 1), :].rearrange("p a d -> p (a d)")
                    pool.tensor_tensor(v, v, gb[:, 1, :], ALU.add).then_inc(x1b, 1)

            @block.vector
            def _(dve):
                st = Steps(dve, dvf)
                dve.wait_ge(ex_in, 4 * 16)
                for e in range(2):
                    st.link(dve.tensor_scalar(w2[:, e, :, :], w2[:, e, :, :], wb[:, e:e + 1], None, ALU.mult))
                st.link(dve.tensor_scalar(b2c[:, :], b2[:, 0, :], wb[:, 0:1], None, ALU.mult))
                st.link(dve.scalar_tensor_tensor(b2c[:, :], b2[:, 1, :], wb[:, 1:2], b2c[:, :], ALU.mult, ALU.add))

                dve.sem_inc(w2_scaled, 1)
                with dve.Fori(0, NG) as g:
                    for u in range(G):
                        v = xf[:, bass.ds(g * G + u, 1), :].rearrange("p a d -> p (a d)")
                        dve.tensor_tensor(v, v, b2c[:, :], ALU.add).then_inc(add_b, 1)
                    for u in range(G):
                        v = xf[:, bass.ds(g * G + u, 1), :].rearrange("p a d -> p (a d)")
                        dve.wait_ge(add_b, g * G + (u + 1))
                        dve.wait_ge(y_ps, g * G + (u + 1))
                        dve.tensor_tensor(v, bank[4 + u % 4][:, 0:D], v, ALU.add).then_inc(o_ready, 1)
                    st.enter(g, 2 * G + 2, 0)
                    dve.wait_ge(o_ready, g * G + G)
                    row_stats(dve, st, xf, g)
                    dve.tensor_scalar(rs[:, 0, bass.ds(g * G, G)], aggr[:, :, 1:2].rearrange("p t o -> p (t o)"),
                                      LN_EPS, None, ALU.add).then_inc(var_ready, 1)
                    dve.wait_ge(sd, g + (NG + 1))
                    st.link(dve.reciprocal(rs[:, 0, bass.ds(g * G, G)], rs[:, 1, bass.ds(g * G, G)]))
                    for u in range(G):
                        t = g * G + u
                        v = xf[:, bass.ds(t, 1), :].rearrange("p a d -> p (a d)")
                        dve.scalar_tensor_tensor(v, v, mu(t), gb[:, 0, :], ALU.subtract, ALU.mult).then_inc(o1, 1)
                    dve.wait_ge(x1b, g * G + G)
                    for u in range(G):
                        t = g * G + u
                        v = xf[:, bass.ds(t, 1), :].rearrange("p a d -> p (a d)")
                        dve.wait_ge(o1, t + 1)
                        dve.scalar_tensor_tensor(v, v, col(0, t),
                                                 x1[:, bass.ds(t, 1), :].rearrange("p a d -> p (a d)"),
                                                 ALU.mult, ALU.add).then_inc(out_ready, 1)
                    st.leave(0)

            @block.sync
            def _(sp):
                with sp.Fori(0, NG) as g:
                    sp.wait_ge(out_ready, g * G + G)
                    sp.dma_start(o_rows[:, bass.ds(g * G, G), :], xf[:, bass.ds(g * G, G), :]).then_inc(stored, 16)
                sp.wait_ge(stored, NG * 16)


DEBUG = False


def kernel(x, src, dst, L0_gnn_Wsrc, L0_gnn_bsrc, L0_gnn_Wdst, L0_gnn_bdst, L0_gnn_Wval, L0_gnn_bval, L0_gnn_attn,
           L0_mix_kln_weight, L0_mix_kln_bias, L0_mix_vln_weight, L0_mix_vln_bias, L0_ffn_Wr, L0_ffn_br, L0_ffn_W1,
           L0_ffn_b1, L0_ffn_W2, L0_ffn_b2, L0_ffn_gamma, L0_ffn_beta):
    import numpy as np
    import concourse.bacc as bacc
    from concourse.bass_utils import run_bass_kernel_spmd as run

    A = lambda v: np.ascontiguousarray(np.asarray(v))
    halves = lambda m: m.reshape(2, P, -1).transpose(1, 0, 2)
    pad_edges = np.full(EP - N_EDGES, PAD_NODE, np.int32)
    dst_p = np.concatenate([A(dst), pad_edges])
    src_p = np.concatenate([A(src), np.zeros(EP - N_EDGES, np.int32)])
    around = np.concatenate([np.int32([-1]), dst_p, np.int32([NP])])
    iota = np.arange(P, dtype=np.float32)
    const = np.zeros((P, C_END), np.float32)
    const[:, C_IDENT:C_IDENT + P] = np.eye(P)
    const[:, C_BLOCK:C_BLOCK + P] = np.kron(np.eye(P // HC), np.ones((HC, HC)))
    const[:, C_IOTA:C_IOTA + P] = iota
    const[:, C_BASE:C_BASE + NT] = P * np.arange(NT)
    const[:, C_NODE:C_NODE + NT] = P * np.arange(NT) + iota[:, None]
    const[:, C_ONE] = 1
    const[:, C_REAL] = P * (NT - 1) + iota < N_NODES
    flat = lambda v: A(v).reshape(-1)
    cols = lambda v: flat(v).reshape(2, P).T
    arrays = {
        "x": np.concatenate([A(x), np.zeros((NP - N_NODES, D), np.float32)]),
        "src_t": src_p.reshape(ET, P).T,
        "dst_t": dst_p.reshape(ET, P).T,
        "dst_last": dst_p.reshape(ET // H, H * P)[:, -1][None, :],
        "dst_line": np.stack([around[q * LW:(q + 1) * LW + 2] for q in range(LINES)]),
        "count_row": np.arange(CE, dtype=np.float32),
        "dst_chunks": np.stack([around[j * CE:(j + 1) * CE + 2] for j in range(CHUNKS)]),
        "wcat": halves(np.concatenate([A(L0_gnn_Wsrc).T, A(L0_gnn_Wval).T, A(L0_gnn_Wdst).T], axis=1)),
        "proj_bias": np.concatenate([A(L0_gnn_bsrc), A(L0_gnn_bval), A(L0_gnn_bdst)]),
        "attn": flat(L0_gnn_attn),
        "mix_rows": np.concatenate([flat(L0_mix_kln_weight), flat(L0_mix_kln_bias),
                                    flat(L0_mix_vln_weight), flat(L0_mix_vln_bias)]),
        "mix_cols": np.concatenate([cols(L0_mix_kln_weight), cols(L0_mix_kln_bias)], axis=1),
        "const": const,
        "wr": halves(A(L0_ffn_Wr)),
        "br": A(L0_ffn_br)[None, :],
        "w1": A(L0_ffn_W1).reshape(EXPERTS, 2, P, FF).transpose(0, 2, 1, 3),
        "w2": A(L0_ffn_W2).reshape(EXPERTS, FF // P, P, D).transpose(0, 2, 1, 3),
        "b1": A(L0_ffn_b1).reshape(EXPERTS, FF // P, P).transpose(0, 2, 1),
        "b2": A(L0_ffn_b2),
        "gamma": A(L0_ffn_gamma),
        "beta": A(L0_ffn_beta),
    }
    nc = bacc.Bacc("TRN2", target_bir_lowering=False, num_devices=1)
    args = {}
    for name, v in arrays.items():
        arrays[name] = np.ascontiguousarray(v)
        args[name] = nc.dram_tensor(f"in_{name}", v.shape, mybir.dt.from_np(v.dtype), kind="ExternalInput").ap()
    out = nc.dram_tensor("out", (NP, D), FP32, kind="ExternalOutput").ap()
    kind = "ExternalOutput" if DEBUG else "Internal"
    dram = {name: nc.dram_tensor(f"s_{name}", shape, dt, kind=kind).ap() for name, shape, dt in (
        ("tab", (NP, 2 * D), FP32), ("h", (NP, D), FP32), ("base", (NP, D), FP32), ("fv", (EP // 2, D), FP32),
        ("d16", (EP,), I16), ("edges", (EP, 2), I32))
        + tuple((f"t_{n}", arrays[n].shape, I32) for n in TABLES)}
    gps_layer(nc, args, out, dram)
    r = run(nc, [{f"in_{name}": v for name, v in arrays.items()}], core_ids=[0])
    if DEBUG:
        return tuple(r.results[0][f"s_{n}"][:N_NODES] for n in ("tab", "h", "base")) + (r.results[0]["out"][:N_NODES],)
    return r.results[0]["out"][:N_NODES]
```

```python
import concourse.bass as bass
from concourse import mybir
from concourse.alu_op_type import AluOpType as ALU
from contextlib import ExitStack

FP32 = mybir.dt.float32
I32 = mybir.dt.int32
U32 = mybir.dt.uint32
I16 = mybir.dt.int16
ACT = mybir.ActivationFunctionType
AX = mybir.AxisListType

N_NODES, N_EDGES, D, HEADS, EXPERTS, FF = 6250, 100000, 256, 8, 8, 512
P = 128
HC = D // HEADS
NT = -(-N_NODES // P)
NP = NT * P
G = 7
NG = NT // G
CHUNKS = P // HEADS
BLOCKS = -(-N_EDGES // (CHUNKS * P))
ET = CHUNKS * BLOCKS
EP = ET * P
CE = BLOCKS * P
U = 16
H = 4
Q = U // H
K = U // 2
ROUNDS = ET // U
MSG = D + HEADS
PAD_NODE = NP - 1
FAR = 1e37
LN_EPS, MIX_EPS = 1e-5, 1e-5
TABLES = ("src_t", "dst_t", "dst_last", "dst_line", "dst_chunks")
CAPACITY = float(-(-int(N_NODES * 1.25) // EXPERTS)) if (N_NODES * 1.25) % 1 == 0 else float(
    -(-int(N_NODES * 1.25 + 1) // EXPERTS))
assert NT == G * NG and ET == U * ROUNDS

C_IDENT, C_BLOCK, C_IOTA = 0, P, 2 * P
C_BASE = 3 * P
C_NODE = C_BASE + NT
C_REAL = C_NODE + NT
C_ONE = C_REAL + 1
C_END = C_ONE + 1
LINES = 112
LW = EP // LINES


def reuse(u, ring, n=G):
    return u - ring + 1 if u >= ring else max(w for w in range(n) if w % ring == u) + 1 - n


class Steps:

    def __init__(self, eng, sem):
        self.eng, self.sem, self.base, self.k, self.i, self.n = eng, sem, 0, 0, None, 0

    def done(self, ins):
        ins.then_inc(self.sem, 1)
        self.k += 1

    def value(self):
        return self.base + self.k if self.i is None else self.i * self.n + (self.base + self.k)

    def link(self, ins):
        self.done(ins)
        self.eng.wait_ge(self.sem, self.value())

    def enter(self, i, n, first):
        self.base, self.k, self.i, self.n = self.base + self.k - first * n, 0, i, n

    def leave(self, last):
        assert self.k == self.n, (self.k, self.n)
        self.base, self.k, self.i = self.base + last * self.n, 0, None


def gps_layer(nc, a, out, dram):
    ctx = ExitStack()
    with ctx:
        def sb(stack, name, shape, dt=FP32):
            return stack.enter_context(nc.sbuf_tensor(name, shape, dt))

        def sem(name):
            return ctx.enter_context(nc.semaphore(name))

        r1 = sb(ctx, "r1", [P, NT * D + 2])
        r2 = sb(ctx, "r2", [P, NT * MSG])
        r3 = sb(ctx, "r3", [P, NT * D])
        const = sb(ctx, "const", [P, C_END])
        rows = sb(ctx, "rows", [P, 3 * D])
        bank01 = ctx.enter_context(nc.psum_tensor("bank01", [P, 2, 512], FP32))
        bank = [bank01[:, 0, :], bank01[:, 1, :]] + [
            ctx.enter_context(nc.psum_tensor(f"bank{i}", [P, 512], FP32)) for i in range(2, 8)]
        ident = const[:, C_IDENT:C_IDENT + P]
        tiles = lambda r: r[:, 0:NT * D].rearrange("p (t d) -> p t d", d=D)
        X, XT_ALL, FDST = tiles(r1), tiles(r2), tiles(r3)

        unsorted = sb(ctx, "unsorted", [1, 1], I32)
        node_phase(nc, sb, sem, a, dram, X, XT_ALL, FDST, r2, unsorted, const, rows, bank, ident)
        sort_phase(nc, sb, sem, a, dram, r1, r2, unsorted, const)
        scores = r1[:, 0:ET * HEADS]
        weights = r1[:, ET * HEADS:2 * ET * HEADS]
        score_phase(nc, sb, sem, a, dram, FDST, scores, r2, const, bank, ident)
        with ExitStack() as edges:
            tables, load, convert = message_tables(sb, sem, edges, dram)
            softmax_phase(nc, sb, sem, dram, r2, r3, scores, r1, bank, ident, weights, load, convert)
            message_phase(nc, sem, dram, tables, weights, r2, r3, const, bank01)
        ffn_phase(nc, sb, sem, a, dram, out, tiles(r3), r1, r2, const, bank, ident)


def node_phase(nc, sb, sem, a, dram, X, XT_ALL, FDST, r2, unsorted, const, rows, bank, ident):
    with ExitStack() as loc:
        AHEAD = 3
        PJ = 4
        uses = lambda s: len(range(s, G, PJ))
        wcat = sb(loc, "wcat", [P, 2, 3 * D])
        stats = sb(loc, "stats", [P, G, 6])
        aggr = sb(loc, "aggr", [P, G, 2])
        mv = sb(loc, "mv", [P, NT, 2])
        rs = sb(loc, "rs", [P, 4, NT])
        xn = sb(loc, "xn", [P, G, D])
        xt = sb(loc, "xt", [P, G, D])
        dz = sb(loc, "dz", [P, G, D])
        z = sb(loc, "z", [P, G, 2, P + 1])
        small = sb(loc, "small", [P, 3, G * HEADS])
        pj = sb(loc, "pj", [P, PJ, 2 * D])
        hst = sb(loc, "hst", [P, G, D])
        sq = lambda g: FDST[:, bass.ds(g * G, G), :]
        kvw = hst[:, 0:4, :].rearrange("p a d -> p (a d)")
        kvc, cols = hst[:, 4, 0:4], hst[:, 4, 8:16]
        kv = dz[:, 0, :].rearrange("p (f q) -> p f q", f=2)
        tmp = dz[:, 1, :].rearrange("p (f q) -> p f q", f=2)
        x_loaded, stats_done = sem("x_loaded"), sem("stats_done")
        x_in, w_in, ones_set = sem("x_in"), sem("w_in"), sem("ones_set")
        dve_a, dve_b = sem("dve_a"), sem("dve_b")
        rstd_sq = sem("rstd_sq")
        var_ready = sem("var_ready")
        xn_ready, xt_in_psum, xt_ready, xt_kept = sem("xn_ready"), sem("xt_in_psum"), sem("xt_ready"), sem("xt_kept")
        dz_ready, sq_ready, ss_ready, sd_ready, z_ready = (
            sem("dz_ready"), sem("sq_ready"), sem("ss_ready"), sem("sd_ready"), sem("z_ready"))
        pj_in_psum, pj_ready, pj_stored = sem("pj_in_psum"), sem("pj_ready"), [sem(f"pj_stored{s}") for s in range(PJ)]
        gram_done, proj_done, h_ready, h_stored = sem("gram_done"), sem("proj_done"), sem("h_ready"), sem("h_stored")
        x_rows = a["x"]
        tab_rows = dram["tab"].rearrange("(t p) d -> p t d", p=P)
        h_rows = dram["h"]
        base_rows = dram["base"]
        scol = sem("scol")
        mu = lambda t: mv[:, bass.ds(t, 1), 0:1].rearrange("p a b -> p (a b)")
        col = lambda k, t: rs[:, k, bass.ds(t, 1)]
        PREP = 2 * G + 5

        lines = FDST[0:LINES, NT - 2 * G:NT - G + 1, :].rearrange("p t d -> p (t d)")
        line = lines[:, 0:LW + 2].bitcast(I32)
        falls, most = lines[:, LW + 2:2 * LW + 3], lines[:, 2 * LW + 3:2 * LW + 4]
        line_in, fall, fall_sum, tables_out, carry = (
            sem("line_in"), sem("fall"), sem("fall_sum"), sem("tables_out"), sem("carry_n"))
        assert 2 * LW + 4 <= (G + 1) * D

        heads = lambda r: r[:, :, :].rearrange("p t (h c) -> p (t h) c", c=HC)
        bc = lambda c: c.unsqueeze(2).to_broadcast([P, G * HEADS, HC])

        with nc.Block() as block:
            @block.vector
            def _(dve):
                st, sa = Steps(dve, dve_b), Steps(dve, dve_a)

                of = lambda g: bass.ds(g * G, G)
                var = aggr[:, :, 1:2].rearrange("p t o -> p (t o)")

                def moments(g):
                    sa.enter(g, PREP, 0)
                    dve.wait_ge(x_loaded, g + 1)
                    dve.sem_inc(stats_done, 1)
                    for u in range(G):
                        ins = dve.bn_stats(stats[:, u, :], X[:, bass.ds(g * G + u, 1), :].rearrange("p a d -> p (a d)"))
                        sa.done(ins) if u < G - 1 else sa.link(ins)
                    dve.sem_inc(stats_done, 1)
                    for u in range(G):
                        ins = dve.bn_aggr(aggr[:, u, :], stats[:, u, :])
                        sa.done(ins) if u < G - 1 else sa.link(ins)
                    sa.link(dve.tensor_copy(mv[:, of(g), :], aggr[:, :, :]))
                    dve.tensor_scalar(rs[:, 3, of(g)], var, LN_EPS, None, ALU.add).then_inc(var_ready, 1)

                def first_norm(g):
                    sl = of(g)
                    dve.wait_ge(rstd_sq, g * 2 + 1)
                    sa.link(dve.reciprocal(rs[:, 0, sl], rs[:, 2, sl]))
                    sa.link(dve.tensor_tensor(rs[:, 3, sl], var, rs[:, 0, sl], ALU.mult))
                    sa.link(dve.tensor_tensor(rs[:, 3, sl], rs[:, 3, sl], rs[:, 0, sl], ALU.mult))
                    dve.tensor_scalar(rs[:, 3, sl], rs[:, 3, sl], LN_EPS, None, ALU.add).then_inc(var_ready, 1)

                def second_norm(g):
                    dve.wait_ge(rstd_sq, g * 2 + 2)
                    sa.link(dve.reciprocal(rs[:, 1, of(g)], rs[:, 2, of(g)]))
                    sa.leave(0)
                    sa.base = 0

                def evac(g, us):
                    for u in us:
                        dve.wait_ge(pj_in_psum, g * G + (u + 1))
                        s = u % PJ
                        if not (isinstance(g, int) and g == 0 and u < PJ):
                            dve.wait_ge(pj_stored[s], g * (16 * uses(s)) + 16 * (u // PJ))
                        b = (bank[2], bank[3]) if u % 2 == 0 else (bank[4], bank[5])
                        dve.scalar_tensor_tensor(pj[:, s, :], b[0][:, :], col(1, g * G + u), rows[:, 0:2 * D],
                                                 ALU.mult, ALU.add).then_inc(pj_ready, 1)
                        dve.scalar_tensor_tensor(FDST[:, bass.ds(g * G + u, 1), :].rearrange("p a d -> p (a d)"),
                                                 b[1][:, 0:D], col(1, g * G + u), rows[:, 2 * D:3 * D],
                                                 ALU.mult, ALU.add).then_inc(proj_done, 1)

                def group(g, before, more=True):
                    first = isinstance(g, int) and g == 0
                    if not first:
                        dve.wait_ge(xt_in_psum, g * 4)
                        dve.wait_ge(h_ready, g)
                    for u in range(G):
                        t = g * G + u
                        dve.tensor_scalar(xn[:, u, :], X[:, bass.ds(t, 1), :].rearrange("p a d -> p (a d)"),
                                          mu(t), col(0, t), ALU.subtract, ALU.mult).then_inc(xn_ready, 1)
                    for u, part in enumerate((moments, first_norm, second_norm)):
                        before(range(u, u + 1))
                        if more:
                            part(g + 1)
                    dve.wait_ge(xn_ready, g * G + G)
                    st.link(dve.tensor_reduce(small[:, 0, :], heads(xn), AX.X, ALU.add))
                    before(range(3, 4))
                    if not first:
                        dve.wait_ge(z_ready, g)
                    dve.scalar_tensor_tensor(heads(dz), bc(small[:, 0, :]), -1.0 / HC, heads(xn),
                                             ALU.mult, ALU.add).then_inc(dz_ready, 1)
                    before(range(4, 6))
                    dve.wait_ge(sq_ready, g + 1)
                    dve.tensor_reduce(small[:, 1, :], sq(g).rearrange("p t (h c) -> p (t h) c", c=HC), AX.X, ALU.add
                                      ).then_inc(ss_ready, 1)
                    before(range(6, 7))
                    dve.wait_ge(sd_ready, g + 1)
                    st.link(dve.tensor_scalar(small[:, 2, :], small[:, 2, :], MIX_EPS, None, ALU.add))
                    st.link(dve.reciprocal(small[:, 1, :], small[:, 2, :]))
                    if not first:
                        dve.wait_ge(gram_done, g)
                    dve.wait_ge(dz_ready, g + 1)
                    zz = z[:, :, :, 0:P].rearrange("p t f (h c) -> p (t f) h c", c=HC)
                    zi = dz[:, :, :].rearrange("p t (f h c) -> p (t f) h c", f=2, c=HC)
                    zr = small[:, 1, :].rearrange("p (t h) -> p t h", h=4).unsqueeze(3).to_broadcast(
                        [P, 2 * G, 4, HC])
                    dve.tensor_tensor(zz, zi, zr, ALU.mult).then_inc(z_ready, 1)

                dve.wait_ge(line_in, 16)
                dve.tensor_tensor(falls, line[:, 0:LW + 1], line[:, 1:LW + 2], ALU.is_gt).then_inc(fall, 1)
                dve.wait_ge(fall, 1)
                dve.tensor_reduce(most, falls, AX.X, ALU.max).then_inc(fall, 1)
                for part in (moments, first_norm, second_norm):
                    part(0)
                dve.wait_ge(fall_sum, 1)
                dve.tensor_copy(unsorted[:, :], bank[5][0:1, 0:1]).then_inc(fall, 1)
                group(0, lambda us: None)
                group(1, lambda us: evac(0, us))
                with dve.Fori(2, NG - 1) as g:
                    st.enter(g, 3, 2)
                    group(g, lambda us: evac(g - 1, us))
                    st.leave(NG - 1)
                group(NG - 1, lambda us: evac(NG - 2, us), False)
                for u in range(G):
                    evac(NG - 1, [u])

            @block.scalar
            def _(act):
                def roots(g):
                    for k in range(2):
                        act.wait_ge(var_ready, g * 2 + (k + 1))
                        act.sem_inc(carry, 1)
                        act.activation(rs[:, 2, bass.ds(g * G, G)], rs[:, 3, bass.ds(g * G, G)], ACT.Sqrt
                                       ).then_inc(rstd_sq, 1)

                def group(g, more=True):
                    first = isinstance(g, int) and g == 0

                    def evac():
                        for k in range(4):
                            n = min(2, G - 2 * k)
                            act.wait_ge(xt_in_psum, g * 4 + (k + 1))
                            act.activation(xt[:, 2 * k:2 * k + n, :].rearrange("p t d -> p (t d)"),
                                           bank[k % 2][:, 0:n * D], ACT.Copy).then_inc(xt_ready, 1)
                    if first:
                        evac()
                    if more:
                        roots(g + 1)
                    act.wait_ge(dz_ready, g + 1)
                    act.activation(sq(g), dz[:, :, :], ACT.Square).then_inc(sq_ready, 1)
                    act.wait_ge(ss_ready, g + 1)
                    act.activation(small[:, 2, :], small[:, 1, :], ACT.Sqrt, scale=1.0 / (HC - 1)).then_inc(sd_ready, 1)
                    if not first:
                        act.wait_ge(pj_in_psum, g * G)
                        act.wait_ge(xt_kept, g)
                        evac()
                roots(0)
                group(0)
                with act.Fori(1, NG - 1) as g:
                    group(g)
                group(NG - 1, False)

            @block.gpsimd
            def _(pool):
                pool.memset(z[:, :, :, P:P + 1], 1.0).then_inc(ones_set, 1)

                def group(g):
                    pool.wait_ge(xn_ready, g * G + G)
                    if not isinstance(g, int):
                        pool.wait_ge(h_stored, g * 16)
                    pool.tensor_tensor(hst[:, :, :], xn[:, :, :],
                                       rs[:, 1, bass.ds(g * G, G)].unsqueeze(2).to_broadcast([P, G, D]), ALU.mult
                                       ).then_inc(h_ready, 1)
                    pool.wait_ge(xt_ready, g * 4 + 4)
                    pool.tensor_copy(XT_ALL[:, bass.ds(g * G, G), :], xt[:, :, :]).then_inc(xt_kept, 1)
                group(0)
                with pool.Fori(1, NG) as g:
                    group(g)

            @block.tensor
            def _(pe):
                pe.wait_ge(fall, 2)
                pe.wait_ge(w_in, 48)
                pe.matmul(bank[5][0:1, 0:1], most, const[0:LINES, C_ONE:C_ONE + 1], start=True, stop=True
                          ).then_inc(fall_sum, 1)
                pe.wait_ge(ones_set, 1)
                pe.wait_ge(fall, 3)

                def gram(g, start=False, stop=False):
                    pe.wait_ge(z_ready, g + 1)
                    for u in range(G):
                        for f in range(2):
                            last = pe.matmul(bank[6 + f][:, 0:P + 1], z[:, u, f, 0:P], z[:, u, f, :],
                                             start=start and u == 0, stop=stop and u == G - 1)
                    last.then_inc(gram_done, 1)

                def group(g):
                    first = isinstance(g, int) and g == 0
                    for k in range(4):
                        n = min(2, G - 2 * k)
                        pe.wait_ge(xn_ready, g * G + (2 * k + n))
                        if not (first and k < 2):
                            pe.wait_ge(xt_ready, g * 4 + (k - 1))
                        for u in range(n):
                            for f in range(2):
                                last = pe.transpose(bank[k % 2][:, (2 * u + f) * P:(2 * u + f + 1) * P],
                                                    xn[:, 2 * k + u, f * P:(f + 1) * P], ident)
                        last.then_inc(xt_in_psum, 1)
                    for u in range(G):
                        if u % 2 == 0:
                            pe.wait_ge(xt_ready, g * 4 + (u // 2 + 1))
                        if not (first and u < 2):
                            pe.wait_ge(proj_done, g * G + reuse(u, 2))
                        b = (bank[2], bank[3]) if u % 2 == 0 else (bank[4], bank[5])
                        for f in range(2):
                            w = xt[:, u, f * P:(f + 1) * P]
                            pe.matmul(b[0][:, :], w, wcat[:, f, 0:2 * D], start=f == 0, stop=f == 1)
                            last = pe.matmul(b[1][:, 0:D], w, wcat[:, f, 2 * D:3 * D], start=f == 0, stop=f == 1)
                        last.then_inc(pj_in_psum, 1)

                group(0)
                gram(0, start=True)
                with pe.Fori(1, NG - 1) as g:
                    group(g)
                    gram(g)
                group(NG - 1)
                gram(NG - 1, stop=True)

            @block.sync
            def _(sp):
                def load(g):
                    sp.dma_start(X[:, bass.ds(g * G, G), :], x_rows[:, bass.ds(g * G, G), :]).then_inc(x_in, 16)

                def loaded(g):
                    sp.wait_ge(x_in, g * 16 + 16)
                    sp.sem_inc(x_loaded, 1)
                load(0)
                sp.dma_start(line[:, :], a["dst_line"]).then_inc(line_in, 16)
                sp.dma_start(const[:, :], a["const"]).then_inc(w_in, 16)
                sp.dma_start(rows[:, :], a["proj_bias"].partition_broadcast(P)).then_inc(w_in, 16)
                sp.dma_start(wcat[:, :, :], a["wcat"]).then_inc(w_in, 16)
                for g in range(AHEAD - 1):
                    loaded(g)
                    load(g + 1)

                def store(g):
                    sp.wait_ge(h_ready, g + 1)
                    sp.dma_start(h_rows[:, bass.ds(g * G, G), :], hst[:, :, :]).then_inc(h_stored, 16)
                    for u in range(G):
                        s = u % PJ
                        sp.wait_ge(pj_ready, g * G + (u + 1))
                        sp.dma_start(tab_rows[:, bass.ds(g * G + u, 1), :].rearrange("p a d -> p (a d)"),
                                     pj[:, s, :]).then_inc(pj_stored[s], 16)
                for name in TABLES:
                    sp.dma_start(dram["t_" + name], a[name]).then_inc(tables_out, 16)
                with sp.Fori(0, NG - AHEAD) as g:
                    loaded(g + (AHEAD - 1))
                    load(g + AHEAD)
                    store(g)
                for g in range(NG - AHEAD, NG):
                    if g == NG - AHEAD:
                        loaded(NG - 1)
                    store(g)
                sp.wait_ge(tables_out, 16 * len(TABLES))
                sp.wait_ge(h_stored, NG * 16)
                for s in range(PJ):
                    sp.wait_ge(pj_stored[s], NG * 16 * uses(s))

        dve_k, kv_ready, row_in_psum, kvin = sem("dve_k"), sem("kv_ready"), sem("row_in_psum"), sem("kvin")
        xt_again, mix_in_psum, base_ready, base_stored = (
            sem("xt_again"), sem("mix_in_psum"), sem("base_ready"), sem("base_stored"))
        z_flat = z[:, :, :, :].rearrange("p t f q -> p (t f q)")
        xts = (xt[:, :, :], z_flat[:, 0:G * D].rearrange("p (t d) -> p t d", d=D))
        assert NG % 2 == 1

        with nc.Block() as block:
            @block.sync
            def _(sp):
                sp.dma_start(kvw[:, :], a["mix_rows"].partition_broadcast(P)).then_inc(kvin, 16)
                sp.dma_start(kvc[:, :], a["mix_cols"]).then_inc(kvin, 16)
                with sp.Fori(0, NG) as g:
                    sp.wait_ge(base_ready, g * G + G)
                    sp.dma_start(base_rows[:, bass.ds(g * G, G), :], X[:, bass.ds(g * G, G), :]
                                 ).then_inc(base_stored, 16)
                sp.wait_ge(base_stored, NG * 16)

            @block.vector
            def _(dve):
                st = Steps(dve, dve_k)
                dve.wait_ge(kvin, 32)
                for f in range(2):
                    st.link(dve.tensor_copy(cols[:, f:f + 1], bank[6 + f][:, P:P + 1]))
                    dve.tensor_copy(tmp[:, f, :], cols[:, f:f + 1].to_broadcast([P, P])).then_inc(scol, 1)
                for f in range(2):
                    wk, bk = kvc[:, f:f + 1], kvc[:, 2 + f:3 + f]
                    wv = kvw[:, 2 * D + f * P:2 * D + (f + 1) * P]
                    bv = kvw[:, 3 * D + f * P:3 * D + (f + 1) * P]
                    o = kv[:, f, :]
                    dve.wait_ge(row_in_psum, f + 1)
                    st.link(dve.tensor_scalar(o, bank[6 + f][:, 0:P], wk, None, ALU.mult))
                    st.link(dve.scalar_tensor_tensor(o, bank[f][:, 0:P], bk, o, ALU.mult, ALU.add))
                    st.link(dve.tensor_tensor(o, o, wv, ALU.mult))
                    st.link(dve.tensor_tensor(cols[:, 2:3], cols[:, f:f + 1], wk, ALU.mult))
                    st.link(dve.scalar_tensor_tensor(cols[:, 3:4], bk, float(N_NODES), cols[:, 2:3], ALU.mult, ALU.add))
                    st.link(dve.scalar_tensor_tensor(o, bv, cols[:, 3:4], o, ALU.mult, ALU.add))
                    st.link(dve.scalar_tensor_tensor(o, o, 1.0 / N_NODES, const[:, C_BLOCK:C_BLOCK + P],
                                                     ALU.mult, ALU.mult))
                    dve.tensor_tensor(o, o, ident, ALU.add).then_inc(kv_ready, 1)

                with dve.Fori(0, NG) as g:
                    for u in range(G):
                        dve.wait_ge(mix_in_psum, g * G + (u + 1))
                        x = X[:, bass.ds(g * G + u, 1), :].rearrange("p a d -> p (a d)")
                        dve.tensor_tensor(x, bank[2 + u % 4][:, 0:D], x, ALU.add).then_inc(base_ready, 1)

            @block.scalar
            def _(act):
                def put(g, k):
                    act.activation(xts[k], XT_ALL[:, bass.ds(g * G, G), :], ACT.Copy).then_inc(xt_again, 1)
                put(0, 0)
                put(1, 1)
                with act.Fori(1, NG // 2) as j:
                    act.wait_ge(mix_in_psum, j * (2 * G) - G)
                    put(j * 2, 0)
                    act.wait_ge(mix_in_psum, j * (2 * G))
                    put(j * 2 + 1, 1)
                act.wait_ge(mix_in_psum, (NG - 2) * G)
                put(NG - 1, 0)

            @block.tensor
            def _(pe):
                for f in range(2):
                    pe.wait_ge(scol, f + 1)
                    pe.matmul(bank[f][:, 0:P], tmp[:, f, :], ident, start=True, stop=True).then_inc(row_in_psum, 1)
                pe.wait_ge(kv_ready, 2)

                def group(g, k, first=False):
                    pe.wait_ge(xt_again, g + 1)
                    for u in range(G):
                        if not (first and u < 4):
                            pe.wait_ge(base_ready, g * G + reuse(u, 4))
                        for f in range(2):
                            last = pe.matmul(bank[2 + u % 4][:, f * P:(f + 1) * P], xts[k][:, u, f * P:(f + 1) * P],
                                             kv[:, f, :], start=True, stop=True)
                        last.then_inc(mix_in_psum, 1)
                group(0, 0, True)
                with pe.Fori(0, NG // 2) as j:
                    group(j * 2 + 1, 1)
                    group(j * 2 + 2, 0)


def pair_loop(eng, cur, prev, last, first_pair, extra_pair, second_pair=None):
    d0 = eng.snap(cur, min_val=0, max_val=NT - 1)
    first_pair(d0)
    with eng.If(last > d0):
        if second_pair:
            second_pair(d0 + 1)
            with eng.If(last > d0 + 1):
                with eng.Fori(d0 + 2, last + 1) as d:
                    extra_pair(d)
                eng.nop()
        else:
            with eng.Fori(d0 + 1, last + 1) as d:
                extra_pair(d)
        eng.nop()
    eng.nop()
    for older, newer in zip(prev[::-1], (prev[-2::-1] if prev else []) + [cur]):
        eng.reg_mov(older, newer)
    eng.reg_mov(cur, last)


def sort_phase(nc, sb, sem, a, dram, r1, r2, unsorted, const):
    with ExitStack() as loc:
        dst = sb(loc, "so_dst", [P, ET], I32)
        src = sb(loc, "so_src", [P, ET], I32)
        dstf = sb(loc, "so_dstf", [P, ET])
        own = sb(loc, "so_own", [P, ET])
        part = sb(loc, "so_part", [P, ET])
        rank = sb(loc, "so_rank", [P, ET])
        edge = sb(loc, "so_edge", [P, 2], I32)
        place = sb(loc, "so_place", [P, 1], I32)
        chunk, key = r2[:, 0:CE].bitcast(I32), r2[:, CE:2 * CE]
        work, number = r1[:, 0:CE], r1[:, CE:2 * CE]
        cols_in, chunk_in, key_set, prepared = sem("so_in"), sem("so_chunk"), sem("so_key"), sem("so_prepared")
        s1, s2, s3, s4 = sem("so_s1"), sem("so_s2"), sem("so_s3"), sem("so_s4")
        own_set, rank_set, carry = sem("so_own_set"), sem("so_rank_set"), sem("so_carry")
        assert BLOCKS <= NT

        with nc.Block() as block:
            @block.sync
            def _(sp):
                with sp.If(sp.value_load(unsorted[0:1, 0:1], min_val=0, max_val=LINES) > 0):
                    sp.dma_start(dst[:, :], a["dst_t"]).then_inc(cols_in, 16)
                    sp.dma_start(src[:, :], a["src_t"]).then_inc(cols_in, 16)
                    sp.dma_start(number, a["count_row"].partition_broadcast(P)).then_inc(cols_in, 16)

                    def load(c):
                        sp.dma_start(chunk, a["dst_chunks"][bass.ds(c, 1), 1:1 + CE].rearrange("a e -> (a e)"
                                     ).partition_broadcast(P)).then_inc(chunk_in, 16)
                    load(0)
                    with sp.Fori(1, CHUNKS) as c:
                        sp.wait_ge(key_set, c)
                        sp.sem_inc(carry, 1)
                        load(c)

            @block.vector
            def _(dve):
                with dve.If(dve.value_load(unsorted[0:1, 0:1], min_val=0, max_val=LINES) > 0):
                    dve.wait_ge(cols_in, 48)
                    for c in range(CHUNKS):
                        dve.tensor_scalar(own[:, c * BLOCKS:(c + 1) * BLOCKS], const[:, C_NODE:C_NODE + BLOCKS],
                                          float(c * CE), None, ALU.add)
                    dve.tensor_copy(dstf[:, :], dst[:, :])
                    dve.memset(rank[:, :], 0.0).then_inc(prepared, 1)
                    dve.wait_ge(prepared, 1)
                    with dve.Fori(0, CHUNKS) as c:
                        dve.wait_ge(chunk_in, c * 16 + 16)
                        dve.tensor_copy(key, chunk).then_inc(key_set, 1)
                        dve.wait_ge(key_set, c + 1)
                        dve.sem_inc(carry, 1)
                        with dve.Fori(0, ET) as t:
                            n = c * ET + t
                            dve.tensor_scalar(work, key, dstf[:, bass.ds(t, 1)], float(EP), ALU.subtract, ALU.mult
                                              ).then_inc(s1, 1)
                            dve.wait_ge(s1, n + 1)
                            dve.scalar_tensor_tensor(work, work, own[:, bass.ds(t, 1)], number, ALU.subtract, ALU.add
                                                     ).then_inc(s2, 1)
                            dve.wait_ge(s2, n + 1)
                            dve.tensor_scalar(work, work, 0.0, None, ALU.is_lt).then_inc(s3, 1)
                            dve.wait_ge(s3, n + 1)
                            dve.tensor_reduce(part[:, bass.ds(t, 1)], work, AX.X, ALU.add).then_inc(s4, 1)
                            dve.wait_ge(s4, n + 1)
                        dve.tensor_scalar(own[:, :], own[:, :], -float(CE), None, ALU.add).then_inc(own_set, 1)
                        dve.tensor_tensor(rank[:, :], rank[:, :], part[:, :], ALU.add).then_inc(rank_set, 1)
                        dve.wait_ge(own_set, c + 1)
                        dve.wait_ge(rank_set, c + 1)

        place_set, moved = sem("so_place_set"), sem("so_moved")
        with nc.Block() as block:
            @block.gpsimd
            def _(pool):
                with pool.If(pool.value_load(unsorted[0:1, 0:1], min_val=0, max_val=LINES) > 0):
                    def move(t):
                        if not isinstance(t, int):
                            pool.wait_ge(moved, t * 16)
                        pool.tensor_copy(place[:, :], rank[:, bass.ds(t, 1)]).then_inc(place_set, 1)
                        pool.tensor_copy(edge[:, 0:1], src[:, bass.ds(t, 1)]).then_inc(place_set, 1)
                        pool.tensor_copy(edge[:, 1:2], dst[:, bass.ds(t, 1)]).then_inc(place_set, 1)
                        pool.wait_ge(place_set, t * 3 + 3)
                        pool.sem_inc(carry, 1)
                        pool.indirect_dma_start(dram["edges"],
                                                bass.IndirectOffsetOnAxis(ap=place[:, :].bitcast(U32), axis=0),
                                                edge[:, :], None).then_inc(moved, 16)
                    move(0)
                    with pool.Fori(1, ET) as t:
                        move(t)
                    pool.wait_ge(moved, ET * 16)

        made = sem("so_made")
        with nc.Block() as block:
            @block.sync
            def _(sp):
                with sp.If(sp.value_load(unsorted[0:1, 0:1], min_val=0, max_val=LINES) > 0):
                    srcs, dsts = dram["edges"][:, 0:1], dram["edges"][:, 1:2]
                    with sp.Fori(0, ET) as t:
                        sp.dma_start(dram["t_src_t"][:, bass.ds(t, 1)], srcs[bass.ds(t * P, P), :],
                                     allow_slow_non_contiguous=True).then_inc(made, 16)
                        sp.dma_start(dram["t_dst_t"][:, bass.ds(t, 1)], dsts[bass.ds(t * P, P), :],
                                     allow_slow_non_contiguous=True).then_inc(made, 16)
                        sp.wait_ge(made, t * 32 + 32)
                        sp.sem_inc(carry, 1)
                    for name, n, w in (("t_dst_line", LINES, LW), ("t_dst_chunks", CHUNKS, CE)):
                        for q in range(n):
                            lo, hi = max(q * w - 1, 0), min((q + 1) * w + 1, EP)
                            at = lo - (q * w - 1)
                            sp.dma_start(dram[name][q:q + 1, at:at + hi - lo].rearrange("a e -> e a"),
                                         dsts[lo:hi, :],
                                     allow_slow_non_contiguous=True).then_inc(made, 16)
                    sp.dma_start(dram["t_dst_last"].rearrange("a s -> s a"),
                                 dram["edges"].rearrange("(s w) c -> s (w c)", w=H * P)[:, 2 * H * P - 1:2 * H * P],
                                     allow_slow_non_contiguous=True).then_inc(made, 16)
                    sp.wait_ge(made, ET * 32 + (LINES + CHUNKS + 1) * 16)


def score_phase(nc, sb, sem, a, dram, FDST, scores, r2, const, bank, ident):
    with ExitStack() as loc:
        src = sb(loc, "src", [P, ET], I32)
        dlast = sb(loc, "dlast", [1, ET // H], I32)
        dline = sb(loc, "dline", [LINES, LW], I32)
        dline16 = sb(loc, "dline16", [LINES, LW], I16)
        idx = sb(loc, "idx", [P, U], I32)
        gath = r2[:, 0:U * 2 * D].rearrange("p (u d) -> p u d", d=2 * D)
        dstb = sb(loc, "dstb", [P, Q, H * P], I16)
        oht = sb(loc, "oht", [P, 2, 2, H * P])
        sil = sb(loc, "sil", [P, 4, 2 * D])
        attn = sb(loc, "attn", [P, 2 * D])
        mark = sb(loc, "mark", [P, 1])
        mul_done = sem("mul_done")
        slot_free = sem("slot_free")
        in_s, d16, d16_out, dl = sem("in_s"), sem("d16"), sem("d16_out"), sem("dl")
        idx_set = sem("idx_set")
        g_in = [sem(f"g_in{q}") for q in range(Q)]
        fv_out = [sem(f"fv_out{q}") for q in range(Q)]
        dstb_in = [sem(f"dstb_in{q}") for q in range(Q)]
        oht_ready, oht_used, z_done, sil_done, score_done, prod_done = (
            sem("oht_ready"), sem("oht_used"), sem("z_done"), sem("sil_done"), sem("score_done"), sem("prod_done"))
        fv_of = lambda s: dram["fv"][bass.ds(s, 1)].rearrange("a p k d -> p (a k) d")
        halves = dram["tab"].rearrange("n (o d) -> (n o) d", o=2)
        AHEAD = 3
        d16_line = dram["d16"].rearrange("(q w) -> q w", w=LW)

        with nc.Block() as block:
            @block.sync
            def _(sp):
                sp.dma_start(src[:, :], dram["t_src_t"]).then_inc(in_s, 16)
                sp.dma_start(dline[:, :], dram["t_dst_line"][:, 1:1 + LW]).then_inc(in_s, 16)
                sp.dma_start(dlast[0:1, :], dram["t_dst_last"]).then_inc(in_s, 16)
                sp.dma_start(attn[:, 0:D], a["attn"].partition_broadcast(P)).then_inc(in_s, 16)
                sp.dma_start(attn[:, D:2 * D], a["attn"].partition_broadcast(P)).then_inc(in_s, 16)
                sp.wait_ge(d16, 1)
                sp.dma_start(d16_line, dline16[:, :]).then_inc(d16_out, 16)
                sp.wait_ge(d16_out, 16)

            @block.vector
            def _(dve):
                dve.wait_ge(in_s, 80)
                dve.tensor_copy(dline16[:, :], dline[:, :]).then_inc(d16, 1)
                odd = src[:, :].rearrange("p (t o) -> p t o", o=2)[:, :, 1:2]
                dve.tensor_scalar(odd, odd, 2, None, ALU.mult)
                dve.tensor_scalar(dlast[0:1, :], dlast[0:1, :], 7, None, ALU.arith_shift_right).then_inc(dl, 1)

        def dtile(eng, s):
            return eng.value_load(dlast[0:1, bass.ds(s, 1)], min_val=0, max_val=NT - 1)

        with nc.Block() as block:
            @block.gpsimd
            def _(pool):
                def rnd(i):
                    first = isinstance(i, int)
                    for u in range(U):
                        if u % H == 0:
                            pool.wait_ge(idx_set, i * Q + (u // H + 1))
                            pool.sem_inc(slot_free, 1)
                        if not first:
                            pool.wait_ge(z_done, i * U + (u - U + 1))
                            if u % 2 == 0:
                                pool.wait_ge(fv_out[u // H], i * 16)
                            pool.sem_inc(slot_free, 1)
                        table, width = (halves, D) if u % 2 else (dram["tab"], 2 * D)
                        pool.indirect_dma_start(gath[:, u, 0:width], None, table,
                                                bass.IndirectOffsetOnAxis(ap=idx[:, u:u + 1].bitcast(U32), axis=0)
                                                ).then_inc(g_in[u // H], 16)
                rnd(0)
                with pool.Fori(1, ROUNDS) as i:
                    rnd(i)

            @block.sync
            def _(sp):
                def destinations(s, slot, first):
                    if not first:
                        sp.wait_ge(prod_done, s + (1 - Q))
                    sp.dma_start(dstb[:, slot, :], dram["d16"][bass.ds(s * (H * P), H * P)].partition_broadcast(P)
                                 ).then_inc(dstb_in[slot], 16)
                for s in range(AHEAD):
                    destinations(s, s, True)

                def rnd(i, more=True):
                    for q in range(Q):
                        if more or q + AHEAD < Q:
                            destinations(i * Q + (q + AHEAD), (q + AHEAD) % Q,
                                         isinstance(i, int) and i == 0 and q + AHEAD < Q)
                        sp.wait_ge(g_in[q], i * (16 * H) + 16 * H)
                        sp.dma_start(fv_of(i * Q + q),
                                     gath[:, q * H:(q + 1) * H:2, D:2 * D]).then_inc(fv_out[q], 16)
                rnd(0)
                with sp.Fori(1, ROUNDS - 1) as i:
                    rnd(i)
                rnd(ROUNDS - 1, False)
                for q in range(Q):
                    sp.wait_ge(fv_out[q], ROUNDS * 16)

            @block.vector
            def _(dve):
                cur, prev = dve.alloc_register("cur_s1v"), dve.alloc_register("prev_s1v")
                dve.reg_mov(cur, 0)
                dve.reg_mov(prev, 0)

                def one_hot(q, k, d):
                    return dve.tensor_scalar(oht[:, q % 2, k, :], dstb[:, q, :],
                                             const[:, bass.ds(d + C_NODE, 1)], None, ALU.is_equal)

                def onehots(i, q, first):
                    s, hf = i * Q + q, q % 2
                    last = dtile(dve, s)
                    dve.wait_ge(dstb_in[q], i * 16 + 16)

                    def first_pair(d):
                        if not first:
                            dve.wait_ge(oht_used, dve.snap(prev, min_val=0, max_val=NT - 1) + (s - 1))
                        one_hot(q, 0, d).then_inc(oht_ready, 1)

                    def extra_pair(d):
                        dve.wait_ge(oht_used, d + s)
                        one_hot(q, 1, d).then_inc(oht_ready, 1)
                    pair_loop(dve, cur, [prev], last, first_pair, extra_pair,
                              lambda d: one_hot(q, 1, d).then_inc(oht_ready, 1))

                def times_attn(s, hf):
                    dve.wait_ge(sil_done, s * 2 + 2)
                    v = sil[:, 2 * hf:2 * hf + 2, :]
                    dve.tensor_tensor(v, v, attn[:, :].unsqueeze(1).to_broadcast([P, 2, 2 * D]), ALU.mult
                                      ).then_inc(mul_done, 1)

                def head_sums(s, hf):
                    dve.wait_ge(mul_done, s + 1)
                    dve.tensor_reduce(scores[:, bass.ds(s * (H * HEADS), H * HEADS)],
                                      sil[:, 2 * hf:2 * hf + 2, :].rearrange("p k (q c) -> p (k q) c", c=HC),
                                      AX.X, ALU.add).then_inc(score_done, 1)

                def rnd(i):
                    for q in range(Q):
                        late = not isinstance(i, int) or q >= 2
                        if late:
                            times_attn(i * Q + (q - 2), q % 2)
                        onehots(i, q, not late)
                        if q or not isinstance(i, int):
                            dve.wait_ge(prod_done, i * Q + q)
                        dve.tensor_copy(mark[:, :], ident[:, 0:1]).then_inc(prod_done, 1)
                        if late:
                            head_sums(i * Q + (q - 2), q % 2)
                rnd(0)
                with dve.Fori(1, ROUNDS) as i:
                    rnd(i)
                for s in (ROUNDS * Q - 2, ROUNDS * Q - 1):
                    times_attn(s, s % 2)
                    head_sums(s, s % 2)

            @block.tensor
            def _(pe):
                cur = pe.alloc_register("cur_s1p")
                pe.reg_mov(cur, 0)
                dest = lambda u: bank[u // 2 % 4][:, (u % 2) * D:(u % 2 + 1) * D]

                def rnd(i):
                    first = isinstance(i, int)
                    for q in range(Q):
                        s, hf = i * Q + q, q % 2
                        last = dtile(pe, s)
                        us = range(q * H, q * H + H)
                        if q >= 2 or not first:
                            pe.wait_ge(sil_done, i * K + (2 * q - 2))

                        def pair(d, start, k):
                            pe.wait_ge(oht_ready, d + (s + 1))
                            for u in us:
                                ins = pe.matmul(dest(u), oht[:, hf, k, (u % H) * P:(u % H + 1) * P],
                                                FDST[:, bass.ds(d, 1), :].rearrange("p a d -> p (a d)"),
                                                start=start and u % 2 == 0, stop=False, skip_group_check=True)
                            ins.then_inc(oht_used, 1)
                        pair_loop(pe, cur, [], last, lambda d: pair(d, True, 0), lambda d: pair(d, False, 1))
                        pe.wait_ge(g_in[q], i * (16 * H) + 16 * H)
                        for u in us:
                            pe.matmul(dest(u), ident, gath[:, u, 0:D], start=False, stop=True,
                                      skip_group_check=True).then_inc(z_done, 1)
                rnd(0)
                with pe.Fori(1, ROUNDS) as i:
                    rnd(i)

            @block.scalar
            def _(act):
                def indices(i, q):
                    act.activation(idx[:, q * H:(q + 1) * H], src[:, bass.ds(i * U + q * H, H)], ACT.Copy
                                   ).then_inc(idx_set, 1)
                for q in range(Q):
                    indices(0, q)

                def rnd(i, more=True):
                    for k in range(K):
                        act.wait_ge(z_done, i * U + (2 * k + 2))
                        if k >= 4 or not (isinstance(i, int) and i == 0):
                            act.wait_ge(score_done, i * Q + (k // 2 - 1))
                        act.activation(sil[:, k % 4, :], bank[k % 4][:, :], ACT.Silu).then_inc(sil_done, 1)
                        if more and k % (H // 2) == H // 2 - 1:
                            indices(i + 1, k // (H // 2))
                rnd(0)
                with act.Fori(1, ROUNDS - 1) as i:
                    rnd(i)
                rnd(ROUNDS - 1, False)


def softmax_phase(nc, sb, sem, dram, r2, r3, scores, r1, bank, ident, weights, load, convert):
    with ExitStack() as loc:
        stage = sb(loc, "stage", [P, G, P])
        stage2 = sb(loc, "stage2", [P, G, P])
        line = sb(loc, "line", [1, 4 * P])
        colv = sb(loc, "colv", [P, 8])
        dst_c = r1[:, ET * HEADS:ET * HEADS + CE + 2].bitcast(I32)
        brk = r2[:, 0:CE + 1]
        sc = r3[:, 0:CE]
        run = r2[:, CE + 1:2 * CE + 1]
        top = r3[:, CE:2 * CE]
        brow = sb(loc, "brow", [1, P])
        in_c, dvs, staged, tin, tout = sem("in_c"), sem("dvs"), sem("staged"), sem("tin"), sem("tout")
        lt, lf = sem("lt"), sem("lf")
        sc4 = scores.rearrange("p (j b h) -> p b h j", b=BLOCKS, h=HEADS)
        w4 = weights.rearrange("p (j b h) -> p b h j", b=BLOCKS, h=HEADS)

        with nc.Block() as block:
            @block.sync
            def _(sp):
                for h in range(HEADS):
                    sp.dma_start(dst_c[h * CHUNKS:(h + 1) * CHUNKS, :], dram["t_dst_chunks"]).then_inc(in_c, 16)

            @block.scalar
            def _(act):
                def group(g):
                    for u in range(G):
                        if not isinstance(g, int) and u % 4 == 0:
                            act.wait_ge(tin, g * 2 + (u // 4 - 1))
                        act.activation(stage[:, u, :].rearrange("p (h j) -> p h j", h=HEADS),
                                       sc4[:, bass.ds(g * G + u, 1), :, :].rearrange("p a h j -> p (a h) j"),
                                       ACT.Copy).then_inc(staged, 1)
                group(0)
                with act.Fori(1, NG) as g:
                    group(g)

            @block.tensor
            def _(pe):
                def group(g):
                    for k in range(2):
                        if not isinstance(g, int):
                            pe.wait_ge(tout, g * 2 + (k - 1))
                        n = 4 - k
                        pe.wait_ge(staged, g * G + (4 * k + n))
                        for u in range(n):
                            last = pe.transpose(bank[k][:, u * P:(u + 1) * P], stage[:, 4 * k + u, :], ident)
                        last.then_inc(tin, 1)
                group(0)
                with pe.Fori(1, NG) as g:
                    group(g)
                for r in range(2):
                    pe.wait_ge(lt, 2 * r + 1)
                    for k in range(2):
                        last = pe.transpose(bank[2][0:1, k * P:(k + 1) * P], colv[:, k:k + 1], ident)
                    last.then_inc(lf, 1)
                    pe.wait_ge(lt, 2 * r + 2)
                    pe.matmul(bank[3][:, 0:1], brow[0:1, :], ident[0:1, 0:1], start=True, stop=True).then_inc(lf, 1)

            @block.vector
            def _(dve):
                st = Steps(dve, dvs)
                with dve.Fori(0, NG) as g:
                    for k in range(2):
                        n = 4 - k
                        dve.wait_ge(tin, g * 2 + (k + 1))
                        dve.tensor_copy(sc[:, bass.ds((g * G + 4 * k) * P, n * P)], bank[k][:, 0:n * P]
                                        ).then_inc(tout, 1)
                dve.wait_ge(in_c, HEADS * 16)
                st.link(dve.tensor_tensor(brk, dst_c[:, 0:CE + 1], dst_c[:, 1:CE + 2], ALU.not_equal))
                st.link(dve.tensor_scalar(brk, brk, -FAR, None, ALU.mult))
                st.link(dve.tensor_tensor(colv[:, 2:3], dst_c[:, 1:2], dst_c[:, CE:CE + 1], ALU.not_equal))
                st.link(dve.tensor_scalar(colv[:, 2:3], colv[:, 2:3], -FAR, None, ALU.mult))
                dve.wait_ge(tout, NG * 2)

                def scan(dst, rev, init):
                    if rev:
                        return dve.tensor_tensor_scan(dst[:, ::-1], brk[:, CE:0:-1], run[:, ::-1], init,
                                                      ALU.add, ALU.max)
                    return dve.tensor_tensor_scan(dst, brk[:, 0:CE], sc, init, ALU.add, ALU.max)

                for r in range(2):
                    dst = top if r else run
                    st.link(scan(dst, r, -FAR))
                    st.link(dve.tensor_copy(colv[:, 0:1], dst[:, 0:1] if r else dst[:, CE - 1:CE]))
                    edge = brk[:, CE:CE + 1] if r else brk[:, 0:1]
                    dve.tensor_tensor(colv[:, 1:2], edge, colv[:, 2:3], ALU.add).then_inc(lt, 1)
                    dve.wait_ge(lf, 2 * r + 1)
                    st.link(dve.tensor_copy(line[:, 0:2 * P], bank[2][0:1, 0:2 * P]))
                    if r:
                        st.link(dve.tensor_tensor_scan(line[:, 3 * P - 1:2 * P - 1:-1], line[:, 2 * P - 1:P - 1:-1],
                                                       line[:, P - 1::-1], -FAR, ALU.add, ALU.max))
                    else:
                        st.link(dve.tensor_tensor_scan(line[:, 2 * P:3 * P], line[:, P:2 * P], line[:, 0:P],
                                                       -FAR, ALU.add, ALU.max))
                    st.link(dve.memset(brow[:, :], -FAR))
                    hj = lambda v: v.rearrange("p (h j) -> p h j", j=CHUNKS)
                    to, of = (slice(0, CHUNKS - 1), slice(1, CHUNKS)) if r else (slice(1, CHUNKS), slice(0, CHUNKS - 1))
                    dve.tensor_copy(hj(brow[:, :])[:, :, to], hj(line[:, 2 * P:3 * P])[:, :, of]).then_inc(lt, 1)
                    dve.wait_ge(lf, 2 * r + 2)
                    st.link(dve.tensor_copy(colv[:, 3 + r:4 + r], bank[3][:, 0:1]))
                    st.link(scan(dst, r, colv[:, 3 + r:4 + r]))

        sub, ex, wps, wev = sem("sub"), sem("ex"), sem("wps"), sem("wev")
        with nc.Block() as block:
            @block.sync
            def _(sp):
                load(sp)

            @block.vector
            def _(dve):
                def differences(g, first=False):
                    if not first:
                        dve.wait_ge(ex, g)
                    sl = bass.ds(g * G * P, G * P)
                    dve.tensor_tensor(stage[:, :, :].rearrange("p u q -> p (u q)"), sc[:, sl], top[:, sl],
                                      ALU.subtract).then_inc(sub, 1)

                def back(g):
                    for k in range(2):
                        n = 4 - k
                        dve.wait_ge(wps, g * 2 + (k + 1))
                        for u in range(n):
                            ins = dve.tensor_copy(
                                w4[:, bass.ds(g * G + 4 * k + u, 1), :, :].rearrange("p a h j -> p (a h) j"),
                                bank[k][:, u * P:(u + 1) * P].rearrange("p (h j) -> p h j", h=HEADS))
                        ins.then_inc(wev, 1)
                differences(0, True)
                with dve.Fori(0, NG - 1) as g:
                    differences(g + 1)
                    back(g)
                convert(dve)
                back(NG - 1)

            @block.scalar
            def _(act):
                def group(g):
                    act.wait_ge(sub, g + 1)
                    if not isinstance(g, int):
                        act.wait_ge(wps, g * 2)
                    act.activation(stage2[:, :, :], stage[:, :, :], ACT.Exp).then_inc(ex, 1)
                group(0)
                with act.Fori(1, NG) as g:
                    group(g)

            @block.tensor
            def _(pe):
                def group(g):
                    pe.wait_ge(ex, g + 1)
                    for k in range(2):
                        if not isinstance(g, int):
                            pe.wait_ge(wev, g * 2 + (k - 1))
                        for u in range(4 - k):
                            last = pe.transpose(bank[k][:, u * P:(u + 1) * P], stage2[:, 4 * k + u, :], ident)
                        last.then_inc(wps, 1)
                group(0)
                with pe.Fori(1, NG) as g:
                    group(g)


def message_tables(sb, sem, stack, dram):
    dlast = sb(stack, "dlast2", [1, ET // H], I32)
    dst = sb(stack, "dst2", [P, ET], I32)
    src = sb(stack, "src2", [P, ET // 2, 2], I32)
    dstf = sb(stack, "dstf", [P, ET])
    zero = sb(stack, "zero", [P, MSG])
    idx = sb(stack, "idx2", [P, Q, H // 2, 1], I32)
    in_m, dl2 = sem("in_m"), sem("dl2")

    def load(sp):
        sp.dma_start(dst[:, :], dram["t_dst_t"]).then_inc(in_m, 16)
        sp.dma_start(src[:, :, :], dram["t_src_t"].rearrange("p (t o) -> p t o", o=2)).then_inc(in_m, 16)
        sp.dma_start(dlast[:, :], dram["t_dst_last"]).then_inc(in_m, 16)

    def convert(dve):
        dve.wait_ge(in_m, 48)
        dve.tensor_copy(dstf[:, :], dst[:, :])
        dve.tensor_scalar(src[:, :, :], src[:, :, :], 2, 1, ALU.mult, ALU.add)
        dve.memset(zero[:, :], 0.0)
        dve.tensor_scalar(dlast[:, :], dlast[:, :], 7, None, ALU.arith_shift_right).then_inc(dl2, 1)
    return (dlast, dstf, src, zero, idx), load, convert


def message_phase(nc, sem, dram, tables, weights, r2, r3, const, bank01):
    dlast, dstf, src, zero, idx = tables
    fv = r3[:, 0:U * D].rearrange("p (u d) -> p u d", d=D)
    msg = r3[:, U * D:U * (D + MSG)].rearrange("p (u m) -> p u m", m=MSG)
    oh = r3[:, U * (D + MSG):U * (D + MSG) + 2 * U * P].rearrange("p (q k u n) -> p q k u n", k=2, u=H, n=P)
    acc = r2[:, :].rearrange("p (t m) -> p t m", m=MSG)
    fv_in = [sem(f"fv_in{q}") for q in range(Q)]
    halves = dram["tab"].rearrange("n (o d) -> (n o) d", o=2)
    idx_set, slot_free = sem("idx_set2"), sem("slot_free2")
    fv_gathered = [sem(f"fv_gathered{q}") for q in range(Q)]
    msg_ready, oh_ready, oh_used, flushed, wcol = (
        sem("msg_ready"), sem("oh_ready"), sem("oh_used"), sem("flushed"), sem("wcol"))
    fv_of = lambda s: dram["fv"][bass.ds(s, 1)].rearrange("a p k d -> p (a k) d")
    iota = const[:, C_IOTA:C_IOTA + P]
    sums = lambda d: bank01[:, bass.ds(d % 2, 1), 0:MSG].rearrange("p a m -> p (a m)")

    def dtile(eng, s):
        return eng.value_load(dlast[0:1, bass.ds(s, 1)], min_val=0, max_val=NT - 1)

    with nc.Block() as block:
        @block.sync
        def _(sp):
            def rnd(i):
                for q in range(Q):
                    if not isinstance(i, int):
                        sp.wait_ge(msg_ready, i * Q + (q + 1 - Q))
                    sp.dma_start(fv[:, q * H:q * H + H:2, :],
                                 fv_of(i * Q + q)).then_inc(fv_in[q], 16)
            rnd(0)
            with sp.Fori(1, ROUNDS) as i:
                rnd(i)

        @block.gpsimd
        def _(pool):
            with pool.Fori(0, ROUNDS) as i:
                for q in range(Q):
                    pool.wait_ge(idx_set, i * Q + (q + 1))
                    pool.sem_inc(slot_free, 1)
                    for k in range(H // 2):
                        pool.indirect_dma_start(
                            fv[:, q * H + 2 * k + 1, :], None, halves,
                            bass.IndirectOffsetOnAxis(ap=idx[:, q, k, :].bitcast(U32), axis=0)
                            ).then_inc(fv_gathered[q], 16)

        @block.scalar
        def _(act):
            cur = act.alloc_register("cur_s2a")
            act.reg_mov(cur, 0)

            def indices(s, q):
                act.activation(idx[:, q, :, :], src[:, bass.ds(s * (H // 2), H // 2), 1:2], ACT.Copy
                               ).then_inc(idx_set, 1)
            for q in range(Q):
                indices(q, q)

            def rnd(i, more=True):
                for q in range(Q):
                    s = i * Q + q
                    last = dtile(act, s)
                    act.wait_ge(msg_ready, s + 1)
                    act.activation(msg[:, q * H:q * H + H, D:MSG],
                                   weights[:, bass.ds(s * H * HEADS, H * HEADS)].rearrange(
                                       "p (u h) -> p u h", h=HEADS), ACT.Copy).then_inc(wcol, 1)
                    if more:
                        indices(s + Q, q)

                    def extra_pair(d):
                        act.wait_ge(oh_used, d + s)
                        act.activation(acc[:, bass.ds(d - 1, 1), :].rearrange("p a m -> p (a m)"),
                                       sums(d - 1), ACT.Copy).then_inc(flushed, 1)
                    pair_loop(act, cur, [], last, lambda d: None, extra_pair)
            with act.Fori(0, ROUNDS - 1) as i:
                rnd(i)
            rnd(ROUNDS - 1, False)
            act.wait_ge(oh_used, ET // H + NT - 1)
            act.activation(acc[:, NT - 1, :], sums(NT - 1), ACT.Copy).then_inc(flushed, 1)

        @block.vector
        def _(dve):
            cur, prev = dve.alloc_register("cur_s2v"), [dve.alloc_register(f"prev{k}_s2v") for k in range(Q - 1)]
            for r in [cur] + prev:
                dve.reg_mov(r, 0)

            def rnd(i):
                first = isinstance(i, int)
                for q in range(Q):
                    s = i * Q + q
                    us = slice(q * H, q * H + H)
                    last = dtile(dve, s)
                    dve.wait_ge(fv_in[q], i * 16 + 16)
                    dve.wait_ge(fv_gathered[q], i * (8 * H) + 8 * H)
                    if not first:
                        dve.wait_ge(oh_used, dve.snap(prev[-1], min_val=0, max_val=NT - 1) + (s - (Q - 1)))
                    wt = weights[:, bass.ds(s * H * HEADS, H * HEADS)].rearrange(
                        "p (u h) -> p u h", h=HEADS).unsqueeze(3).to_broadcast([P, H, HEADS, HC])
                    dve.tensor_tensor(msg[:, us, 0:D].rearrange("p u (h c) -> p u h c", c=HC),
                                      fv[:, q * H:q * H + H, :].rearrange("p u (h c) -> p u h c", c=HC), wt,
                                      ALU.mult).then_inc(msg_ready, 1)

                    def one_hot(d, k):
                        return dve.scalar_tensor_tensor(
                            oh[:, q, k, :, :], iota.unsqueeze(1).to_broadcast([P, H, P]),
                            const[:, bass.ds(d + C_BASE, 1)],
                            dstf[:, bass.ds(s * H, H)].unsqueeze(2).to_broadcast([P, H, P]),
                            ALU.add, ALU.is_equal)

                    def extra_pair(d):
                        dve.wait_ge(oh_used, d + s)
                        one_hot(d, 1).then_inc(oh_ready, 1)
                    pair_loop(dve, cur, prev, last, lambda d: one_hot(d, 0).then_inc(oh_ready, 1), extra_pair,
                              lambda d: one_hot(d, 1).then_inc(oh_ready, 1))
            rnd(0)
            with dve.Fori(1, ROUNDS) as i:
                rnd(i)

        @block.tensor
        def _(pe):
            cur = pe.alloc_register("cur_s2p")
            pe.reg_mov(cur, 0)
            pe.matmul(sums(0), zero[:, 0:P], zero[:, :], start=True, stop=True).then_inc(flushed, 1)

            with pe.Fori(0, ROUNDS) as i:
                for q in range(Q):
                    s = i * Q + q
                    last = dtile(pe, s)
                    pe.wait_ge(wcol, s + 1)

                    def pair(d, start, k):
                        pe.wait_ge(oh_ready, d + (s + 1))
                        for u in range(H):
                            ins = pe.matmul(sums(d), oh[:, q, k, u, :], msg[:, q * H + u, :],
                                            start=start and u == 0, stop=True, skip_group_check=True)
                        ins.then_inc(oh_used, 1)

                    def extra_pair(d):
                        pe.wait_ge(flushed, d)
                        pair(d, True, 1)
                    pair_loop(pe, cur, [], last, lambda d: pair(d, False, 0), extra_pair)


def ffn_phase(nc, sb, sem, a, dram, out, x1, r1, r2, const, bank, ident):
    xf = r1[:, 0:NT * D].rearrange("p (t d) -> p t d", d=D)
    FC = FF // P
    with ExitStack() as loc:
        stats = sb(loc, "stats_f", [P, G, 6])
        aggr = sb(loc, "aggr_f", [P, G, 2])
        mv = sb(loc, "mv_f", [P, NT, 2])
        rs = sb(loc, "rs_f", [P, 2, NT])
        wr = sb(loc, "wr", [P, 2, EXPERTS])
        ones = sb(loc, "ones", [P, P])
        br = sb(loc, "br", [1, EXPERTS])
        w1 = sb(loc, "w1", [P, 2, 2, FF])
        w2 = sb(loc, "w2", [P, 2, FC, D])
        b1 = sb(loc, "b1", [P, 2, FC])
        b2 = sb(loc, "b2", [P, 2, D])
        b2c = sb(loc, "b2c", [P, D])
        gb = sb(loc, "gb", [P, 2, D])
        rt = sb(loc, "rt", [1, 12, 8])
        rti = sb(loc, "rti", [1, 8], U32)
        mrow = sb(loc, "mrow", [1, D])
        mcol = sb(loc, "mcol", [P, 2])
        wb = sb(loc, "wb", [P, 2])
        gt = sb(loc, "gt", [P, 2 * FC, G * P])
        slot = lambda k: gt[:, 2 * k:2 * k + 2, :].rearrange("p a b -> p (a b)").rearrange("p (u d) -> p u d", d=D)
        xs, base, hh, pre = slot(0), slot(1), slot(2), slot(3)
        sl = w1[:, :, :, :].rearrange("p e k f -> p (e k f)")[:, 0:G * D].rearrange("p (u d) -> p u d", d=D)
        den = sb(loc, "den", [P, G, HEADS])
        rec = sb(loc, "rec", [P, G, HEADS])
        acc = r2[:, :].rearrange("p (t m) -> p t m", m=MSG)
        h_rows = dram["h"]
        base_rows = dram["base"]
        stats_done = sem("stats_done_f")
        w_in, dva, dvb, var_ready, sd = sem("w_in_f"), sem("dva"), sem("dvb"), sem("var_f"), sem("sd_f")

        def row_stats(dve, st, src, g):
            dve.sem_inc(stats_done, 1)
            for u in range(G):
                ins = dve.bn_stats(stats[:, u, :], src[:, bass.ds(g * G + u, 1), :].rearrange("p a d -> p (a d)"))
                st.done(ins) if u < G - 1 else st.link(ins)
            dve.sem_inc(stats_done, 1)
            for u in range(G):
                ins = dve.bn_aggr(aggr[:, u, :], stats[:, u, :])
                st.done(ins) if u < G - 1 else st.link(ins)
            st.link(dve.tensor_copy(mv[:, bass.ds(g * G, G), :], aggr[:, :, :]))

        in_b, in_h, dvc, pre_ready, sl_ready, x1_ready, ones_set = (
            sem("in_b"), sem("in_h"), sem("dvc"), sem("pre_ready"), sem("sl_ready"), sem("x1_ready"), sem("ones_set_f"))
        xs_ready, t_ps, t_ev, kept, sum_done = sem("xs_ready"), sem("t_ps"), sem("t_ev"), sem("kept"), sem("sum_done")
        mr, mc, exs, exd, wbd, wbp = sem("mr"), sem("mc"), sem("exs"), sem("exd"), sem("wbd"), sem("wbp")
        idx_ready, ex_in, w1_in = sem("idx_ready"), sem("ex_in"), [sem("w1_in0"), sem("w1_in1")]
        col = lambda k, t: rs[:, k, bass.ds(t, 1)]
        mu = lambda t: mv[:, bass.ds(t, 1), 0:1].rearrange("p a b -> p (a b)")

        with nc.Block() as block:
            @block.vector
            def _(dve):
                dve.memset(ones[:, :], 1.0).then_inc(ones_set, 1)
                sa, sc = Steps(dve, dvc), Steps(dve, dva)

                def divide(g):
                    first = isinstance(g, int) and g == 0
                    sa.enter(g, 3, 0)
                    sa.link(dve.tensor_scalar(den[:, :, :], acc[:, bass.ds(g * G, G), D:MSG], 1e-30, None, ALU.max))
                    sa.link(dve.reciprocal(rec[:, :, :], den[:, :, :]))
                    if not first:
                        dve.wait_ge(sl_ready, g)
                    sa.link(dve.tensor_tensor(
                        pre[:, :, :].rearrange("p t (h c) -> p t h c", c=HC),
                        acc[:, bass.ds(g * G, G), 0:D].rearrange("p t (h c) -> p t h c", c=HC),
                        rec[:, :, :].unsqueeze(3).to_broadcast([P, G, HEADS, HC]), ALU.mult))
                    sa.leave(0)
                    sa.base = 0

                def add_h(g):
                    dve.wait_ge(in_h, g * 16 + 16)
                    dve.tensor_tensor(pre[:, :, :], pre[:, :, :], hh[:, :, :], ALU.add).then_inc(pre_ready, 1)

                def moments(g):
                    sc.enter(g, 2 * G + 2, 0)
                    dve.wait_ge(x1_ready, g + 1)
                    row_stats(dve, sc, x1, g)
                    dve.tensor_scalar(rs[:, 0, bass.ds(g * G, G)], aggr[:, :, 1:2].rearrange("p t o -> p (t o)"),
                                      LN_EPS, None, ALU.add).then_inc(var_ready, 1)

                def norm(g):
                    first = isinstance(g, int) and g == 0
                    dve.wait_ge(sd, g + 1)
                    sc.link(dve.reciprocal(rs[:, 0, bass.ds(g * G, G)], rs[:, 1, bass.ds(g * G, G)]))
                    if not first:
                        dve.wait_ge(t_ps, g * 4)
                        dve.wait_ge(kept, g)
                        dve.wait_ge(sum_done, g)
                    for u in range(G):
                        t = g * G + u
                        dve.tensor_scalar(xs[:, u, :], x1[:, bass.ds(t, 1), :].rearrange("p a d -> p (a d)"),
                                          mu(t), col(0, t), ALU.subtract, ALU.mult).then_inc(xs_ready, 1)
                    sc.leave(0)
                    sc.base = 0
                for g in range(2):
                    divide(g)
                    add_h(g)

                def both(g):
                    moments(g - 2)
                    divide(g)
                    norm(g - 2)
                    add_h(g)
                both(2)
                with dve.Fori(3, NG) as g:
                    both(g)
                for g in range(NG - 2, NG):
                    moments(g)
                    norm(g)
                st = Steps(dve, dvb)
                dve.wait_ge(sum_done, NG)
                dve.tensor_scalar(mrow[:, :], bank[6][0:1, 0:D], 1.0 / N_NODES, None, ALU.mult).then_inc(mr, 1)
                dve.wait_ge(mc, 1)
                st.link(dve.tensor_copy(mcol[:, :], bank[7][:, 0:2]))
                dve.tensor_copy(mcol[:, :], mcol[:, :]).then_inc(mr, 1)
                dve.wait_ge(mc, 2)
                r = lambda k: rt[:, k, :]
                r1c = lambda k, c: rt[:, k, c:c + 1]
                st.link(dve.tensor_tensor(r(0), bank[5][0:1, 0:EXPERTS], br[:, :], ALU.add))

                def softmax(src, n, dst, k):
                    st.link(dve.tensor_reduce(r1c(k, 0), rt[:, src, 0:n], AX.X, ALU.max))
                    dve.tensor_scalar(rt[:, dst, 0:n], rt[:, src, 0:n], r1c(k, 0), None, ALU.subtract).then_inc(exs, 1)
                    count[0] += 1
                    dve.wait_ge(exd, count[0])
                    st.link(dve.tensor_reduce(r1c(k, 1), rt[:, dst, 0:n], AX.X, ALU.add))
                    st.link(dve.reciprocal(r1c(k, 2), r1c(k, 1)))
                    st.link(dve.tensor_scalar(rt[:, dst, 0:n], rt[:, dst, 0:n], r1c(k, 2), None, ALU.mult))
                count = [0]
                softmax(0, EXPERTS, 1, 2)
                st.link(dve.tensor_scalar(r(3), r(1), float(N_NODES), 1e-30, ALU.mult, ALU.max))
                st.link(dve.reciprocal(r(3), r(3)))
                st.link(dve.tensor_scalar(r(3), r(3), CAPACITY, 1.0, ALU.mult, ALU.min))
                st.link(dve.tensor_tensor(r(4), r(3), r(1), ALU.mult))
                softmax(4, EXPERTS, 5, 6)
                st.link(dve.max(r(7), r(5)))
                dve.max_index(rti[:, :], r(7), r(5)).then_inc(idx_ready, 1)
                softmax(7, 2, 8, 9)
                dve.tensor_copy(rt[:, 10, 0:2], rt[:, 8, 0:2]).then_inc(wbp, 1)
                dve.wait_ge(wbd, 1)
                st.link(dve.tensor_copy(wb[:, :], bank[4][:, 0:2]))

            @block.gpsimd
            def _(pool):
                with pool.Fori(0, NG) as g:
                    pool.wait_ge(sl_ready, g + 1)
                    pool.wait_ge(in_b, g * 16 + 16)
                    pool.tensor_tensor(x1[:, bass.ds(g * G, G), :], base[:, :, :], sl[:, :, :], ALU.add
                                       ).then_inc(x1_ready, 1)

            @block.tensor
            def _(pe):
                pe.wait_ge(ones_set, 1)
                pe.wait_ge(w_in, 64)

                def group(g, start, stop):
                    first = isinstance(g, int) and start
                    for k in range(4):
                        n = min(2, G - 2 * k)
                        pe.wait_ge(xs_ready, g * G + (2 * k + n))
                        if not (first and k < 2):
                            pe.wait_ge(t_ev, g * 4 + (k - 1))
                        for u in range(n):
                            for f in range(2):
                                last = pe.transpose(bank[k % 2][:, (2 * u + f) * P:(2 * u + f + 1) * P],
                                                    xs[:, 2 * k + u, f * P:(f + 1) * P], ident)
                        last.then_inc(t_ps, 1)
                    for u in range(G):
                        one = const[:, C_REAL:C_REAL + 1] if stop and u == G - 1 else ones[:, 0:1]
                        last = pe.matmul(bank[6][0:1, 0:D], one, xs[:, u, :],
                                         start=start and u == 0, stop=stop and u == G - 1)
                    last.then_inc(sum_done, 1)
                group(0, True, False)
                with pe.Fori(1, NG - 1) as g:
                    group(g, False, False)
                group(NG - 1, False, True)
                pe.wait_ge(mr, 1)
                for f in range(2):
                    last = pe.matmul(bank[7][:, f:f + 1], mrow[0:1, f * P:(f + 1) * P], ones[0:1, 0:1],
                                     start=True, stop=True)
                last.then_inc(mc, 1)
                pe.wait_ge(mr, 2)
                for f in range(2):
                    last = pe.matmul(bank[5][0:1, 0:EXPERTS], mcol[:, f:f + 1], wr[:, f, :], start=f == 0, stop=f == 1)
                last.then_inc(mc, 1)
                pe.wait_ge(wbp, 1)
                pe.matmul(bank[4][:, 0:2], ones[0:1, :], rt[:, 10, 0:2], start=True, stop=True).then_inc(wbd, 1)

            @block.scalar
            def _(act):
                def silu(g):
                    if not (isinstance(g, int) and g == 0):
                        act.wait_ge(x1_ready, g)
                    act.wait_ge(pre_ready, g + 1)
                    act.activation(sl[:, :, :], pre[:, :, :], ACT.Silu).then_inc(sl_ready, 1)

                def norm(g):
                    act.wait_ge(var_ready, g + 1)
                    act.activation(rs[:, 1, bass.ds(g * G, G)], rs[:, 0, bass.ds(g * G, G)], ACT.Sqrt).then_inc(sd, 1)
                    for k in range(4):
                        n = min(2, G - 2 * k)
                        act.wait_ge(t_ps, g * 4 + (k + 1))
                        act.activation(r2[:, bass.ds((g * G + 2 * k) * D, n * D)], bank[k % 2][:, 0:n * D],
                                       ACT.Copy).then_inc(t_ev, 1)
                    act.activation(xf[:, bass.ds(g * G, G), :], xs[:, :, :], ACT.Copy).then_inc(kept, 1)
                silu(0)
                silu(1)
                with act.Fori(2, NG) as g:
                    norm(g - 2)
                    silu(g)
                norm(NG - 2)
                norm(NG - 1)
                for c, (dst, n) in enumerate(((1, EXPERTS), (5, EXPERTS), (8, 2))):
                    act.wait_ge(exs, c + 1)
                    act.activation(rt[:, dst, 0:n], rt[:, dst, 0:n], ACT.Exp).then_inc(exd, 1)

            @block.sync
            def _(sp):
                def rows_in(g):
                    if not isinstance(g, int):
                        sp.wait_ge(pre_ready, g)
                    sp.dma_start(hh[:, :, :], h_rows[:, bass.ds(g * G, G), :]).then_inc(in_h, 16)
                    if not isinstance(g, int):
                        sp.wait_ge(x1_ready, g)
                    sp.dma_start(base[:, :, :], base_rows[:, bass.ds(g * G, G), :]).then_inc(in_b, 16)
                rows_in(0)
                sp.dma_start(wr[:, :, :], a["wr"]).then_inc(w_in, 16)
                sp.dma_start(br[:, :], a["br"]).then_inc(w_in, 16)
                sp.dma_start(gb[:, 0, :], a["gamma"].partition_broadcast(P)).then_inc(w_in, 16)
                sp.dma_start(gb[:, 1, :], a["beta"].partition_broadcast(P)).then_inc(w_in, 16)
                with sp.Fori(1, NG) as g:
                    rows_in(g)
                sp.wait_ge(idx_ready, 1)
                xs_ = []
                for e in range(2):
                    xs_.append(sp.value_load(rti[0:1, e:e + 1], min_val=0, max_val=EXPERTS - 1))
                    one = lambda v: v[bass.ds(xs_[e], 1)]
                    sp.dma_start(w1[:, e, :, :], one(a["w1"]).rearrange("a p k f -> p (a k) f")).then_inc(w1_in[e], 16)
                    sp.dma_start(b1[:, e, :], one(a["b1"]).rearrange("a p k -> p (a k)")).then_inc(w1_in[e], 16)
                for e in range(2):
                    one = lambda v: v[bass.ds(xs_[e], 1)]
                    sp.dma_start(w2[:, e, :, :], one(a["w2"]).rearrange("a p k f -> p (a k) f")).then_inc(ex_in, 16)
                    sp.dma_start(b2[:, e, :], one(a["b2"]).rearrange("a d -> (a d)").partition_broadcast(P)
                                 ).then_inc(ex_in, 16)

        up, act_done, y_ps, o_ready, x1b, dvf = (
            sem("up"), sem("act_done"), sem("y_ps"), sem("o_ready"), sem("x1b"), sem("dvf"))
        w2_scaled = sem("w2_scaled")
        add_b, o1, out_ready, stored = sem("add_b"), sem("o1"), sem("out_ready"), sem("stored")
        o_rows = out
        xft3 = r2[:, 0:NT * D].rearrange("p (t f q) -> p f t q", f=2, q=P)

        with nc.Block() as block:
            @block.tensor
            def _(pe):
                def group(g):
                    first = isinstance(g, int) and g == 0
                    n = 0
                    for e in range(2):
                        if first:
                            pe.wait_ge(w1_in[e], 32)
                        for c in range(FC):
                            for q in range(2):
                                t0, nt = (0, 4) if q == 0 else (4, 3)
                                if not (first and n < 4):
                                    pe.wait_ge(act_done, g * (4 * FC) + (n - 3))
                                for f in range(2):
                                    last = pe.matmul(bank[n % 4][:, 0:nt * P].rearrange("p (t q) -> p t q", q=P),
                                                     w1[:, e, f, c * P:(c + 1) * P],
                                                     xft3[:, f, bass.ds(g * G + t0, nt), :],
                                                     start=f == 0, stop=f == 1)
                                last.then_inc(up, 1)
                                n += 1
                    pe.wait_ge(act_done, g * (4 * FC) + 4 * FC)
                    if first:
                        pe.wait_ge(w2_scaled, 1)
                    for u in range(G):
                        if not (first and u < 4):
                            pe.wait_ge(o_ready, g * G + reuse(u, 4))
                        for m in range(2 * FC):
                            last = pe.matmul(bank[4 + u % 4][:, 0:D], gt[:, m, u * P:(u + 1) * P],
                                             w2[:, m // FC, m % FC, :], start=m == 0, stop=m == 2 * FC - 1)
                        last.then_inc(y_ps, 1)
                group(0)
                with pe.Fori(1, NG) as g:
                    group(g)

            @block.scalar
            def _(act):
                def root(g):
                    act.wait_ge(var_ready, g + (NG + 1))
                    act.activation(rs[:, 1, bass.ds(g * G, G)], rs[:, 0, bass.ds(g * G, G)], ACT.Sqrt).then_inc(sd, 1)

                def group(g):
                    if not isinstance(g, int):
                        act.wait_ge(y_ps, g * G)
                    n = 0
                    for e in range(2):
                        for c in range(FC):
                            for q in range(2):
                                if n == 2 * FC and not isinstance(g, int):
                                    root(g - 1)
                                t0, nt = (0, 4) if q == 0 else (4, 3)
                                act.wait_ge(up, g * (4 * FC) + (n + 1))
                                act.activation(gt[:, e * FC + c, t0 * P:(t0 + nt) * P], bank[n % 4][:, 0:nt * P],
                                               ACT.Gelu, bias=b1[:, e, c:c + 1]).then_inc(act_done, 1)
                                n += 1
                group(0)
                with act.Fori(1, NG) as g:
                    group(g)
                root(NG - 1)

            @block.gpsimd
            def _(pool):
                with pool.Fori(0, NT) as t:
                    v = x1[:, bass.ds(t, 1), :].rearrange("p a d -> p (a d)")
                    pool.tensor_tensor(v, v, gb[:, 1, :], ALU.add).then_inc(x1b, 1)

            @block.vector
            def _(dve):
                st = Steps(dve, dvf)
                dve.wait_ge(ex_in, 4 * 16)
                for e in range(2):
                    st.link(dve.tensor_scalar(w2[:, e, :, :], w2[:, e, :, :], wb[:, e:e + 1], None, ALU.mult))
                st.link(dve.tensor_scalar(b2c[:, :], b2[:, 0, :], wb[:, 0:1], None, ALU.mult))
                st.link(dve.scalar_tensor_tensor(b2c[:, :], b2[:, 1, :], wb[:, 1:2], b2c[:, :], ALU.mult, ALU.add))

                dve.sem_inc(w2_scaled, 1)
                with dve.Fori(0, NG) as g:
                    for u in range(G):
                        v = xf[:, bass.ds(g * G + u, 1), :].rearrange("p a d -> p (a d)")
                        dve.tensor_tensor(v, v, b2c[:, :], ALU.add).then_inc(add_b, 1)
                    for u in range(G):
                        v = xf[:, bass.ds(g * G + u, 1), :].rearrange("p a d -> p (a d)")
                        dve.wait_ge(add_b, g * G + (u + 1))
                        dve.wait_ge(y_ps, g * G + (u + 1))
                        dve.tensor_tensor(v, bank[4 + u % 4][:, 0:D], v, ALU.add).then_inc(o_ready, 1)
                    st.enter(g, 2 * G + 2, 0)
                    dve.wait_ge(o_ready, g * G + G)
                    row_stats(dve, st, xf, g)
                    dve.tensor_scalar(rs[:, 0, bass.ds(g * G, G)], aggr[:, :, 1:2].rearrange("p t o -> p (t o)"),
                                      LN_EPS, None, ALU.add).then_inc(var_ready, 1)
                    dve.wait_ge(sd, g + (NG + 1))
                    st.link(dve.reciprocal(rs[:, 0, bass.ds(g * G, G)], rs[:, 1, bass.ds(g * G, G)]))
                    for u in range(G):
                        t = g * G + u
                        v = xf[:, bass.ds(t, 1), :].rearrange("p a d -> p (a d)")
                        dve.scalar_tensor_tensor(v, v, mu(t), gb[:, 0, :], ALU.subtract, ALU.mult).then_inc(o1, 1)
                    dve.wait_ge(x1b, g * G + G)
                    for u in range(G):
                        t = g * G + u
                        v = xf[:, bass.ds(t, 1), :].rearrange("p a d -> p (a d)")
                        dve.wait_ge(o1, t + 1)
                        dve.scalar_tensor_tensor(v, v, col(0, t),
                                                 x1[:, bass.ds(t, 1), :].rearrange("p a d -> p (a d)"),
                                                 ALU.mult, ALU.add).then_inc(out_ready, 1)
                    st.leave(0)

            @block.sync
            def _(sp):
                with sp.Fori(0, NG) as g:
                    sp.wait_ge(out_ready, g * G + G)
                    sp.dma_start(o_rows[:, bass.ds(g * G, G), :], xf[:, bass.ds(g * G, G), :]).then_inc(stored, 16)
                sp.wait_ge(stored, NG * 16)


def kernel(x, src, dst, L0_gnn_Wsrc, L0_gnn_bsrc, L0_gnn_Wdst, L0_gnn_bdst, L0_gnn_Wval, L0_gnn_bval, L0_gnn_attn,
           L0_mix_kln_weight, L0_mix_kln_bias, L0_mix_vln_weight, L0_mix_vln_bias, L0_ffn_Wr, L0_ffn_br, L0_ffn_W1,
           L0_ffn_b1, L0_ffn_W2, L0_ffn_b2, L0_ffn_gamma, L0_ffn_beta):
    import numpy as np
    import concourse.bacc as bacc
    from concourse.bass_utils import run_bass_kernel_spmd as run

    A = lambda v: np.ascontiguousarray(np.asarray(v))
    halves = lambda m: m.reshape(2, P, -1).transpose(1, 0, 2)
    pad_edges = np.full(EP - N_EDGES, PAD_NODE, np.int32)
    dst_p = np.concatenate([A(dst), pad_edges])
    src_p = np.concatenate([A(src), np.zeros(EP - N_EDGES, np.int32)])
    around = np.concatenate([np.int32([-1]), dst_p, np.int32([NP])])
    iota = np.arange(P, dtype=np.float32)
    const = np.zeros((P, C_END), np.float32)
    const[:, C_IDENT:C_IDENT + P] = np.eye(P)
    const[:, C_BLOCK:C_BLOCK + P] = np.kron(np.eye(P // HC), np.ones((HC, HC)))
    const[:, C_IOTA:C_IOTA + P] = iota
    const[:, C_BASE:C_BASE + NT] = P * np.arange(NT)
    const[:, C_NODE:C_NODE + NT] = P * np.arange(NT) + iota[:, None]
    const[:, C_ONE] = 1
    const[:, C_REAL] = P * (NT - 1) + iota < N_NODES
    flat = lambda v: A(v).reshape(-1)
    cols = lambda v: flat(v).reshape(2, P).T
    arrays = {
        "x": np.concatenate([A(x), np.zeros((NP - N_NODES, D), np.float32)]).reshape(NT, P, D).transpose(1, 0, 2),
        "src_t": src_p.reshape(ET, P).T,
        "dst_t": dst_p.reshape(ET, P).T,
        "dst_last": dst_p.reshape(ET // H, H * P)[:, -1][None, :],
        "dst_line": np.stack([around[q * LW:(q + 1) * LW + 2] for q in range(LINES)]),
        "count_row": np.arange(CE, dtype=np.float32),
        "dst_chunks": np.stack([around[j * CE:(j + 1) * CE + 2] for j in range(CHUNKS)]),
        "wcat": halves(np.concatenate([A(L0_gnn_Wsrc).T, A(L0_gnn_Wval).T, A(L0_gnn_Wdst).T], axis=1)),
        "proj_bias": np.concatenate([A(L0_gnn_bsrc), A(L0_gnn_bval), A(L0_gnn_bdst)]),
        "attn": flat(L0_gnn_attn),
        "mix_rows": np.concatenate([flat(L0_mix_kln_weight), flat(L0_mix_kln_bias),
                                    flat(L0_mix_vln_weight), flat(L0_mix_vln_bias)]),
        "mix_cols": np.concatenate([cols(L0_mix_kln_weight), cols(L0_mix_kln_bias)], axis=1),
        "const": const,
        "wr": halves(A(L0_ffn_Wr)),
        "br": A(L0_ffn_br)[None, :],
        "w1": A(L0_ffn_W1).reshape(EXPERTS, 2, P, FF).transpose(0, 2, 1, 3),
        "w2": A(L0_ffn_W2).reshape(EXPERTS, FF // P, P, D).transpose(0, 2, 1, 3),
        "b1": A(L0_ffn_b1).reshape(EXPERTS, FF // P, P).transpose(0, 2, 1),
        "b2": A(L0_ffn_b2),
        "gamma": A(L0_ffn_gamma),
        "beta": A(L0_ffn_beta),
    }
    nc = bacc.Bacc("TRN2", target_bir_lowering=False, num_devices=1)
    args = {}
    for name, v in arrays.items():
        arrays[name] = np.ascontiguousarray(v)
        args[name] = nc.dram_tensor(f"in_{name}", v.shape, mybir.dt.from_np(v.dtype), kind="ExternalInput").ap()
    out = nc.dram_tensor("out", (P, NT, D), FP32, kind="ExternalOutput").ap()
    dram = {name: nc.dram_tensor(f"s_{name}", shape, dt, kind="Internal").ap() for name, shape, dt in (
        ("tab", (NP, 2 * D), FP32), ("h", (P, NT, D), FP32), ("base", (P, NT, D), FP32),
        ("fv", (ET // H, P, H // 2, D), FP32),
        ("d16", (EP,), I16), ("edges", (EP, 2), I32))
        + tuple((f"t_{n}", arrays[n].shape, I32) for n in TABLES)}
    gps_layer(nc, args, out, dram)
    r = run(nc, [{f"in_{name}": v for name, v in arrays.items()}], core_ids=[0])
    return r.results[0]["out"].transpose(1, 0, 2).reshape(NP, D)[:N_NODES]
```
